# Optimizing a Trainium2 kernel written in Bass

```python
import numpy as np
import jax
import jax.numpy as jnp

def _softmax(x, axis=-1):
    return jax.nn.softmax(x, axis=axis)

def _gelu(x):
    return jax.nn.gelu(x, approximate=True)

def _silu(x):
    return jax.nn.silu(x)

def _sigmoid(x):
    return jax.nn.sigmoid(x)

def _layernorm(x, axis=-1, eps=1e-05):
    m = jnp.mean(x, axis=axis, keepdims=True)
    v = jnp.var(x, axis=axis, keepdims=True)
    return (x - m) / jnp.sqrt(v + eps)

def _scatter_add(tgt, idx, src, axis=0):
    return tgt.at[idx].add(src)

def _segment_sum(src, seg, n):
    return jax.ops.segment_sum(src, seg, n)
kernel_name = 'mk_gnn_resnorm_d2_gnn_r8_3b9643'

def setup_inputs(seed: int=0):
    np.random.seed(seed)
    _w = jnp.asarray

    def _rec_inputs():
        import jax
        import jax.numpy as jnp
        _gk = jax.random.key(seed)
        x = -0.0007083 + 1.001 * jax.random.normal(jax.random.fold_in(_gk, 1), (6250, 48), jnp.float32)
        src = jax.random.randint(jax.random.fold_in(_gk, 2), (200000,), 0, 6250, jnp.int32)
        dst = jnp.minimum((6250 * jax.random.uniform(jax.random.fold_in(_gk, 3), (200000,)) ** 2.0).astype(jnp.int32), 49999)
        _o = jnp.argsort(dst, stable=True)
        src = src[_o]
        dst = dst[_o]
        edge_attr_40 = jax.random.uniform(jax.random.fold_in(_gk, 12), (200000, 40), jnp.float32, 0.0, 1)
        edge_weight = jax.random.uniform(jax.random.fold_in(_gk, 14), (200000,), jnp.float32, 0.0, 7.99999)
        node_type_119 = jax.random.randint(jax.random.fold_in(_gk, 15), (6250,), 0, 119, jnp.int32)
        node_vec = jax.random.uniform(jax.random.fold_in(_gk, 16), (6250,), jnp.float32, 0.0, 3.99996)
        return (x, src, dst, edge_attr_40, edge_weight, node_type_119, node_vec)
    x, src, dst, edge_attr_40, edge_weight, node_type_119, node_vec = _rec_inputs()

    def _L0_gnn_setup():
        import jax, jax.numpy as jnp
        import numpy as np
        N = 6250
        E = 150000
        H = 48
        RBF = 40
        L = 4
        NELEM = 119
        G = 32
        CUT = 6.0

        def _ln(x, g, b):
            m = x.mean(-1, keepdims=True)
            v = ((x - m) ** 2).mean(-1, keepdims=True)
            return (x - m) * jax.lax.rsqrt(v + 1e-05) * g + b
        key = jax.random.key(seed)
        k = jax.random.split(key, 16)
        s = 0.1
        return {'h': jax.random.normal(k[0], (N, H), jnp.float32), 'edge_index': jax.random.randint(k[1], (2, E), 0, N), 'edge_attr': jax.random.uniform(k[2], (E, RBF), dtype=jnp.float32), 'distances': jax.random.uniform(k[3], (E,), dtype=jnp.float32) * 8.0, 'atom_z': jax.random.randint(k[4], (N,), 0, NELEM), 'node_mult': jax.random.uniform(k[5], (N,), dtype=jnp.float32) * 3.0 + 1.0, 'batch': jnp.sort(jax.random.randint(k[6], (N,), 0, 64)), 'Wq': jax.random.normal(k[7], (L, H, H), jnp.float32) * s, 'gq': jnp.ones((L, H), jnp.float32), 'bq': jnp.zeros((L, H), jnp.float32), 'Wk': jax.random.normal(k[8], (L, H, H), jnp.float32) * s, 'gk': jnp.ones((L, H), jnp.float32), 'bk': jnp.zeros((L, H), jnp.float32), 'Wm': jax.random.normal(k[9], (L, H, H), jnp.float32) * s, 'Wu': jax.random.normal(k[10], (L, 2 * H, H), jnp.float32) * s, 'go': jnp.ones((L, H), jnp.float32), 'bo': jnp.zeros((L, H), jnp.float32), 'F1W': jax.random.normal(k[11], (RBF, H), jnp.float32) * s, 'F1b': jnp.zeros((H,), jnp.float32), 'F2W': jax.random.normal(k[12], (H, H), jnp.float32) * s, 'F2b': jnp.zeros((H,), jnp.float32), 'gn': jnp.ones((H,), jnp.float32), 'bn': jnp.zeros((H,), jnp.float32), 'emb': jax.random.normal(k[13], (NELEM, G), jnp.float32) * 0.01, 'adapt': jax.random.normal(k[14], (G, G), jnp.float32) * 0.01}
    _L0_gnn_all = _L0_gnn_setup()
    _L0_gnn_in = {k: v for k, v in _L0_gnn_all.items() if k in ('Wq', 'gq', 'bq', 'Wk', 'gk', 'bk', 'Wm', 'Wu', 'go', 'bo', 'F1W', 'F1b', 'F2W', 'F2b', 'gn', 'bn', 'emb', 'adapt')}
    del _L0_gnn_all

    def _L1_gnn_setup():
        import jax, jax.numpy as jnp
        import numpy as np
        N = 12500
        E = 200000
        D = 48
        K = 5
        ALPHA = 0.8
        key = jax.random.key(seed)
        k1, k2 = jax.random.split(key)
        x = jax.random.normal(k1, (N, D), dtype=jnp.float32)
        edge_index = jax.random.randint(k2, (2, E), 0, N, dtype=jnp.int32)
        return {'x': x, 'edge_index': edge_index}
    _L1_gnn_all = _L1_gnn_setup()
    _L1_gnn_in = {k: v for k, v in _L1_gnn_all.items() if k in ()}
    del _L1_gnn_all
    return {'x': x, 'src': src, 'dst': dst, 'edge_attr_40': edge_attr_40, 'edge_weight': edge_weight, 'node_type_119': node_type_119, 'node_vec': node_vec, 'L0_gnn_Wq': _L0_gnn_in['Wq'], 'L0_gnn_gq': _L0_gnn_in['gq'], 'L0_gnn_bq': _L0_gnn_in['bq'], 'L0_gnn_Wk': _L0_gnn_in['Wk'], 'L0_gnn_gk': _L0_gnn_in['gk'], 'L0_gnn_bk': _L0_gnn_in['bk'], 'L0_gnn_Wm': _L0_gnn_in['Wm'], 'L0_gnn_Wu': _L0_gnn_in['Wu'], 'L0_gnn_go': _L0_gnn_in['go'], 'L0_gnn_bo': _L0_gnn_in['bo'], 'L0_gnn_F1W': _L0_gnn_in['F1W'], 'L0_gnn_F1b': _L0_gnn_in['F1b'], 'L0_gnn_F2W': _L0_gnn_in['F2W'], 'L0_gnn_F2b': _L0_gnn_in['F2b'], 'L0_gnn_gn': _L0_gnn_in['gn'], 'L0_gnn_bn': _L0_gnn_in['bn'], 'L0_gnn_emb': _L0_gnn_in['emb'], 'L0_gnn_adapt': _L0_gnn_in['adapt']}

def reference(x, src, dst, edge_attr_40, edge_weight, node_type_119, node_vec, L0_gnn_Wq, L0_gnn_gq, L0_gnn_bq, L0_gnn_Wk, L0_gnn_gk, L0_gnn_bk, L0_gnn_Wm, L0_gnn_Wu, L0_gnn_go, L0_gnn_bo, L0_gnn_F1W, L0_gnn_F1b, L0_gnn_F2W, L0_gnn_F2b, L0_gnn_gn, L0_gnn_bn, L0_gnn_emb, L0_gnn_adapt):
    import jax
    import jax.numpy as jnp

    def _L0_gnn_ref(h, edge_index, edge_attr, distances, atom_z, node_mult, batch, Wq, gq, bq, Wk, gk, bk, Wm, Wu, go, bo, F1W, F1b, F2W, F2b, gn, bn, emb, adapt):
        import jax, jax.numpy as jnp
        import numpy as np
        N = 6250
        E = 150000
        H = 48
        RBF = 40
        L = 4
        NELEM = 119
        G = 32
        CUT = 6.0

        def _ln(x, g, b):
            m = x.mean(-1, keepdims=True)
            v = ((x - m) ** 2).mean(-1, keepdims=True)
            return (x - m) * jax.lax.rsqrt(v + 1e-05) * g + b
        src, dst = (edge_index[0], edge_index[1])
        gate = jax.nn.silu(edge_attr @ F1W + F1b) @ F2W + F2b
        ei = emb[atom_z[src]]
        ej = emb[atom_z[dst]]
        gate = gate + (ei * (ej @ adapt)).sum(-1, keepdims=True)
        cw = jnp.where(distances < CUT, 0.5 * (jnp.cos(jnp.pi * distances / CUT) + 1.0), 0.0)
        mj = node_mult[dst]
        msg = gate * h[dst] * (cw * mj)[:, None]
        agg = jax.ops.segment_sum(msg, src, num_segments=N)
        tot = jnp.clip(jax.ops.segment_sum(mj, src, num_segments=N), 1e-08, None)
        h = _ln(h + agg / tot[:, None], gn, bn)
        logm = jnp.log(jnp.clip(node_mult, 1.0, None))
        for i in range(L):
            Q = _ln(h @ Wq[i], gq[i], bq[i])
            K = _ln(h @ Wk[i], gk[i], bk[i])
            qi = Q[src]
            kj = K[dst]
            score = (qi * kj).sum(-1) + 0.1 * (edge_attr * qi[:, :RBF]).sum(-1) + logm[dst]
            smax = jax.ops.segment_max(score, src, num_segments=N)
            es = jnp.exp(jnp.minimum(score - smax[src], 20.0))
            denom = jax.ops.segment_sum(es, src, num_segments=N)
            alpha = es / (denom[src] + 1e-10)
            m = h[dst] @ Wm[i]
            aggi = jax.ops.segment_sum(alpha[:, None] * m, src, num_segments=N)
            z = jnp.concatenate([h, aggi], axis=-1) @ Wu[i]
            z = jnp.where(z > 0, z, 0.01 * z)
            h = _ln(h + z, go[i], bo[i])
        return h

    def _L1_gnn_ref(x, edge_index):
        import jax, jax.numpy as jnp
        import numpy as np
        N = 12500
        E = 200000
        D = 48
        K = 5
        ALPHA = 0.8
        n = x.shape[0]
        loops = jnp.arange(n, dtype=edge_index.dtype)
        row = jnp.concatenate([edge_index[0], loops])
        col = jnp.concatenate([edge_index[1], loops])
        deg = jax.ops.segment_sum(jnp.ones(row.shape, x.dtype), col, num_segments=n)
        dinv = jnp.where(deg > 0, jax.lax.rsqrt(deg), jnp.zeros((), x.dtype))
        w = dinv[row] * dinv[col]

        def step(h, _):
            m = jax.ops.segment_sum(w[:, None] * h[row], col, num_segments=n)
            h = (1.0 - ALPHA) * m + ALPHA * x
            return (h, None)
        h, _ = jax.lax.scan(step, x, None, length=K)
        return h
    edge_index = jnp.stack([src, dst])
    batch0 = jnp.zeros((6250,), jnp.int32)
    x = _layernorm(x + _L0_gnn_ref(x, edge_index, edge_attr_40, edge_weight, node_type_119, node_vec, batch0, L0_gnn_Wq, L0_gnn_gq, L0_gnn_bq, L0_gnn_Wk, L0_gnn_gk, L0_gnn_bk, L0_gnn_Wm, L0_gnn_Wu, L0_gnn_go, L0_gnn_bo, L0_gnn_F1W, L0_gnn_F1b, L0_gnn_F2W, L0_gnn_F2b, L0_gnn_gn, L0_gnn_bn, L0_gnn_emb, L0_gnn_adapt), axis=-1)
    x = _layernorm(x + _L1_gnn_ref(x, edge_index), axis=-1)
    return x

_drawn_inputs = setup_inputs


def setup_inputs(seed=0):
    import zlib

    import numpy as np

    out = dict(_drawn_inputs(seed))
    spreads = {'L0_gnn_gq': (1.0, 0.2),
     'L0_gnn_bq': (0.0, 0.1),
     'L0_gnn_gk': (1.0, 0.2),
     'L0_gnn_bk': (0.0, 2.0),
     'L0_gnn_go': (1.0, 0.2),
     'L0_gnn_bo': (0.0, 0.1),
     'L0_gnn_F1b': (0.0, 2.0),
     'L0_gnn_F2b': (0.0, 0.461),
     'L0_gnn_gn': (1.0, 0.2),
     'L0_gnn_bn': (0.0, 0.1)}
    factors = {'L0_gnn_emb': 64.0, 'L0_gnn_adapt': 64.0}
    for name, (base, spread) in spreads.items():
        noise = np.random.default_rng([zlib.crc32(name.encode()), seed]).standard_normal(out[name].shape)
        drawn = base * np.exp(spread * noise) if base else spread * noise
        out[name] = jnp.asarray(drawn.astype(out[name].dtype))
    for name, factor in factors.items():
        out[name] = (out[name] * factor).astype(out[name].dtype)
    return out
```

```python
import concourse.bass as bass
import numpy as np
from concourse import mybir
from contextlib import ExitStack, contextmanager

F32 = mybir.dt.float32
BF16 = mybir.dt.bfloat16
I32 = mybir.dt.int32
ALU = mybir.AluOpType
ACT = mybir.ActivationFunctionType
AX = mybir.AxisListType.X

P = 128
N = 6250
E = 200000
H = 48
RBF = 40
LAYERS = 4
G = 32
NELEM = 119
STEPS = 5
RING = 0.2
ALPHA = 0.8
HI = -(-N // P)
NP = HI * P
LASTN = N - (HI - 1) * P
GRP = 8
KE = -(-E // (P * GRP)) * GRP
NG = KE // GRP
PADS = P * KE - E
SLOTS = 8
ROWS = NP + P * KE // SLOTS
COLS = -(-ROWS // P)
RINGC = 5
NIT = COLS // RINGC
assert NIT * RINGC == COLS
ZW = COLS * SLOTS
PARS = 16 * 17
REC = RBF + H + 2
W0 = H + G + 1
WK = 2 * H + 1
WS = H + 2
W1 = H + 1
BIG = 1e30
NT = [(a, min(a + 3, HI)) for a in range(0, HI, 3)]
NNT = len(NT)


def done(eng, ins, signal, value):
    ins.then_inc(signal, 1)
    eng.wait_ge(signal, value)


class Steps:

    def __init__(self, eng, signal):
        self.eng, self.sem, self.base, self.k = eng, signal, 0, 0

    def __call__(self, ins):
        self.k += 1
        ins.then_inc(self.sem, 1)
        self.eng.wait_ge(self.sem, self.base + self.k)

    @contextmanager
    def loop(self, n, per):
        base, k = self.base, self.k
        with self.eng.Fori(0, n) as i:
            self.base, self.k = base + k + i * per, 0
            yield i
            assert self.k == per, (self.k, per)
        self.base, self.k = base, k + n * per


def bc(ap, axis, n):
    a = ap.unsqueeze(axis)
    shape = list(a.shape)
    shape[axis] = n
    return a.to_broadcast(shape)


def build(nc, io, out):
    ctx = ExitStack()
    with ctx:
        def sem(name):
            return ctx.enter_context(nc.semaphore(name))

        def dram(name, shape, dt=F32):
            return nc.dram_tensor(name, shape, dt, kind="Internal").ap()

        def sbx(c):
            return lambda name, shape, dt=F32: c.enter_context(nc.sbuf_tensor(name, shape, dt))

        sb = sbx(ctx)
        recS = dram("recS", (P * COLS * SLOTS, REC))
        idxD = dram("idxD", (P * COLS * SLOTS, 1), I32)
        attrE = dram("attrE", (P, COLS, SLOTS * RBF))
        mark = [dram(f"mark{k}", (P * COLS, 1)) for k in range(2)]
        tab0 = dram("tab0", (NP + 1, W0))
        tabE = dram("tabE", (NP + 1, G))
        tabQ = dram("tabQ", (NP + 1, H))
        tabK = dram("tabK", (NP + 1, WK))
        tabX = dram("tabX", (NP + 1, H))
        st0 = dram("st0", (P * COLS, W1))
        stA = dram("stA", (P * COLS, WS))
        stX = dram("stX", (P * COLS, H))
        cr0 = dram("cr0", (P + 1, W1))
        crA = dram("crA", (P + 1, WS))
        crX = dram("crX", (P + 1, H))

        iotai = sb("iotai", [P, P], I32)
        parti = sb("parti", [P, 1], I32)
        iota = sb("iota", [P, P])
        iotab = sb("iotab", [P, P], BF16)
        part = sb("part", [P, 1])
        ident = sb("ident", [P, P])
        identb = sb("identb", [P, P], BF16)
        triu = sb("triu", [P, P])
        tril = sb("tril", [P, P])
        ones = sb("ones", [P, P])
        edge245 = sb("edge245", [P, P])
        epsc = sb("epsc", [P, 1])
        halfpi = sb("halfpi", [P, 1])
        nullA = sb("nullA", [1, WS])
        nullK = sb("nullK", [1, WK])
        lnp = {n: sb(f"p_{n}", [P, LAYERS, H]) for n in ("gq", "bq", "gk", "bk", "go", "bo")}
        lnn = {n: sb(f"p_{n}", [P, 1, H]) for n in ("gn", "bn")}
        wqkm = sb("wqkm", [H, LAYERS, 3 * H])
        wu = sb("wu", [2 * H, LAYERS, H])
        f1w = sb("f1w", [RBF, H])
        f1b = sb("f1b", [H, 1])
        f2w = sb("f2w", [H + 1, H])
        adapt = sb("adapt", [G, G])
        x0 = sb("x0", [P, HI, H])
        h = sb("h", [P, HI, H])
        cat = sb("cat", [P, HI, 2 * H])
        mult = sb("mult", [P, HI])
        logm = sb("logm", [P, HI])
        dinv = sb("dinv", [P, HI])
        t1 = sb("t1", [P, HI, H])
        t2 = sb("t2", [P, HI, H])
        n1 = sb("n1", [P, HI])
        n2 = sb("n2", [P, HI])
        n3 = sb("n3", [P, HI])
        n4 = sb("n4", [P, HI])
        lasti = [sb(f"lasti{k}", [P, HI], I32) for k in range(2)]
        carryi = [sb(f"carryi{k}", [P, HI], I32) for k in range(2)]
        idxR = sb("idxR", [P, COLS + RINGC, SLOTS + 1], I32)
        keep = [sb(f"keep{k}", [P, COLS]) for k in range(2)]
        drop = sb("drop", [P, COLS])
        maskneg = sb("maskneg", [P, P])
        maskQP = [sb(f"maskQP{k}", [P, P]) for k in range(2)]
        maskPQ = sb("maskPQ", [P, P])
        stg = sb("stg", [P, RINGC, SLOTS + 1], I32)
        hist = sb("hist", [P, RINGC, WS])
        cin = sb("cin", [P, WS])
        mrow = sb("mrow", [P, P])
        mtr = sb("mtr", [P, P])
        c1 = sb("c1", [P, 1])
        c2 = sb("c2", [P, 1])

        zero = sb("zero", [P, ZW + RINGC * SLOTS])
        idxP = zero[:, :].bitcast(I32).rearrange("p (w s) -> p w s", s=SLOTS)

        sort = ExitStack()
        sbs = sbx(sort)
        key = [sbs(f"key{k}", [P, KE], I32) for k in range(2)]
        klo = [sbs(f"klo{k}", [P, KE], BF16) for k in range(2)]
        khi = [sbs(f"khi{k}", [P, KE], BF16) for k in range(2)]
        pos = [sbs(f"pos{k}", [P, KE], I32) for k in range(2)]
        rowi = [sbs(f"rowi{k}", [P, KE], I32) for k in range(2)]
        cw = sbs("cw", [P, KE])
        ohl = sbs("ohl", [P, 2, GRP, P], BF16)
        ohh = sbs("ohh", [P, 2, GRP, HI], BF16)
        ohtb = sbs("ohtb", [P, 2, GRP, P], BF16)
        ohtf = sbs("ohtf", [P, 2, GRP, P])
        eqm = sbs("eqm", [P, 2, GRP, P], BF16)
        run = sbs("run", [P, 2, GRP + 1, HI])
        gsel = sbs("gsel", [P, 2, GRP, HI])
        posf = sbs("posf", [P, 2, GRP])
        zb = sbs("zb", [P, P], BF16)
        rec = sbs("rec", [P, 2, GRP, REC])
        aT = sbs("aT", [RBF, GRP * P])
        hid = sbs("hid", [H + 1, GRP * P])
        sort_i = sbs("sort_i", [P, HI], I32)
        zi = sbs("zi", [P, HI], I32)
        eb = sbs("eb", [P, HI, G])
        ebT = sbs("ebT", [G, 3 * P])
        rowbi = [sbs(f"rowbi{k}", [P, HI], I32) for k in range(2)]
        markt = sbs("markt", [P, COLS])
        cum = sbs("cum", [P, COLS])
        zrow = sbs("zrow", [P, COLS])
        rowb = [sbs(f"rowb{k}", [P, HI]) for k in range(2)]
        nodef = sbs("nodef", [P, COLS])
        rowt = [sbs(f"rowt{k}", [P, HI]) for k in range(4)]
        t0 = cat[:, :, 0:W0]
        rcp = cat[:, :, :].rearrange("p h c -> p (h c)").bitcast(BF16)[:, 0:HI * P].rearrange("p (h c) -> p h c", c=P)
        nfl = sbs("nfl", [P, 2, P])
        pst = [sbs(f"pst{k}", [P, 2, GRP], I32) for k in range(2)]
        srcst = sbs("srcst", [P, 2, GRP], I32)
        sort.close()
        lay = ExitStack()
        sbl = sbx(lay)
        qkm = sbl("qkm", [P, HI, 3 * H])
        kt = sbl("kt", [P, HI, WK])
        sA = sbl("sA", [P, HI, WS])
        sC = sbl("sC", [P, HI, WS])
        Gk = sbl("Gk", [P, RINGC, SLOTS, WK])
        Gq = sbl("Gq", [P, RINGC, H])
        att = sbl("att", [P, RINGC, SLOTS, RBF])
        recL = sbl("recL", [P, RINGC, SLOTS, REC])
        prod = sbl("prod", [P, SLOTS, H + RBF])
        prod2 = sbl("prod2", [P, SLOTS, H])
        sc = sbl("sc", [P, 2, SLOTS])
        scal = sbl("scal", [P, 8])
        ar = sbl("ar", [P, W1])
        hT = sbl("hT", [2 * H, 2, 3 * P])
        lay.close()

        wide = [ctx.enter_context(nc.psum_tensor(f"wide{i}", [P, 1024], F32)) for i in range(2)]
        bank = [ctx.enter_context(nc.psum_tensor(f"bank{i}", [P, 512], F32)) for i in range(4)]


        class s:
            act_step = sem("act_step")
            att_in = [sem(f"att_in{k}") for k in range(RINGC)]
            att_out = [sem(f"att_out{k}") for k in range(RINGC)]
            carryA_mm = sem("carryA_mm")
            carryA_ready = sem("carryA_ready")
            carryX_mm = sem("carryX_mm")
            carryX_ready = sem("carryX_ready")
            carry_mm = sem("carry_mm")
            carry_ready = sem("carry_ready")
            cat_ready = sem("cat_ready")
            cexp_ready = sem("cexp_ready")
            cleared = sem("cleared")
            cm_ready = sem("cm_ready")
            cmax_ready = sem("cmax_ready")
            cnt_ready = sem("cnt_ready")
            col_done = sem("col_done")
            col_g = [sem(f"col_g{k}") for k in range(RINGC)]
            colstg = sem("colstg")
            colx_done = sem("colx_done")
            colx_g = [sem(f"colx_g{k}") for k in range(RINGC)]
            colx_stg = sem("colx_stg")
            const_ready = sem("const_ready")
            cos_ready = sem("cos_ready")
            cwT_ready = sem("cwT_ready")
            cw_ready = sem("cw_ready")
            deg_ready = sem("deg_ready")
            dist_ready = sem("dist_ready")
            dve_go = sem("dve_go")
            dve_step = sem("dve_step")
            e_T = sem("e_T")
            e_Tc = sem("e_Tc")
            e_done = sem("e_done")
            e_mm = sem("e_mm")
            emb_g = sem("emb_g")
            ends_ready = sem("ends_ready")
            exp_ready = sem("exp_ready")
            g_ready = sem("g_ready")
            h_all = sem("h_all")
            h_mm = [sem(f"h_mm{k}") for k in range(2)]
            h_oh = [sem(f"h_oh{k}") for k in range(2)]
            h_ready = sem("h_ready")
            idx_out = [sem(f"idx_out{k}") for k in range(2)]
            idxp_ld = sem("idxp_ld")
            iota = sem("iota")
            k_ready = sem("k_ready")
            keys = sem("keys")
            l0_done = sem("l0_done")
            l0_g = [sem(f"l0_g{k}") for k in range(RINGC)]
            l0_in = [sem(f"l0_in{k}") for k in range(RINGC)]
            l0_stg = sem("l0_stg")
            logm_ready = sem("logm_ready")
            m_T = sem("m_T")
            m_aT = sem("m_aT")
            m_f1 = sem("m_f1")
            m_f2 = sem("m_f2")
            m_hid = sem("m_hid")
            mark_ld = sem("mark_ld")
            mark_used = sem("mark_used")
            marked = [sem(f"marked{k}") for k in range(2)]
            max_ready = sem("max_ready")
            mult_ready = sem("mult_ready")
            nexp_ready = sem("nexp_ready")
            nmax_ready = sem("nmax_ready")
            nodes = sem("nodes")
            null = sem("null")
            p_T = sem("p_T")
            p_Tc = sem("p_Tc")
            p_done = sem("p_done")
            p_mm = sem("p_mm")
            par = sem("par")
            pe_go = sem("pe_go")
            pool_go = sem("pool_go")
            pre_mm = sem("pre_mm")
            q_ready = sem("q_ready")
            rec_fill = sem("rec_fill")
            rec_gate = sem("rec_gate")
            rec_in = [sem(f"rec_in{k}") for k in range(2)]
            rec_out = [sem(f"rec_out{k}") for k in range(2)]
            result = sem("result")
            rk_T = [sem(f"rk_T{k}") for k in range(2)]
            rk_cnt = [sem(f"rk_cnt{k}") for k in range(2)]
            rk_cp = [sem(f"rk_cp{k}") for k in range(2)]
            rk_eq = [sem(f"rk_eq{k}") for k in range(2)]
            rk_eqm = [sem(f"rk_eqm{k}") for k in range(2)]
            rk_g = [sem(f"rk_g{k}") for k in range(2)]
            rk_oh = [sem(f"rk_oh{k}") for k in range(2)]
            rk_pos = sem("rk_pos")
            rows_ready = sem("rows_ready")
            run_ready = sem("run_ready")
            scan_ready = sem("scan_ready")
            sqdeg_ready = sem("sqdeg_ready")
            stA_g = sem("stA_g")
            stA_out = sem("stA_out")
            stX_g = sem("stX_g")
            stX_out = sem("stX_out")
            st_g = sem("st_g")
            st_out = sem("st_out")
            std_ready = sem("std_ready")
            stored = sem("stored")
            t0_ready = sem("t0_ready")
            tab0_w = sem("tab0_w")
            tab_w = sem("tab_w")
            tabx_w = sem("tabx_w")
            u_T = sem("u_T")
            u_Tc = sem("u_Tc")
            u_done = sem("u_done")
            u_mm = sem("u_mm")
            var_ready = sem("var_ready")
            zero_set = sem("zero_set")
            zeroed = sem("zeroed")

        block = ctx.enter_context(nc.Block())
        Gk2 = Gk[:, :, :, :].rearrange("p c s w -> p c (s w)")
        G0 = [Gk2[:, c, 0:SLOTS * W0].rearrange("p (s w) -> p s w", w=W0) for c in range(RINGC)]
        Gx = [Gk2[:, c, 0:SLOTS * H].rearrange("p (s w) -> p s w", w=H) for c in range(RINGC)]
        recLi = recL[:, :, :, :].bitcast(I32)
        reci = rec[:, :, :, :].bitcast(I32)
        hist2 = hist[:, :, :].rearrange("p c w -> p (c w)")
        h0 = hist2[:, 0:RINGC * W1].rearrange("p (c w) -> p c w", w=W1)
        hX = hist2[:, 0:RINGC * H].rearrange("p (c w) -> p c w", w=H)
        sA2, sC2 = sA[:, :, :].rearrange("p h w -> p (h w)"), sC[:, :, :].rearrange("p h w -> p (h w)")
        sA0, sC0 = (t[:, 0:HI * W1].rearrange("p (h w) -> p h w", w=W1) for t in (sA2, sC2))
        sAX, sCX = (t[:, 0:HI * H].rearrange("p (h w) -> p h w", w=H) for t in (sA2, sC2))
        rec_v = recS.rearrange("(p w s) c -> p w (s c)", p=P, s=SLOTS)
        idx_v = idxD.rearrange("(p w s) c -> p w (s c)", p=P, s=SLOTS)
        st0_v, stA_v, stX_v = (t.rearrange("(p w) c -> p w c", p=P) for t in (st0, stA, stX))
        tabT = [bank[0][:, :].bitcast(BF16), bank[1][:, :].bitcast(BF16)]
        ea = io["edge_attr_40"]
        ea_v = ea[0:(P - 1) * KE].rearrange("(p t) c -> p t c", t=KE)
        ea_l = ea[E - KE:E].unsqueeze(0)
        OH = HI * GRP

        def by_node(ap):
            return ap[1:NP + 1].rearrange("(h p) c -> p h c", p=P)

        def load_edges(eng, tile, src, signal):
            eng.dma_start(tile[0:P - 1, :], src[0:(P - 1) * KE].rearrange("(p t) -> p t", t=KE)).then_inc(signal, 16)
            eng.dma_start(tile[P - 1:P, :], src[E - KE:E].unsqueeze(0)).then_inc(signal, 16)

        def load_nodes(eng, tile, src, signal):
            spec = "(h p) c -> p h c" if len(src.shape) == 2 else "(h p) -> p h"
            eng.dma_start(tile[:, 0:HI - 1], src[0:(HI - 1) * P].rearrange(spec, p=P),
                          allow_slow_non_contiguous=len(src.shape) == 1).then_inc(signal, 16)
            eng.dma_start(tile[0:LASTN, HI - 1:HI], src[(HI - 1) * P:N].unsqueeze(1)).then_inc(signal, 16)

        @block.sync
        def _(sp):
            sp.wait_ge(s.cleared, 1)
            for k, name in enumerate(("src", "dst")):
                load_edges(sp, rowi[k], io[name], s.keys)
            load_edges(sp, cw, io["edge_weight"], s.keys)
            load_nodes(sp, x0, io["x"], s.nodes)
            load_nodes(sp, mult, io["node_vec"], s.nodes)
            load_nodes(sp, zi, io["node_type_119"], s.nodes)
            sp.dma_start(f1w[:, :], io["L0_gnn_F1W"]).then_inc(s.par, 16)
            sp.dma_start(f1b[:, :], io["L0_gnn_F1b"].unsqueeze(1)).then_inc(s.par, 16)
            sp.dma_start(f2w[0:H, :], io["L0_gnn_F2W"]).then_inc(s.par, 16)
            sp.dma_start(f2w[H:H + 1, :], io["L0_gnn_F2b"].unsqueeze(0)).then_inc(s.par, 16)
            sp.dma_start(adapt[:, :], io["L0_gnn_adapt"]).then_inc(s.par, 16)
            for j, n in enumerate(("Wq", "Wk", "Wm")):
                sp.dma_start(wqkm[:, :, j * H:(j + 1) * H], io["L0_gnn_" + n].rearrange("l a b -> a l b")).then_inc(s.par, 16)
            sp.dma_start(wu[:, :, :], io["L0_gnn_Wu"].rearrange("l a b -> a l b")).then_inc(s.par, 16)
            for n, t in lnp.items():
                sp.dma_start(t[:, :, :], io["L0_gnn_" + n].unsqueeze(0).to_broadcast([P, LAYERS, H])).then_inc(s.par, 16)
            for n, t in lnn.items():
                sp.dma_start(t[:, :, :], io["L0_gnn_" + n].unsqueeze(0).unsqueeze(0).to_broadcast([P, 1, H])).then_inc(s.par, 16)
            for t in (tab0, tabE, tabQ, tabX, cr0, crX):
                sp.dma_start(t[0:1, :], zero[0:1, 0:t.shape[1]]).then_inc(s.null, 16)
            sp.dma_start(tabK[0:1, :], nullK[:, :]).then_inc(s.null, 16)
            sp.dma_start(crA[0:1, :], nullA[:, :]).then_inc(s.null, 16)
            for k in range(2):
                sp.wait_ge(s.marked[k], 16 * HI)
                if k:
                    sp.wait_ge(s.mark_used, 1)
                sp.dma_start(markt[:, :], mark[k].rearrange("(p w) c -> p (w c)", p=P)).then_inc(s.mark_ld, 16)
            with sp.Fori(0, NG // 2) as i:
                for b in range(2):
                    sp.wait_ge(s.rec_out[b], 16 * GRP * i)
                    cols = bass.ds(8 * (2 * i + b), GRP)
                    for lo, hi in ((0, 112), (112, P - 1)):
                        sp.dma_start(rec[lo:hi, b, :, 0:RBF], ea_v[lo:hi, cols, :]).then_inc(s.rec_in[b], 16)
                    sp.dma_start(rec[P - 1:P, b, :, 0:RBF], ea_l[:, cols, :]).then_inc(s.rec_in[b], 16)
            sp.wait_ge(s.t0_ready, 1)
            sp.dma_start(by_node(tab0), t0[:, :, :]).then_inc(s.tab0_w, 16)
            sp.wait_ge(s.emb_g, 16 * HI)
            sp.dma_start(by_node(tabE), eb[:, :, :]).then_inc(s.tab0_w, 16)
            sp.wait_ge(s.tab0_w, 32)
            for b in range(2):
                sp.wait_ge(s.rec_out[b], 16 * GRP * (NG // 2))
            for b in range(2):
                sp.wait_ge(s.idx_out[b], 16 * GRP * (NG // 2))
            sp.wait_ge(s.zeroed, 64)
            sp.wait_ge(s.null, 128)
            sp.dma_start(idxP[:, 0:COLS, :], idx_v).then_inc(s.idxp_ld, 16)
            for c in range(RINGC):
                sp.dma_start(recL[:, c, :, :].rearrange("p s c -> p (s c)"), rec_v[:, c, :]).then_inc(s.l0_in[c], 16)
            with sp.Fori(0, NIT - 1) as i:
                for c in range(RINGC):
                    sp.wait_ge(s.l0_done, RINGC * i + c + 1)
                    sp.wait_ge(s.att_out[c], 16 * (i + 1))
                    sp.dma_start(recL[:, c, :, :].rearrange("p s c -> p (s c)"),
                                 rec_v[:, bass.ds(RINGC * (i + 1) + c, 1), :].rearrange("p w c -> p (w c)")).then_inc(s.l0_in[c], 16)
                sp.dma_start(st0_v[:, bass.ds(RINGC * i, RINGC), :], h0).then_inc(s.st_out, 16)
            sp.wait_ge(s.l0_done, COLS)
            sp.dma_start(st0_v[:, COLS - RINGC:COLS, :], h0).then_inc(s.st_out, 16)
            sp.wait_ge(s.carry_ready, 1)
            sp.dma_start(cr0[1:P + 1, :], cin[:, 0:W1]).then_inc(s.st_out, 16)
            for c in range(RINGC):
                sp.wait_ge(s.att_out[c], 16 * NIT)
            with sp.Fori(0, LAYERS) as L:
                sp.wait_ge(s.q_ready, L + 1)
                sp.dma_start(by_node(tabQ), qkm[:, :, 0:H]).then_inc(s.tab_w, 16)
                sp.wait_ge(s.k_ready, L + 1)
                sp.dma_start(by_node(tabK), kt[:, :, :]).then_inc(s.tab_w, 16)
                for c in range(RINGC):
                    sp.dma_start(att[:, c, :, :].rearrange("p s c -> p (s c)"), attrE[:, c, :]).then_inc(s.att_in[c], 16)
                with sp.Fori(0, NIT - 1) as i:
                    for c in range(RINGC):
                        sp.wait_ge(s.col_done, COLS * L + RINGC * i + c + 1)
                        sp.dma_start(att[:, c, :, :].rearrange("p s c -> p (s c)"),
                                     attrE[:, bass.ds(RINGC * (i + 1) + c, 1), :].rearrange("p w c -> p (w c)")).then_inc(s.att_in[c], 16)
                    sp.dma_start(stA_v[:, bass.ds(RINGC * i, RINGC), :], hist[:, :, :]).then_inc(s.stA_out, 16)
                sp.wait_ge(s.col_done, COLS * (L + 1))
                sp.dma_start(stA_v[:, COLS - RINGC:COLS, :], hist[:, :, :]).then_inc(s.stA_out, 16)
                sp.wait_ge(s.carryA_ready, L + 1)
                sp.dma_start(crA[1:P + 1, :], cin[:, :]).then_inc(s.stA_out, 16)
            with sp.Fori(0, STEPS) as L:
                sp.wait_ge(s.g_ready, L + 1)
                sp.dma_start(by_node(tabX), t1[:, :, :]).then_inc(s.tabx_w, 16)
                with sp.Fori(0, NIT) as i:
                    sp.wait_ge(s.colx_done, COLS * L + RINGC * i + RINGC)
                    sp.dma_start(stX_v[:, bass.ds(RINGC * i, RINGC), :], hX).then_inc(s.stX_out, 16)
                sp.wait_ge(s.carryX_ready, L + 1)
                sp.dma_start(crX[1:P + 1, :], cin[:, 0:H]).then_inc(s.stX_out, 16)
            sp.wait_ge(s.result, 1)
            sp.dma_start(out[0:(HI - 1) * P].rearrange("(h p) c -> p h c", p=P), h[:, 0:HI - 1, :]).then_inc(s.stored, 16)
            sp.dma_start(out[(HI - 1) * P:N].unsqueeze(1), h[0:LASTN, HI - 1:HI, :]).then_inc(s.stored, 16)
            sp.wait_ge(s.stored, 32)

        @block.gpsimd
        def _(pool):
            nc.gpsimd.iota(iotai[:, :], pattern=[[1, P]], base=0, channel_multiplier=0).then_inc(s.iota, 1)
            nc.gpsimd.iota(parti[:, :], pattern=[[0, 1]], base=0, channel_multiplier=1).then_inc(s.iota, 1)
            pool.wait_ge(s.nodes, 96)
            for hi in range(HI):
                pool.indirect_dma_start(eb[:, hi, :], None, io["L0_gnn_emb"][:, :],
                                        bass.IndirectOffsetOnAxis(zi[:, hi:hi + 1], 0)).then_inc(s.emb_g, 16)
            for k in range(2):
                pool.wait_ge(s.rows_ready, k + 1)
                pool.wait_ge(s.zeroed, 64)
                for hi in range(HI):
                    pool.indirect_dma_start(mark[k][:, :], bass.IndirectOffsetOnAxis(rowbi[k][:, hi:hi + 1], 0),
                                            ones[:, 0:1], None).then_inc(s.marked[k], 16)
            with pool.Fori(0, NG // 2) as i:
                for b in range(2):
                    pool.wait_ge(s.rec_gate, 2 * i + b + 1)
                    pool.wait_ge(s.rec_fill, 2 * i + b + 1)
                    pool.sem_inc(s.pool_go, 1)
                    for j in range(GRP):
                        pool.indirect_dma_start(recS[:, :], bass.IndirectOffsetOnAxis(pst[0][:, b, j:j + 1], 0),
                                                rec[:, b, j, :], None).then_inc(s.rec_out[b], 16)
                        pool.indirect_dma_start(idxD[:, :], bass.IndirectOffsetOnAxis(pst[1][:, b, j:j + 1], 0),
                                                srcst[:, b, j:j + 1], None).then_inc(s.idx_out[b], 16)
            pool.wait_ge(s.tab0_w, 32)
            pool.wait_ge(s.null, 128)
            with pool.Fori(0, NIT) as i:
                for c in range(RINGC):
                    pool.wait_ge(s.l0_in[c], 16 * (i + 1))
                    pool.wait_ge(s.l0_stg, RINGC * i + c + 1)
                    pool.sem_inc(s.pool_go, 1)
                    for j in range(SLOTS):
                        pool.indirect_dma_start(G0[c][:, j, :], None, tab0[:, :],
                                                bass.IndirectOffsetOnAxis(recLi[:, c, j, REC - 1:REC], 0)).then_inc(s.l0_g[c], 16)
                    pool.indirect_dma_start(Gq[:, c, 0:G], None, tabE[:, :],
                                            bass.IndirectOffsetOnAxis(stg[:, c, SLOTS:SLOTS + 1], 0)).then_inc(s.l0_g[c], 16)
            pool.wait_ge(s.st_out, 16 * (NIT + 1))
            for hi in range(HI):
                pool.indirect_dma_start(sA0[:, hi, :], None, st0[:, :],
                                        bass.IndirectOffsetOnAxis(lasti[0][:, hi:hi + 1], 0)).then_inc(s.st_g, 16)
                pool.indirect_dma_start(sC0[:, hi, :], None, cr0[:, :],
                                        bass.IndirectOffsetOnAxis(carryi[0][:, hi:hi + 1], 0)).then_inc(s.st_g, 16)
            with pool.Fori(0, LAYERS) as L:
                pool.wait_ge(s.tab_w, 32 * L + 32)
                pool.sem_inc(s.pool_go, 1)
                with pool.Fori(0, NIT) as i:
                    for c in range(RINGC):
                        pool.wait_ge(s.colstg, (COLS + RINGC) * L + RINGC * i + c + 1)
                        pool.sem_inc(s.pool_go, 1)
                        pool.indirect_dma_start(Gq[:, c, :], None, tabQ[:, :],
                                                bass.IndirectOffsetOnAxis(stg[:, c, SLOTS:SLOTS + 1], 0)).then_inc(s.col_g[c], 16)
                        for j in range(SLOTS):
                            pool.indirect_dma_start(Gk[:, c, j, :], None, tabK[:, :],
                                                    bass.IndirectOffsetOnAxis(stg[:, c, j:j + 1], 0)).then_inc(s.col_g[c], 16)
                pool.wait_ge(s.stA_out, (16 * (NIT + 1)) * L + 16 * (NIT + 1))
                pool.sem_inc(s.pool_go, 1)
                for hi in range(HI):
                    pool.indirect_dma_start(sA[:, hi, :], None, stA[:, :],
                                            bass.IndirectOffsetOnAxis(lasti[0][:, hi:hi + 1], 0)).then_inc(s.stA_g, 16)
                    pool.indirect_dma_start(sC[:, hi, :], None, crA[:, :],
                                            bass.IndirectOffsetOnAxis(carryi[0][:, hi:hi + 1], 0)).then_inc(s.stA_g, 16)
            with pool.Fori(0, STEPS) as L:
                pool.wait_ge(s.tabx_w, 16 * L + 16)
                pool.sem_inc(s.pool_go, 1)
                with pool.Fori(0, NIT) as i:
                    for c in range(RINGC):
                        pool.wait_ge(s.colx_stg, (COLS + RINGC) * L + RINGC * i + c + 1)
                        pool.sem_inc(s.pool_go, 1)
                        for j in range(SLOTS):
                            pool.indirect_dma_start(Gx[c][:, j, :], None, tabX[:, :],
                                                    bass.IndirectOffsetOnAxis(stg[:, c, j:j + 1], 0)).then_inc(s.colx_g[c], 16)
                pool.wait_ge(s.stX_out, (16 * (NIT + 1)) * L + 16 * (NIT + 1))
                pool.sem_inc(s.pool_go, 1)
                for hi in range(HI):
                    pool.indirect_dma_start(sAX[:, hi, :], None, stX[:, :],
                                            bass.IndirectOffsetOnAxis(lasti[1][:, hi:hi + 1], 0)).then_inc(s.stX_g, 16)
                    pool.indirect_dma_start(sCX[:, hi, :], None, crX[:, :],
                                            bass.IndirectOffsetOnAxis(carryi[1][:, hi:hi + 1], 0)).then_inc(s.stX_g, 16)

        @block.scalar
        def _(act):
            a = Steps(act, s.act_step)
            act.wait_ge(s.zero_set, 1)
            wr = COLS * SLOTS * REC // ZW
            act.dma_start(recS.rearrange("(p r) c -> p (r c)", p=P).rearrange("p (a z) -> p a z", z=ZW),
                          bc(zero[:, 0:ZW], 1, wr)).then_inc(s.zeroed, 16)
            act.dma_start(idxD.rearrange("(p a) c -> p (a c)", p=P), zero[:, 0:ZW].bitcast(I32)).then_inc(s.zeroed, 16)
            for k in range(2):
                act.dma_start(mark[k].rearrange("(p a) c -> p (a c)", p=P), zero[:, 0:COLS]).then_inc(s.zeroed, 16)
            act.wait_ge(s.dist_ready, 1)
            done(act, nc.scalar.activation(cw[:, :], cw[:, :], ACT.Sin, bias=halfpi[:, 0:1], scale=-float(np.pi) / 6.0), s.cos_ready, 1)
            act.wait_ge(s.mult_ready, 1)
            done(act, nc.scalar.activation(logm[:, :], logm[:, :], ACT.Ln), s.logm_ready, 1)
            act.wait_ge(s.deg_ready, 1)
            done(act, nc.scalar.activation(n4[:, :], n3[:, :], ACT.Sqrt), s.sqdeg_ready, 1)
            with act.Fori(0, NG) as i:
                for k in range(2):
                    act.wait_ge(s.rk_T[k], i + 1)
                    act.wait_ge(s.rk_g[k], i)
                    nc.scalar.copy(ohtb[:, k, :, :].rearrange("p j e -> p (j e)"), tabT[k][:, 0:GRP * P]).then_inc(s.rk_cp[k], 1)
                    nc.scalar.copy(ohtf[:, k, :, :].rearrange("p j e -> p (j e)"), tabT[k][:, 0:GRP * P]).then_inc(s.rk_cp[k], 1)
            with act.Fori(0, NG // 2) as i:
                for b in range(2):
                    g = 2 * i + b
                    act.wait_ge(s.m_T, g + 1)
                    nc.scalar.copy(aT[:, :], wide[0][0:RBF, :]).then_inc(s.m_aT, 1)
                    act.wait_ge(s.m_f1, g + 1)
                    nc.scalar.activation(hid[0:H, :], wide[1][0:H, :], ACT.Silu, bias=f1b[:, 0:1]).then_inc(s.m_hid, 1)
                    act.wait_ge(s.m_f2, g + 1)
                    nc.scalar.copy(rec[:, b, :, RBF:RBF + H], bank[0][:, 0:GRP * H].rearrange("p (j c) -> p j c", c=H)).then_inc(s.rec_gate, 1)
            for g, (lo, hi) in enumerate(NT):
                act.wait_ge(s.e_T, g + 1)
                nc.scalar.copy(ebT[:, 0:(hi - lo) * P], bank[1][0:G, 0:(hi - lo) * P]).then_inc(s.e_Tc, 1)
                act.wait_ge(s.e_mm, g + 1)
                nc.scalar.copy(t0[:, lo:hi, H:H + G], bank[2][:, 0:(hi - lo) * G].rearrange("p (j c) -> p j c", c=G)).then_inc(s.e_done, 1)
            with act.Fori(0, NIT) as i:
                for c in range(RINGC):
                    act.wait_ge(s.l0_in[c], 16 * (i + 1))
                    act.dma_start(attrE[:, bass.ds(RINGC * i + c, 1), :].rearrange("p w (s c) -> p (w s) c", c=RBF),
                                  recL[:, c, :, 0:RBF]).then_inc(s.att_out[c], 16)

            def root(n):
                act.wait_ge(s.var_ready, n)
                done(act, nc.scalar.activation(n2[:, :], n1[:, :], ACT.Sqrt, bias=epsc[:, 0:1], scale=1.0 / H), s.std_ready, n)
            root(1)
            with act.Fori(0, LAYERS) as L:
                for g, (lo, hi) in enumerate(NT):
                    act.wait_ge(s.p_T, NNT * L + g + 1)
                    nc.scalar.copy(hT[0:H, g % 2, 0:(hi - lo) * P], bank[g % 2][0:H, 0:(hi - lo) * P]).then_inc(s.p_Tc, 1)
                    act.wait_ge(s.p_mm, NNT * L + g + 1)
                    nc.scalar.copy(qkm[:, lo:hi, :], bank[2 + g % 2][:, 0:(hi - lo) * 3 * H].rearrange("p (j c) -> p j c", c=3 * H)).then_inc(s.p_done, 1)
                root(3 * L + 2)
                root(3 * L + 3)
                with act.Fori(0, NIT) as i:
                    for c in range(RINGC):
                        w = COLS * L + RINGC * i + c
                        act.wait_ge(s.max_ready, w + 1)
                        nc.scalar.activation(sc[:, 1, :], sc[:, 0, :], ACT.Exp, bias=scal[:, 2:3], accum_out=ar[:, 0:1]).then_inc(s.exp_ready, 1)
                        nc.scalar.activation(scal[:, 3:4], scal[:, 1:2], ACT.Exp, bias=scal[:, 2:3]).then_inc(s.exp_ready, 1)
                act.wait_ge(s.cmax_ready, L + 1)
                done(act, nc.scalar.activation(mtr[:, :], mrow[:, :], ACT.Exp, bias=c1[:, 0:1]), s.cexp_ready, L + 1)
                act.wait_ge(s.nmax_ready, L + 1)
                done(act, nc.scalar.activation(n3[:, :], n3[:, :], ACT.Exp), s.nexp_ready, 2 * L + 1)
                done(act, nc.scalar.activation(n4[:, :], n4[:, :], ACT.Exp), s.nexp_ready, 2 * L + 2)
                for g, (lo, hi) in enumerate(NT):
                    act.wait_ge(s.u_T, NNT * L + g + 1)
                    nc.scalar.copy(hT[:, g % 2, 0:(hi - lo) * P], bank[g % 2][0:2 * H, 0:(hi - lo) * P]).then_inc(s.u_Tc, 1)
                    act.wait_ge(s.u_mm, NNT * L + g + 1)
                    nc.scalar.copy(t1[:, lo:hi, :], bank[2 + g % 2][:, 0:(hi - lo) * H].rearrange("p (j c) -> p j c", c=H)).then_inc(s.u_done, 1)
                root(3 * L + 4)
            root(3 * LAYERS + 2)
            root(3 * LAYERS + 3)

        @block.tensor
        def _(pe):
            pe.wait_ge(s.const_ready, 1)
            for k in range(2):
                nc.tensor.matmul(bank[k][:, 0:HI], zb[:, :], zb[:, 0:HI], start=True, stop=False).then_inc(s.h_mm[k], 1)
            with pe.Fori(0, NG) as i:
                for k in range(2):
                    pe.wait_ge(s.h_oh[k], i + 1)
                    for j in range(GRP):
                        last = nc.tensor.matmul(bank[k][:, 0:HI], ohl[:, k, j, :], ohh[:, k, j, :], start=False, stop=False)
                    last.then_inc(s.h_mm[k], 1)
            for k in range(2):
                nc.tensor.matmul(bank[k][:, 0:HI], zb[:, :], zb[:, 0:HI], start=False, stop=True).then_inc(s.h_all, 1)
            for k in range(2):
                pe.wait_ge(s.cnt_ready, k + 1)
                nc.tensor.matmul(bank[2][:, 0:HI], triu[:, :], rowt[0][:, :], start=True, stop=True)
                nc.tensor.matmul(bank[3][:, 0:HI], ones[:, :], rowt[0][:, :], start=True, stop=True).then_inc(s.pre_mm, 1)
                pe.wait_ge(s.scan_ready, k + 1)
                nc.tensor.matmul(bank[2][:, 64:65], triu[:, :], cum[:, COLS - 1:COLS], start=True, stop=True).then_inc(s.pre_mm, 1)
                pe.wait_ge(s.ends_ready, k + 1)
                nc.tensor.matmul(bank[2][:, 128:256], nfl[:, 0, :], ident[:, :], start=True, stop=True)
                nc.tensor.matmul(bank[3][:, 128:256], nfl[:, 1, :], ident[:, :], start=True, stop=True).then_inc(s.pre_mm, 1)
            pe.wait_ge(s.run_ready, 2)
            with pe.Fori(0, NG) as i:
                for k in range(2):
                    pe.wait_ge(s.rk_oh[k], i + 1)
                    for j in range(GRP):
                        last = nc.tensor.transpose(tabT[k][:, j * P:(j + 1) * P], ohl[:, k, j, :], identb[:, :])
                    last.then_inc(s.rk_T[k], 1)
                    for j in range(GRP):
                        last = nc.tensor.matmul(bank[2 + k][:, j * HI:(j + 1) * HI], ohl[:, k, j, :], ohh[:, k, j, :], start=True, stop=True)
                    last.then_inc(s.rk_cnt[k], 1)
                for k in range(2):
                    pe.wait_ge(s.rk_cp[k], 2 * i + 2)
                    if k:
                        pe.wait_ge(s.rk_eqm[0], i + 1)
                    for j in range(GRP):
                        last = nc.tensor.matmul(wide[0][:, j * P:(j + 1) * P], ohtb[:, k, j, :], ohtb[:, k, j, :], start=True, stop=True)
                    last.then_inc(s.rk_eq[k], 1)
                for k in range(2):
                    pe.wait_ge(s.rk_eqm[k], i + 1)
                    for j in range(GRP):
                        o = wide[1][:, 512 * k + j * HI:512 * k + (j + 1) * HI]
                        nc.tensor.matmul(o, eqm[:, k, j, :], ohh[:, k, j, :], start=True, stop=False)
                        last = nc.tensor.matmul(o, ohtf[:, k, j, :], run[:, k, j, :], start=False, stop=True)
                    last.then_inc(s.rk_g[k], 1)
            pe.wait_ge(s.par, PARS)
            pe.wait_ge(s.rk_pos, NG)
            with pe.Fori(0, NG // 2) as i:
                for b in range(2):
                    g = 2 * i + b
                    pe.wait_ge(s.rec_in[b], 48 * (i + 1))
                    pe.wait_ge(s.m_aT, g)
                    pe.sem_inc(s.pe_go, 1)
                    for j in range(GRP):
                        last = nc.tensor.transpose(wide[0][0:RBF, j * P:(j + 1) * P], rec[:, b, j, 0:RBF], ident[:, :])
                    last.then_inc(s.m_T, 1)
                    pe.wait_ge(s.m_aT, g + 1)
                    pe.sem_inc(s.pe_go, 1)
                    for j in range(2):
                        last = nc.tensor.matmul(wide[1][0:H, j * 512:(j + 1) * 512], f1w[:, :], aT[:, j * 512:(j + 1) * 512], start=True, stop=True)
                    last.then_inc(s.m_f1, 1)
                    pe.wait_ge(s.m_hid, g + 1)
                    pe.wait_ge(s.rec_gate, g)
                    pe.sem_inc(s.pe_go, 1)
                    for j in range(GRP):
                        last = nc.tensor.matmul(bank[0][:, j * H:(j + 1) * H], hid[:, j * P:(j + 1) * P], f2w[:, :], start=True, stop=True)
                    last.then_inc(s.m_f2, 1)
            pe.wait_ge(s.emb_g, 16 * HI)
            for g, (lo, hi) in enumerate(NT):
                if g:
                    pe.wait_ge(s.e_Tc, g)
                for j in range(lo, hi):
                    last = nc.tensor.transpose(bank[1][0:G, (j - lo) * P:(j - lo + 1) * P], eb[:, j, :], ident[:, :])
                last.then_inc(s.e_T, 1)
                pe.wait_ge(s.e_Tc, g + 1)
                if g:
                    pe.wait_ge(s.e_done, g)
                for j in range(lo, hi):
                    last = nc.tensor.matmul(bank[2][:, (j - lo) * G:(j - lo + 1) * G], ebT[:, (j - lo) * P:(j - lo + 1) * P], adapt[:, :], start=True, stop=True)
                last.then_inc(s.e_mm, 1)
            pe.wait_ge(s.l0_done, COLS)
            nc.tensor.matmul(bank[0][:, 0:W1], maskQP[0][:, :], h0[:, RINGC - 1, :], start=True, stop=True).then_inc(s.carry_mm, 1)
            with pe.Fori(0, LAYERS) as L:
                pe.wait_ge(s.h_ready, L + 1)
                for g, (lo, hi) in enumerate(NT):
                    pe.wait_ge(s.p_done, NNT * L + max(g - 1, 0))
                    pe.sem_inc(s.pe_go, 1)
                    for j in range(lo, hi):
                        last = nc.tensor.transpose(bank[g % 2][0:H, (j - lo) * P:(j - lo + 1) * P], h[:, j, :], ident[:, :])
                    last.then_inc(s.p_T, 1)
                    pe.wait_ge(s.p_Tc, NNT * L + g + 1)
                    pe.sem_inc(s.pe_go, 1)
                    for j in range(lo, hi):
                        last = nc.tensor.matmul(bank[2 + g % 2][:, (j - lo) * 3 * H:(j - lo + 1) * 3 * H], hT[0:H, g % 2, (j - lo) * P:(j - lo + 1) * P],
                                                wqkm[:, bass.ds(L, 1), :].rearrange("p l c -> p (l c)"), start=True, stop=True)
                    last.then_inc(s.p_mm, 1)
                pe.wait_ge(s.cm_ready, L + 1)
                nc.tensor.matmul(wide[0][:, 0:P], mtr[:, :], ident[:, :], start=True, stop=True).then_inc(s.carryA_mm, 1)
                pe.wait_ge(s.cw_ready, L + 1)
                nc.tensor.transpose(wide[0][:, 512:512 + P], mtr[:, :], ident[:, :]).then_inc(s.carryA_mm, 1)
                pe.wait_ge(s.cwT_ready, L + 1)
                nc.tensor.matmul(wide[1][:, 0:W1], mrow[:, :], hist[:, RINGC - 1, 1:WS], start=True, stop=True).then_inc(s.carryA_mm, 1)
                pe.wait_ge(s.cat_ready, L + 1)
                for g, (lo, hi) in enumerate(NT):
                    pe.wait_ge(s.u_done, NNT * L + max(g - 1, 0))
                    pe.sem_inc(s.pe_go, 1)
                    for j in range(lo, hi):
                        last = nc.tensor.transpose(bank[g % 2][0:2 * H, (j - lo) * P:(j - lo + 1) * P], cat[:, j, :], ident[:, :])
                    last.then_inc(s.u_T, 1)
                    pe.wait_ge(s.u_Tc, NNT * L + g + 1)
                    pe.sem_inc(s.pe_go, 1)
                    for j in range(lo, hi):
                        last = nc.tensor.matmul(bank[2 + g % 2][:, (j - lo) * H:(j - lo + 1) * H], hT[:, g % 2, (j - lo) * P:(j - lo + 1) * P],
                                                wu[:, bass.ds(L, 1), :].rearrange("p l c -> p (l c)"), start=True, stop=True)
                    last.then_inc(s.u_mm, 1)
            with pe.Fori(0, STEPS) as L:
                pe.wait_ge(s.colx_done, COLS * L + COLS)
                nc.tensor.matmul(bank[0][:, 0:H], maskQP[1][:, :], hX[:, RINGC - 1, :], start=True, stop=True).then_inc(s.carryX_mm, 1)

        @block.vector
        def _(dve):
            v = Steps(dve, s.dve_step)
            V = nc.vector

            def tt(o, x, y, op):
                return V.tensor_tensor(o, x, y, op)

            for t in (x0, mult, zi, idxR, hist, ones, stg):
                v(V.memset(t[:], 1 if t is ones else 0))
            v(V.memset(zb[:], 0))
            v(V.memset(epsc[:], 1e-5))
            v(V.memset(halfpi[:], float(np.pi) / 2))
            v(V.memset(hid[:], 1.0))
            v(V.memset(zrow[:], 0))
            v(V.memset(nullA[:], 0))
            v(V.memset(nullK[:], 0))
            v(V.memset(nullA[:, 0:1], -BIG))
            v(V.memset(nullK[:, H:H + 1], -BIG))
            done(dve, V.memset(zero[:], 0), s.zero_set, 1)
            v(V.memset(rec[:], 0))
            done(dve, V.memset(rowb[0][:], 0), s.cleared, 1)
            dve.wait_ge(s.iota, 2)
            v(V.tensor_copy(iota[:], iotai[:]))
            v(V.tensor_copy(part[:], parti[:]))
            v(V.tensor_scalar(ident[:], iota[:], part[:, 0:1], None, ALU.is_equal))
            v(V.tensor_copy(identb[:], ident[:]))
            v(V.tensor_scalar(triu[:], iota[:], part[:, 0:1], None, ALU.is_gt))
            v(V.tensor_scalar(tril[:], iota[:], part[:, 0:1], None, ALU.is_lt))
            v(V.tensor_scalar(edge245[:], iota[:], float(COLS), None, ALU.mult))
            done(dve, V.tensor_copy(iotab[:], iota[:]), s.const_ready, 1)
            dve.wait_ge(s.keys, 96)
            v(V.tensor_scalar(c1[:], part[:], float(P - 1), None, ALU.is_lt))
            v(V.tensor_scalar(c2[:], c1[:], -float(NP - 1), float(NP - 1), ALU.mult, ALU.add))
            for k in range(2):
                v(V.tensor_copy(key[k][:], rowi[k][:]))
                v(V.tensor_scalar(key[k][:, 0:PADS], rowi[k][:, 0:PADS], c1[:, 0:1], c2[:, 0:1], ALU.mult, ALU.add))
                v(V.tensor_scalar(pos[k][:], key[k][:], P - 1, None, ALU.bitwise_and))
                v(V.tensor_copy(klo[k][:], pos[k][:]))
                v(V.tensor_scalar(pos[k][:], key[k][:], 7, None, ALU.logical_shift_right))
                v(V.tensor_copy(khi[k][:], pos[k][:]))
                v(V.tensor_scalar(rowi[k][:], rowi[k][:], 1, None, ALU.add))
            within = key[0][:, :].bitcast(F32)
            v(V.tensor_scalar(within[:, :], cw[:], 6.0, None, ALU.is_lt))
            done(dve, V.tensor_scalar(cw[:], cw[:], 6.0, None, ALU.min), s.dist_ready, 1)
            dve.wait_ge(s.nodes, 96)
            done(dve, V.tensor_scalar(logm[:], mult[:], 1.0, None, ALU.max), s.mult_ready, 1)
            dve.wait_ge(s.cos_ready, 1)
            v(V.tensor_scalar(cw[:], cw[:], 1.0, 0.5, ALU.add, ALU.mult))
            v(tt(cw[:], cw[:], within[:, :], ALU.mult))

            def one_hots(k, i, slot):
                cols = bass.ds(GRP * i, GRP)
                tt(ohl[:, slot, :, :], bc(klo[k][:, cols], 2, P), bc(iotab[:, :], 1, GRP), ALU.is_equal)
                return tt(ohh[:, slot, :, :], bc(khi[k][:, cols], 2, HI), bc(iotab[:, 0:HI], 1, GRP), ALU.is_equal)

            with dve.Fori(0, NG) as i:
                for k in range(2):
                    dve.wait_ge(s.h_mm[k], i + 1)
                    one_hots(k, i, k).then_inc(s.h_oh[k], 1)
            dve.wait_ge(s.h_all, 2)
            for k in range(2):
                cnt, rows, last, run_in, tmp = rowt[1], rowt[0], rowt[1], run, rowt[2]
                v(V.tensor_copy(cnt[:], bank[k][:, 0:HI]))
                if k:
                    done(dve, V.tensor_scalar(n3[:], cnt[:], 1.0, None, ALU.add), s.deg_ready, 1)
                    dve.wait_ge(s.sqdeg_ready, 1)
                    v(V.reciprocal(dinv[:], n4[:]))
                v(V.tensor_scalar(sort_i[:], cnt[:], float(SLOTS - 1), None, ALU.add))
                v(V.tensor_scalar(sort_i[:], sort_i[:], SLOTS.bit_length() - 1, None, ALU.logical_shift_right))
                done(dve, V.tensor_scalar(rows[:], sort_i[:], 1.0, None, ALU.max), s.cnt_ready, k + 1)
                dve.wait_ge(s.pre_mm, 3 * k + 1)
                v(V.tensor_tensor_scan(tmp[:], bank[3][:, 0:HI], zrow[:, 0:HI], 0.0, ALU.add, ALU.add))
                v(tt(tmp[:], tmp[:], bank[3][:, 0:HI], ALU.subtract))
                v(tt(rowb[k][:], tmp[:], bank[2][:, 0:HI], ALU.add))
                done(dve, V.tensor_copy(rowbi[k][:], rowb[k][:]), s.rows_ready, k + 1)
                v(tt(last[:], rowb[k][:], rows[:], ALU.add))
                v(V.tensor_scalar(last[:], last[:], -1.0, None, ALU.add))
                v(V.tensor_copy(lasti[k][:], last[:]))
                v(tt(rcp[:, :, :], bc(last[:, :], 2, P), bc(edge245[:, :], 1, HI), ALU.is_ge))
                v(V.tensor_reduce(tmp[:], rcp[:, :, :], AX, ALU.add))
                v(V.tensor_scalar(rowt[3][:], tmp[:], float(COLS), -float(COLS), ALU.mult, ALU.add))
                v(tt(rowt[3][:], rowb[k][:], rowt[3][:], ALU.is_lt))
                v(tt(carryi[k][:], rowt[3][:], tmp[:], ALU.mult))
                done(dve, V.tensor_scalar(run[:, k, 0, :], rowb[k][:], float(SLOTS), None, ALU.mult), s.run_ready, k + 1)
                dve.wait_ge(s.mark_ld, 16 * (k + 1))
                done(dve, V.tensor_tensor_scan(cum[:], markt[:, :], zrow[:, :], 0.0, ALU.add, ALU.add), s.scan_ready, k + 1)
                if k == 0:
                    v(V.tensor_scalar(drop[:], markt[:], -BIG, None, ALU.mult))
                done(dve, V.tensor_scalar(keep[k][:], markt[:], -1.0, 1.0, ALU.mult, ALU.add), s.mark_used, k + 1)
                dve.wait_ge(s.pre_mm, 3 * k + 2)
                v(V.tensor_copy(c1[:], bank[2][:, 64:65]))
                v(V.tensor_scalar(nodef[:], cum[:], c1[:, 0:1], None, ALU.add))
                if k == 0:
                    v(V.tensor_copy(idxR[:, 0:COLS, SLOTS:SLOTS + 1], nodef[:, :].unsqueeze(2)))
                v(V.tensor_scalar(nfl[:, 0, :], ones[:], nodef[:, 0:1], None, ALU.mult))
                done(dve, V.tensor_scalar(nfl[:, 1, :], ones[:], nodef[:, COLS - 1:COLS], None, ALU.mult), s.ends_ready, k + 1)
                dve.wait_ge(s.pre_mm, 3 * k + 3)
                v(V.scalar_tensor_tensor(maskQP[k][:], bank[2][:, 128:256], nodef[:, COLS - 1:COLS], triu[:], ALU.is_equal, ALU.mult))
                if k == 0:
                    v(V.scalar_tensor_tensor(maskPQ[:], bank[3][:, 128:256], nodef[:, 0:1], tril[:], ALU.is_equal, ALU.mult))
                    v(V.tensor_scalar(maskneg[:], maskPQ[:], -1.0, BIG, ALU.add, ALU.mult))
            with v.loop(NG, 2 * (GRP + 3)) as i:
                for k in range(2):
                    one_hots(k, i, k).then_inc(s.rk_oh[k], 1)
                for k in range(2):
                    dve.wait_ge(s.rk_cnt[k], i + 1)
                    for j in range(GRP):
                        v(tt(run[:, k, j + 1, :], run[:, k, j, :], bank[2 + k][:, j * HI:(j + 1) * HI], ALU.add))
                    dve.wait_ge(s.rk_eq[k], i + 1)
                    tt(eqm[:, k, :, :], wide[0][:, :].rearrange("p (j e) -> p j e", e=P), bc(triu[:, :], 1, GRP),
                       ALU.mult).then_inc(s.rk_eqm[k], 1)
                for k in range(2):
                    dve.wait_ge(s.rk_g[k], i + 1)
                    v(tt(gsel[:, k, :, :], wide[1][:, 512 * k:512 * k + OH].rearrange("p (j c) -> p j c", c=HI), ohh[:, k, :, :], ALU.mult))
                    v(V.tensor_reduce(posf[:, k, :], gsel[:, k, :, :], AX, ALU.add))
                    v(V.tensor_copy(run[:, k, 0, :], run[:, k, GRP, :]))
                    last = V.tensor_scalar(pos[k][:, bass.ds(GRP * i, GRP)], posf[:, k, :], 0.0, None, ALU.add)
                done(dve, last, s.rk_pos, i + 1)
            with dve.Fori(0, NG // 2) as i:
                for b in range(2):
                    cols = bass.ds(GRP * (2 * i + b), GRP)
                    dve.wait_ge(s.rec_out[b], 16 * GRP * i)
                    dve.wait_ge(s.idx_out[b], 16 * GRP * i)
                    V.tensor_scalar(rec[:, b, :, REC - 2], cw[:, cols], 1.0, None, ALU.mult)
                    V.tensor_scalar(reci[:, b, :, REC - 1], rowi[1][:, cols], 0, None, ALU.add)
                    V.tensor_scalar(srcst[:, b, :], rowi[0][:, cols], 0, None, ALU.add)
                    for k in range(2):
                        last = V.tensor_scalar(pst[k][:, b, :], pos[k][:, cols], 0, None, ALU.add)
                    last.then_inc(s.rec_fill, 1)
            v(V.tensor_copy(t0[:, :, 0:H], x0[:, :, :]))
            dve.wait_ge(s.e_done, NNT)
            done(dve, V.tensor_copy(t0[:, :, W0 - 1:W0], mult[:, :].unsqueeze(2)), s.t0_ready, 1)
            for b in range(2):
                dve.wait_ge(s.rec_out[b], 16 * GRP * (NG // 2))
                dve.wait_ge(s.idx_out[b], 16 * GRP * (NG // 2))

            def by_slot(ap):
                return ap.rearrange("p s c -> p c s")

            def int_copy(o, i_):
                return V.tensor_scalar(o, i_, 0, None, ALU.add)

            for c in range(RINGC):
                done(dve, int_copy(stg[:, c, SLOTS:], idxR[:, c, SLOTS:]), s.l0_stg, c + 1)
            with v.loop(NIT, 9 * RINGC) as i:
                dve.wait_ge(s.st_out, 16 * i)
                for c in range(RINGC):
                    w = RINGC * i + c
                    dve.wait_ge(s.l0_g[c], 16 * (SLOTS + 1) * (i + 1))
                    g0 = G0[c]
                    v(tt(prod[:, :, 0:G], g0[:, :, H:H + G], bc(Gq[:, c, 0:G], 1, SLOTS), ALU.mult))
                    v(V.tensor_reduce(sc[:, 0, :], prod[:, :, 0:G], AX, ALU.add))
                    v(tt(prod2[:, :, :], recL[:, c, :, RBF:RBF + H], bc(sc[:, 0, :], 2, H), ALU.add))
                    v(tt(prod2[:, :, :], prod2[:, :, :], g0[:, :, 0:H], ALU.mult))
                    v(tt(sc[:, 1, :], recL[:, c, :, REC - 2], g0[:, :, W0 - 1], ALU.mult))
                    v(tt(prod2[:, :, :], prod2[:, :, :], bc(sc[:, 1, :], 2, H), ALU.mult))
                    v(V.tensor_reduce(ar[:, 0:H], by_slot(prod2[:, :, :]), AX, ALU.add))
                    v(V.tensor_reduce(ar[:, H:W1], g0[:, :, W0 - 1], AX, ALU.add))
                    v(int_copy(idxR[:, bass.ds(w, 1), 0:SLOTS].rearrange("p w s -> p (w s)"), recLi[:, c, :, REC - 1]))
                    done(dve, V.scalar_tensor_tensor(h0[:, c, :], h0[:, (c - 1) % RINGC, :], keep[0][:, bass.ds(w, 1)], ar[:, :],
                                                     ALU.mult, ALU.add), s.l0_done, w + 1)
                    done(dve, int_copy(stg[:, c, SLOTS:], idxR[:, bass.ds(w + RINGC, 1), SLOTS:].rearrange("p w s -> p (w s)")),
                         s.l0_stg, w + RINGC + 1)
            dve.wait_ge(s.carry_mm, 1)
            done(dve, V.tensor_copy(cin[:, 0:W1], bank[0][:, 0:W1]), s.carry_ready, 1)

            def layer_norm(o, x, n, gain=None, bias=None, signal=None, value=None):
                v(V.tensor_reduce(n1[:, :], x, AX, ALU.add))
                v(V.tensor_scalar(n1[:, :], n1[:, :], 1.0 / H, None, ALU.mult))
                v(tt(t2[:, :, :], x, bc(n1[:, :], 2, H), ALU.subtract))
                v(tt(o, t2[:, :, :], t2[:, :, :], ALU.mult))
                done(dve, V.tensor_reduce(n1[:, :], o, AX, ALU.add), s.var_ready, n)
                dve.wait_ge(s.std_ready, n)
                v(V.reciprocal(n3[:, :], n2[:, :]))
                last = tt(o, t2[:, :, :], bc(n3[:, :], 2, H), ALU.mult)
                if gain is not None:
                    v(last)
                    v(tt(o, o, gain, ALU.mult))
                    last = tt(o, o, bias, ALU.add)
                if signal is None:
                    v(last)
                else:
                    done(dve, last, signal, value)

            dve.wait_ge(s.st_g, 32 * HI)
            dve.wait_ge(s.par, PARS)
            v(tt(sA0[:, :, :], sA0[:, :, :], sC0[:, :, :], ALU.add))
            v(V.tensor_scalar(n1[:, :], sA0[:, :, H], 1e-8, None, ALU.max))
            v(V.reciprocal(n4[:, :], n1[:, :]))
            v(tt(t1[:, :, :], sA0[:, :, 0:H], bc(n4[:, :], 2, H), ALU.mult))
            v(tt(t1[:, :, :], t1[:, :, :], x0[:, :, :], ALU.add))

            def all_nodes(p):
                return p.to_broadcast([P, HI, H])

            layer_norm(h[:, :, :], t1[:, :, :], 1, all_nodes(lnn["gn"][:, :, :]), all_nodes(lnn["bn"][:, :, :]), s.h_ready, 1)

            def layer(L):
                def par(n):
                    return all_nodes(lnp[n][:, bass.ds(L, 1), :])

                dve.wait_ge(s.p_done, NNT * L + NNT)
                layer_norm(qkm[:, :, 0:H], qkm[:, :, 0:H], 3 * L + 2, par("gq"), par("bq"), s.q_ready, L + 1)
                layer_norm(kt[:, :, 0:H], qkm[:, :, H:2 * H], 3 * L + 3, par("gk"), par("bk"))
                v(V.tensor_copy(kt[:, :, H:H + 1], logm[:, :].unsqueeze(2)))
                done(dve, V.tensor_copy(kt[:, :, H + 1:WK], qkm[:, :, 2 * H:3 * H]), s.k_ready, L + 1)
                v(V.memset(hist[:, RINGC - 1, :], 0))
                v(V.memset(hist[:, RINGC - 1, 0:1], -BIG))
                for c in range(RINGC):
                    done(dve, int_copy(stg[:, c, :], idxR[:, c, :]), s.colstg, (COLS + RINGC) * L + c + 1)

            def column(L, i, c):
                w = RINGC * i + c
                prev = hist[:, (c - 1) % RINGC, :]
                dve.wait_ge(s.att_in[c], (16 * NIT) * L + 16 * i + 16)
                dve.wait_ge(s.col_g[c], (16 * (SLOTS + 1) * NIT) * L + 16 * (SLOTS + 1) * i + 16 * (SLOTS + 1))
                v(tt(prod[:, :, 0:H], Gk[:, c, :, 0:H], bc(Gq[:, c, :], 1, SLOTS), ALU.mult))
                v(V.scalar_tensor_tensor(prod[:, :, H:], att[:, c, :, :], 0.1, bc(Gq[:, c, 0:RBF], 1, SLOTS), ALU.mult, ALU.mult))
                v(V.tensor_reduce(sc[:, 0, :], prod[:, :, :], AX, ALU.add))
                v(tt(sc[:, 0, :], sc[:, 0, :], Gk[:, c, :, H], ALU.add))
                v(V.tensor_reduce(scal[:, 0:1], sc[:, 0, :], AX, ALU.max))
                v(tt(scal[:, 1:2], prev[:, 0:1], drop[:, bass.ds(w, 1)], ALU.add))
                v(tt(hist[:, c, 0:1], scal[:, 0:1], scal[:, 1:2], ALU.max))
                done(dve, V.tensor_scalar(scal[:, 2:3], hist[:, c, 0:1], -1.0, None, ALU.mult), s.max_ready, COLS * L + w + 1)
                dve.wait_ge(s.exp_ready, (2 * COLS) * L + 2 * w + 2)
                v(tt(prod2[:, :, :], Gk[:, c, :, H + 1:WK], bc(sc[:, 1, :], 2, H), ALU.mult))
                v(V.tensor_reduce(ar[:, 1:W1], by_slot(prod2[:, :, :]), AX, ALU.add))
                v(tt(scal[:, 4:5], scal[:, 3:4], keep[0][:, bass.ds(w, 1)], ALU.mult))
                done(dve, V.scalar_tensor_tensor(hist[:, c, 1:WS], prev[:, 1:WS], scal[:, 4:5], ar[:, :], ALU.mult, ALU.add),
                     s.col_done, COLS * L + w + 1)
                done(dve, int_copy(stg[:, c, :], idxR[:, bass.ds(w + RINGC, 1), :].rearrange("p w s -> p (w s)")),
                     s.colstg, (COLS + RINGC) * L + w + RINGC + 1)

            def finish_layer(L):
                done(dve, V.tensor_scalar(mtr[:], ones[:], hist[:, RINGC - 1, 0:1], None, ALU.mult), s.cm_ready, L + 1)
                dve.wait_ge(s.carryA_mm, 3 * L + 1)
                v(tt(mrow[:], wide[0][:, 0:P], maskPQ[:], ALU.mult))
                v(tt(mrow[:], mrow[:], maskneg[:], ALU.add))
                v(V.tensor_reduce(cin[:, 0:1], mrow[:], AX, ALU.max))
                done(dve, V.tensor_scalar(c1[:], cin[:, 0:1], -1.0, None, ALU.mult), s.cmax_ready, L + 1)
                dve.wait_ge(s.cexp_ready, L + 1)
                done(dve, tt(mtr[:], mtr[:], maskPQ[:], ALU.mult), s.cw_ready, L + 1)
                dve.wait_ge(s.carryA_mm, 3 * L + 2)
                done(dve, V.tensor_copy(mrow[:], wide[0][:, 512:512 + P]), s.cwT_ready, L + 1)
                dve.wait_ge(s.carryA_mm, 3 * L + 3)
                done(dve, V.tensor_copy(cin[:, 1:WS], wide[1][:, 0:W1]), s.carryA_ready, L + 1)
                dve.wait_ge(s.stA_g, (32 * HI) * L + 32 * HI)
                v(tt(n1[:, :], sA[:, :, 0], sC[:, :, 0], ALU.max))
                v(tt(n3[:, :], sA[:, :, 0], n1[:, :], ALU.subtract))
                done(dve, tt(n4[:, :], sC[:, :, 0], n1[:, :], ALU.subtract), s.nmax_ready, L + 1)
                dve.wait_ge(s.nexp_ready, 2 * L + 2)
                v(tt(sA[:, :, 1:WS], sA[:, :, 1:WS], bc(n3[:, :], 2, W1), ALU.mult))
                v(tt(sC[:, :, 1:WS], sC[:, :, 1:WS], bc(n4[:, :], 2, W1), ALU.mult))
                v(tt(sA[:, :, 1:WS], sA[:, :, 1:WS], sC[:, :, 1:WS], ALU.add))
                v(V.tensor_scalar(n1[:, :], sA[:, :, 1], 1e-10, None, ALU.add))
                v(V.reciprocal(n4[:, :], n1[:, :]))
                v(tt(cat[:, :, H:2 * H], sA[:, :, 2:WS], bc(n4[:, :], 2, H), ALU.mult))
                done(dve, V.tensor_copy(cat[:, :, 0:H], h[:, :, :]), s.cat_ready, L + 1)
                dve.wait_ge(s.u_done, NNT * L + NNT)
                v(V.tensor_scalar(t2[:, :, :], t1[:, :, :], 0.01, None, ALU.mult))
                v(tt(t1[:, :, :], t1[:, :, :], t2[:, :, :], ALU.max))
                v(tt(t1[:, :, :], t1[:, :, :], h[:, :, :], ALU.add))
                layer_norm(h[:, :, :], t1[:, :, :], 3 * L + 4, all_nodes(lnp["go"][:, bass.ds(L, 1), :]),
                           all_nodes(lnp["bo"][:, bass.ds(L, 1), :]), s.h_ready, L + 2)

            around = 39
            with v.loop(LAYERS, 10 * COLS + around) as L:
                layer(L)
                dve.sem_inc(s.dve_go, 1)
                with v.loop(NIT, 10 * RINGC) as i:
                    dve.wait_ge(s.stA_out, (16 * (NIT + 1)) * L + 16 * i)
                    for c in range(RINGC):
                        column(L, i, c)
                finish_layer(L)
            v(tt(t1[:, :, :], x0[:, :, :], h[:, :, :], ALU.add))
            layer_norm(h[:, :, :], t1[:, :, :], 3 * LAYERS + 2)
            v(V.tensor_copy(cat[:, :, 0:H], h[:, :, :]))
            v(V.tensor_scalar(cat[:, :, H:2 * H], h[:, :, :], ALPHA, None, ALU.mult))
            dve.wait_ge(s.idxp_ld, 16)
            with v.loop(STEPS, 1 + COLS + 4) as L:
                done(dve, tt(t1[:, :, :], h[:, :, :], bc(dinv[:, :], 2, H), ALU.mult), s.g_ready, L + 1)
                v(V.memset(hX[:, RINGC - 1, :], 0))
                for c in range(RINGC):
                    done(dve, int_copy(stg[:, c, 0:SLOTS], idxP[:, c, :]), s.colx_stg, (COLS + RINGC) * L + c + 1)
                dve.sem_inc(s.dve_go, 1)
                with v.loop(NIT, RINGC) as i:
                    dve.wait_ge(s.stX_out, (16 * (NIT + 1)) * L + 16 * i)
                    for c in range(RINGC):
                        w = RINGC * i + c
                        dve.wait_ge(s.colx_g[c], (16 * SLOTS * NIT) * L + 16 * SLOTS * i + 16 * SLOTS)
                        v(V.tensor_reduce(ar[:, 0:H], by_slot(Gx[c][:, :, :]), AX, ALU.add))
                        done(dve, V.scalar_tensor_tensor(hX[:, c, :], hX[:, (c - 1) % RINGC, :], keep[1][:, bass.ds(w, 1)], ar[:, 0:H],
                                                         ALU.mult, ALU.add), s.colx_done, COLS * L + w + 1)
                        done(dve, int_copy(stg[:, c, 0:SLOTS], idxP[:, bass.ds(w + RINGC, 1), :].rearrange("p w s -> p (w s)")),
                             s.colx_stg, (COLS + RINGC) * L + w + RINGC + 1)
                dve.wait_ge(s.carryX_mm, L + 1)
                done(dve, V.tensor_copy(cin[:, 0:H], bank[0][:, 0:H]), s.carryX_ready, L + 1)
                dve.wait_ge(s.stX_g, (32 * HI) * L + 32 * HI)
                v(tt(sAX[:, :, :], sAX[:, :, :], sCX[:, :, :], ALU.add))
                v(tt(sAX[:, :, :], sAX[:, :, :], t1[:, :, :], ALU.add))
                v(tt(sAX[:, :, :], sAX[:, :, :], bc(dinv[:, :], 2, H), ALU.mult))
                v(V.scalar_tensor_tensor(h[:, :, :], sAX[:, :, :], RING, cat[:, :, H:2 * H], ALU.mult, ALU.add))
            v(tt(t1[:, :, :], cat[:, :, 0:H], h[:, :, :], ALU.add))
            layer_norm(h[:, :, :], t1[:, :, :], 3 * LAYERS + 3, signal=s.result, value=1)


def kernel(**inputs):
    import concourse.bacc as bacc
    from concourse.bass_utils import run_bass_kernel_spmd

    nc = bacc.Bacc("TRN2", target_bir_lowering=False, num_devices=1)
    arrays, io = {}, {}
    for name, value in inputs.items():
        a = np.ascontiguousarray(value)
        arrays[f"in_{name}"] = a
        io[name] = nc.dram_tensor(f"in_{name}", a.shape, mybir.dt.from_np(a.dtype), kind="ExternalInput").ap()
    out = nc.dram_tensor("out_0", (N, H), F32, kind="ExternalOutput").ap()
    build(nc, io, out)
    r = run_bass_kernel_spmd(nc, [arrays], core_ids=[0])
    return r.results[0]["out_0"]
```

```python
import concourse.bass as bass
import numpy as np
from concourse import mybir
from contextlib import ExitStack, contextmanager

F32 = mybir.dt.float32
BF16 = mybir.dt.bfloat16
I32 = mybir.dt.int32
ALU = mybir.AluOpType
ACT = mybir.ActivationFunctionType
AX = mybir.AxisListType.X

P = 128
N = 6250
E = 200000
H = 48
RBF = 40
LAYERS = 4
G = 32
NELEM = 119
STEPS = 5
RING = 0.2
ALPHA = 0.8
HI = -(-N // P)
NP = HI * P
ADJR = 7
NPH = NP // 2
PC = NPH // 7
LASTN = N - (HI - 1) * P
GRP = 8
KE = -(-E // (P * GRP)) * GRP
NG = KE // GRP
PADS = P * KE - E
SLOTS = 8
ROWS = NP + P * KE // SLOTS
COLS = -(-ROWS // P)
RINGC = 5
NIT = COLS // RINGC
assert NIT * RINGC == COLS
ZW = COLS * SLOTS
PARS = 16 * 17
REC = RBF + H + 2
W0 = H + G + 1
WK = 2 * H + 1
TPI = 21
TOFF = [0, 4, 8, 12, 16, TPI]
NTC = LAYERS * NIT * TPI
assert NTC >= HI * HI + P * KE // P
WS = H + 2
W1 = H + 1
BIG = 1e30
NT = [(a, min(a + 3, HI)) for a in range(0, HI, 3)]
NNT = len(NT)


def done(eng, ins, signal, value):
    ins.then_inc(signal, 1)
    eng.wait_ge(signal, value)


class Steps:

    def __init__(self, eng, signal):
        self.eng, self.sem, self.base, self.k = eng, signal, 0, 0

    def __call__(self, ins):
        self.k += 1
        ins.then_inc(self.sem, 1)
        self.eng.wait_ge(self.sem, self.base + self.k)

    def start(self, ins):
        self.k += 1
        ins.then_inc(self.sem, 1)
        return self.k

    def after(self, k):
        self.eng.wait_ge(self.sem, self.base + k)

    @contextmanager
    def loop(self, n, per):
        base, k = self.base, self.k
        with self.eng.Fori(0, n) as i:
            self.base, self.k = base + k + i * per, 0
            yield i
            assert self.k == per, (self.k, per)
        self.base, self.k = base, k + n * per


def bc(ap, axis, n):
    a = ap.unsqueeze(axis)
    shape = list(a.shape)
    shape[axis] = n
    return a.to_broadcast(shape)


def build(nc, io, out):
    ctx = ExitStack()
    with ctx:
        def sem(name):
            return ctx.enter_context(nc.semaphore(name))

        def dram(name, shape, dt=F32):
            return nc.dram_tensor(name, shape, dt, kind="Internal").ap()

        def sbx(c):
            return lambda name, shape, dt=F32: c.enter_context(nc.sbuf_tensor(name, shape, dt))

        sb = sbx(ctx)
        recS = dram("recS", (P * COLS * SLOTS, REC))
        pairs = dram("pairs", (P * NTC, 1), I32)
        tfirst = dram("tfirst", (NTC, 1))
        tdest = dram("tdest", (NTC, 1), I32)
        adj = dram("adj", ((HI + 1) * P * HI, P))
        attrE = dram("attrE", (P, COLS, SLOTS * RBF))
        mark = dram("mark", (P * COLS, 1))
        tab0 = dram("tab0", (NP + 1, W0))
        tabE = dram("tabE", (NP + 1, G))
        tabQ = dram("tabQ", (NP + 1, H))
        tabK = dram("tabK", (NP + 1, WK))
        st0 = dram("st0", (P * COLS, W1))
        stA = dram("stA", (P * COLS, WS))
        cr0 = dram("cr0", (P + 1, W1))
        crA = dram("crA", (P + 1, WS))

        iotai = sb("iotai", [P, P], I32)
        parti = sb("parti", [P, 1], I32)
        iota = sb("iota", [P, P])
        iotab = sb("iotab", [P, P], BF16)
        part = sb("part", [P, 1])
        ident = sb("ident", [P, P])
        identb = sb("identb", [P, P], BF16)
        triu = sb("triu", [P, P])
        tril = sb("tril", [P, P])
        ones = sb("ones", [P, P])
        edge245 = sb("edge245", [P, P])
        iotab1 = sb("iotab1", [P, P], BF16)
        zb = sb("zb", [P, 512], BF16)
        epsc = sb("epsc", [P, 1])
        halfpi = sb("halfpi", [P, 1])
        nullA = sb("nullA", [1, WS])
        nullK = sb("nullK", [1, WK])
        lnp = {n: sb(f"p_{n}", [P, LAYERS, H]) for n in ("gq", "bq", "gk", "bk", "go", "bo")}
        lnn = {n: sb(f"p_{n}", [P, 1, H]) for n in ("gn", "bn")}
        wqkm = sb("wqkm", [H, LAYERS, 3 * H])
        wu = sb("wu", [2 * H, LAYERS, H])
        f1w = sb("f1w", [RBF, H])
        f1b = sb("f1b", [H, 1])
        f2w = sb("f2w", [H + 1, H])
        adapt = sb("adapt", [G, G])
        x0 = sb("x0", [P, HI, H])
        h = sb("h", [P, HI, H])
        cat = sb("cat", [P, HI, 2 * H])
        mult = sb("mult", [P, HI])
        logm = sb("logm", [P, HI])
        dinv = sb("dinv", [P, HI])
        t1 = sb("t1", [P, HI, H])
        t2 = sb("t2", [P, HI, H])
        n1 = sb("n1", [P, HI])
        n2 = sb("n2", [P, HI])
        n3 = sb("n3", [P, HI])
        n4 = sb("n4", [P, HI])
        lasti = sb("lasti", [P, HI], I32)
        carryi = sb("carryi", [P, HI], I32)
        idxR = sb("idxR", [P, COLS + RINGC, SLOTS + 1], I32)
        keep = sb("keep", [P, COLS])
        drop = sb("drop", [P, COLS])
        maskneg = sb("maskneg", [P, P])
        maskQP = sb("maskQP", [P, P])
        maskPQ = sb("maskPQ", [P, P])
        stg = sb("stg", [P, RINGC, SLOTS + 1], I32)
        hist = sb("hist", [P, RINGC, WS])
        cin = sb("cin", [P, WS])
        mrow = sb("mrow", [P, P])
        mtr = sb("mtr", [P, P])
        c1 = sb("c1", [P, 1])
        c2 = sb("c2", [P, 1])

        zero = sb("zero", [P, NTC // 2])
        plo = zero[:, :].bitcast(BF16)

        sort = ExitStack()
        sbs = sbx(sort)
        key = [sbs(f"key{k}", [P, KE], I32) for k in range(2)]
        klo = [sbs(f"klo{k}", [P, KE], BF16) for k in range(2)]
        khi = [sbs(f"khi{k}", [P, KE], BF16) for k in range(2)]
        keyt = sbs("keyt", [P, KE], I32)
        pair = sbs("pair", [P, KE], I32)
        rowi = [sbs(f"rowi{k}", [P, KE], I32) for k in range(2)]
        cw = sbs("cw", [P, KE])
        ohl = sbs("ohl", [P, 2, GRP, P], BF16)
        ohh = sbs("ohh", [P, 2, GRP, HI], BF16)
        ohtb = sbs("ohtb", [P, 2, GRP, P], BF16)
        ohtf = sbs("ohtf", [P, 2, GRP, P])
        eqm = sbs("eqm", [P, 2, GRP, P], BF16)
        run = sbs("run", [P, 2, GRP + 1, HI])
        gsel = sbs("gsel", [P, 2, GRP, HI])
        qi = sbs("qi", [P, 2, GRP], I32)
        posf = sbs("posf", [P, 2, GRP])
        rec = sbs("rec", [P, 2, GRP, REC])
        aT = sbs("aT", [RBF, 4 * P])
        hid = sbs("hid", [H + 1, 4 * P])
        sort_i = sbs("sort_i", [P, HI], I32)
        zi = sbs("zi", [P, HI], I32)
        eb = sbs("eb", [P, HI, G])
        ebT = sbs("ebT", [G, 3 * P])
        rowbi = sbs("rowbi", [P, HI], I32)
        lastt = sbs("lastt", [P, HI], I32)
        firstt = sbs("firstt", [P, HI], I32)
        destv = sbs("destv", [P, HI], I32)
        markt = sbs("markt", [P, COLS])
        cum = sbs("cum", [P, COLS])
        zrow = sbs("zrow", [P, COLS])
        rowb = sbs("rowb", [P, HI])
        nodef = sbs("nodef", [P, COLS])
        rowt = [sbs(f"rowt{k}", [P, HI]) for k in range(4)]
        t0 = cat[:, :, 0:W0]
        rcp = cat[:, :, :].rearrange("p h c -> p (h c)").bitcast(BF16)[:, 0:HI * P].rearrange("p (h c) -> p h c", c=P)
        nfl = sbs("nfl", [P, 2, P])
        pst = [sbs(f"pst{k}", [P, 2, GRP], I32) for k in range(2)]
        srcst = sbs("srcst", [P, 2, GRP], I32)
        sort.close()
        lay = ExitStack()
        sbl = sbx(lay)
        qkm = sbl("qkm", [P, HI, 3 * H])
        kt = sbl("kt", [P, HI, WK])
        sA, sC = (qkm[:, :, :].rearrange("p h c -> p (h c)")[:, k * HI * WS:(k + 1) * HI * WS].rearrange("p (h c) -> p h c", c=WS)
                  for k in range(2))
        Gk = sbl("Gk", [P, RINGC, SLOTS, WK])
        Gq = sbl("Gq", [P, RINGC, H])
        att = sbl("att", [P, RINGC, SLOTS, RBF])
        recL = kt[:, :, :].rearrange("p h c -> p (h c)")[:, 0:RINGC * SLOTS * REC].rearrange(
            "p (r s c) -> p r s c", r=RINGC, s=SLOTS)
        pairt = qkm[:, :, :].rearrange("p h c -> p (h c)").bitcast(I32)[:, 0:NTC]
        phi = sbl("phi", [P, NTC], BF16)
        tkeep = sbl("tkeep", [P, NTC])
        tslot = sbl("tslot", [TPI, NTC // TPI], I32)
        tnone = sbl("tnone", [TPI, NTC // TPI], I32)
        oht = sbl("oht", [P, 2, 5, P], BF16)
        acc = sbl("acc", [P, 10, P])
        prod = sbl("prod", [P, SLOTS, H + RBF])
        prod2 = sbl("prod2", [P, SLOTS, H])
        sc = sbl("sc", [P, 2, 2, SLOTS])
        scal = sbl("scal", [P, 2, 8])
        ar = sbl("ar", [P, 2, W1])
        hT = sbl("hT", [2 * H, 2, 3 * P])
        lay.close()
        walk = ExitStack()
        sbw = sbx(walk)
        adjr = sbw("adjr", [P, ADJR, NPH])
        blk = sbw("blk", [P, ADJR, H])
        sums = sbw("sums", [H, NP])
        walk.close()

        wide = [ctx.enter_context(nc.psum_tensor(f"wide{i}", [P, 1024], F32)) for i in range(2)]
        bank = [ctx.enter_context(nc.psum_tensor(f"bank{i}", [P, 512], F32)) for i in range(4)]


        class s:
            adj_in = [sem(f"adj_in{k}") for k in range(ADJR)]
            adj_used = sem("adj_used")
            att_in = [sem(f"att_in{k}") for k in range(RINGC)]
            att_out = [sem(f"att_out{k}") for k in range(RINGC)]
            blk_ready = sem("blk_ready")
            carryA_mm = sem("carryA_mm")
            carryA_ready = sem("carryA_ready")
            carry_mm = sem("carry_mm")
            carry_ready = sem("carry_ready")
            cat_ready = sem("cat_ready")
            cexp_ready = sem("cexp_ready")
            cleared = sem("cleared")
            cm_ready = sem("cm_ready")
            cmax_ready = sem("cmax_ready")
            cnt_done = sem("cnt_done")
            cnt_mm = sem("cnt_mm")
            cnt_oh = sem("cnt_oh")
            cnt_out = [sem(f"cnt_out{k}") for k in range(RINGC)]
            cnt_ready = sem("cnt_ready")
            col_done = sem("col_done")
            col_g = [sem(f"col_g{k}") for k in range(RINGC)]
            colstg = sem("colstg")
            const_ready = sem("const_ready")
            cos_ready = sem("cos_ready")
            cwT_ready = sem("cwT_ready")
            cw_ready = sem("cw_ready")
            deg_ready = sem("deg_ready")
            dist_ready = sem("dist_ready")
            dve_step = sem("dve_step")
            e_T = sem("e_T")
            e_Tc = sem("e_Tc")
            e_done = sem("e_done")
            e_mm = sem("e_mm")
            emb_g = sem("emb_g")
            ends_ready = sem("ends_ready")
            exp_ready = sem("exp_ready")
            g_ready = sem("g_ready")
            go = sem("go")
            h_all = sem("h_all")
            h_mm = sem("h_mm")
            h_oh = [sem(f"h_oh{k}") for k in range(2)]
            h_ready = sem("h_ready")
            idx_out = [sem(f"idx_out{k}") for k in range(2)]
            iota = sem("iota")
            k_ready = sem("k_ready")
            keep_ld = sem("keep_ld")
            keys = sem("keys")
            l0_done = sem("l0_done")
            l0_g = [sem(f"l0_g{k}") for k in range(RINGC)]
            l0_in = [sem(f"l0_in{k}") for k in range(RINGC)]
            l0_stg = sem("l0_stg")
            logm_ready = sem("logm_ready")
            m_T = sem("m_T")
            m_aT = sem("m_aT")
            m_f1 = sem("m_f1")
            m_f2 = sem("m_f2")
            m_hid = sem("m_hid")
            mark_ld = sem("mark_ld")
            marked = sem("marked")
            max_ready = sem("max_ready")
            mult_ready = sem("mult_ready")
            nexp_ready = sem("nexp_ready")
            nmax_ready = sem("nmax_ready")
            nodes = sem("nodes")
            null = sem("null")
            p_T = sem("p_T")
            p_Tc = sem("p_Tc")
            p_done = sem("p_done")
            p_mm = sem("p_mm")
            pair_ld = sem("pair_ld")
            par = sem("par")
            pre_mm = sem("pre_mm")
            prop_T = sem("prop_T")
            prop_cp = sem("prop_cp")
            prop_mm = sem("prop_mm")
            q_ready = sem("q_ready")
            rec_fill = sem("rec_fill")
            rec_gate = sem("rec_gate")
            rec_in = [sem(f"rec_in{k}") for k in range(2)]
            rec_out = [sem(f"rec_out{k}") for k in range(2)]
            result = sem("result")
            rk_T = sem("rk_T")
            rk_cnt = sem("rk_cnt")
            rk_cp = sem("rk_cp")
            rk_eq = sem("rk_eq")
            rk_eqm = sem("rk_eqm")
            rk_g = sem("rk_g")
            rk_oh = sem("rk_oh")
            rows_ready = sem("rows_ready")
            run_ready = sem("run_ready")
            scan_ready = sem("scan_ready")
            slot_ld = sem("slot_ld")
            slots_ready = sem("slots_ready")
            sqdeg_ready = sem("sqdeg_ready")
            stA_g = sem("stA_g")
            stA_out = sem("stA_out")
            st_g = sem("st_g")
            st_out = sem("st_out")
            std_ready = sem("std_ready")
            stored = sem("stored")
            t0_ready = sem("t0_ready")
            tab0_w = sem("tab0_w")
            tab_w = sem("tab_w")
            tiles_ready = sem("tiles_ready")
            tmarked = sem("tmarked")
            u_T = sem("u_T")
            u_Tc = sem("u_Tc")
            u_done = sem("u_done")
            u_mm = sem("u_mm")
            unpacked = sem("unpacked")
            var_ready = sem("var_ready")
            x_ready = sem("x_ready")
            zero_set = sem("zero_set")
            zeroed = sem("zeroed")

        block = ctx.enter_context(nc.Block())
        Gk2 = Gk[:, :, :, :].rearrange("p c s w -> p c (s w)")
        G0 = [Gk2[:, c, 0:SLOTS * W0].rearrange("p (s w) -> p s w", w=W0) for c in range(RINGC)]
        recLi = recL.bitcast(I32)
        reci = rec[:, :, :, :].bitcast(I32)
        hist2 = hist[:, :, :].rearrange("p c w -> p (c w)")
        h0 = hist2[:, 0:RINGC * W1].rearrange("p (c w) -> p c w", w=W1)
        sA2, sC2 = sA.rearrange("p h w -> p (h w)"), sC.rearrange("p h w -> p (h w)")
        sA0, sC0 = (t[:, 0:HI * W1].rearrange("p (h w) -> p h w", w=W1) for t in (sA2, sC2))
        rec_v = recS.rearrange("(p w s) c -> p w (s c)", p=P, s=SLOTS)
        st0_v, stA_v = (t.rearrange("(p w) c -> p w c", p=P) for t in (st0, stA))
        tabT = [wide[1][:, 512 * k:512 * (k + 1)].bitcast(BF16) for k in range(2)]
        adj_v = adj[0:HI * P * HI].rearrange("(i p j) c -> i p (j c)", i=HI, p=P)
        halves = [wide[k][:, 512 * q:512 * (q + 1)] for k in range(2) for q in range(2)]
        prop = halves + bank[0:3]
        propT = [bank[3]] + halves
        ea = io["edge_attr_40"]
        ea_v = ea[0:(P - 1) * KE].rearrange("(p t) c -> p t c", t=KE)
        ea_l = ea[E - KE:E].unsqueeze(0)
        OH = HI * GRP

        def acc_slot(c, j):
            return 5 * (c % 2) + j - TOFF[c]

        def by_node(ap):
            return ap[1:NP + 1].rearrange("(h p) c -> p h c", p=P)

        def load_edges(eng, tile, src, signal):
            eng.dma_start(tile[0:P - 1, :], src[0:(P - 1) * KE].rearrange("(p t) -> p t", t=KE)).then_inc(signal, 16)
            eng.dma_start(tile[P - 1:P, :], src[E - KE:E].unsqueeze(0)).then_inc(signal, 16)

        def load_nodes(eng, tile, src, signal):
            spec = "(h p) c -> p h c" if len(src.shape) == 2 else "(h p) -> p h"
            eng.dma_start(tile[:, 0:HI - 1], src[0:(HI - 1) * P].rearrange(spec, p=P),
                          allow_slow_non_contiguous=len(src.shape) == 1).then_inc(signal, 16)
            eng.dma_start(tile[0:LASTN, HI - 1:HI], src[(HI - 1) * P:N].unsqueeze(1)).then_inc(signal, 16)

        @block.sync
        def _(sp):
            sp.wait_ge(s.cleared, 1)
            for k, name in enumerate(("src", "dst")):
                load_edges(sp, rowi[k], io[name], s.keys)
            load_edges(sp, cw, io["edge_weight"], s.keys)
            load_nodes(sp, x0, io["x"], s.nodes)
            load_nodes(sp, mult, io["node_vec"], s.nodes)
            load_nodes(sp, zi, io["node_type_119"], s.nodes)
            sp.dma_start(f1w[:, :], io["L0_gnn_F1W"]).then_inc(s.par, 16)
            sp.dma_start(f1b[:, :], io["L0_gnn_F1b"].unsqueeze(1)).then_inc(s.par, 16)
            sp.dma_start(f2w[0:H, :], io["L0_gnn_F2W"]).then_inc(s.par, 16)
            sp.dma_start(f2w[H:H + 1, :], io["L0_gnn_F2b"].unsqueeze(0)).then_inc(s.par, 16)
            sp.dma_start(adapt[:, :], io["L0_gnn_adapt"]).then_inc(s.par, 16)
            for j, n in enumerate(("Wq", "Wk", "Wm")):
                sp.dma_start(wqkm[:, :, j * H:(j + 1) * H], io["L0_gnn_" + n].rearrange("l a b -> a l b")).then_inc(s.par, 16)
            sp.dma_start(wu[:, :, :], io["L0_gnn_Wu"].rearrange("l a b -> a l b")).then_inc(s.par, 16)
            for n, t in lnp.items():
                sp.dma_start(t[:, :, :], io["L0_gnn_" + n].unsqueeze(0).to_broadcast([P, LAYERS, H])).then_inc(s.par, 16)
            for n, t in lnn.items():
                sp.dma_start(t[:, :, :], io["L0_gnn_" + n].unsqueeze(0).unsqueeze(0).to_broadcast([P, 1, H])).then_inc(s.par, 16)
            for t in (tab0, tabE, tabQ, cr0):
                sp.dma_start(t[0:1, :], zero[0:1, 0:t.shape[1]]).then_inc(s.null, 16)
            sp.dma_start(tabK[0:1, :], nullK[:, :]).then_inc(s.null, 16)
            sp.dma_start(crA[0:1, :], nullA[:, :]).then_inc(s.null, 16)
            sp.wait_ge(s.marked, 16 * HI)
            sp.dma_start(markt[:, :], mark.rearrange("(p w) c -> p (w c)", p=P)).then_inc(s.mark_ld, 16)
            with sp.Fori(0, NG // 2) as i:
                for b in range(2):
                    sp.wait_ge(s.rec_out[b], 16 * GRP * i)
                    cols = bass.ds(8 * (2 * i + b), GRP)
                    for lo, hi in ((0, 112), (112, P - 1)):
                        sp.dma_start(rec[lo:hi, b, :, 0:RBF], ea_v[lo:hi, cols, :]).then_inc(s.rec_in[b], 16)
                    sp.dma_start(rec[P - 1:P, b, :, 0:RBF], ea_l[:, cols, :]).then_inc(s.rec_in[b], 16)
            sp.wait_ge(s.t0_ready, 1)
            sp.dma_start(by_node(tab0), t0[:, :, :]).then_inc(s.tab0_w, 16)
            sp.wait_ge(s.emb_g, 16 * HI)
            sp.dma_start(by_node(tabE), eb[:, :, :]).then_inc(s.tab0_w, 16)
            sp.wait_ge(s.tab0_w, 32)
            for b in range(2):
                sp.wait_ge(s.rec_out[b], 16 * GRP * (NG // 2))
            for b in range(2):
                sp.wait_ge(s.idx_out[b], 16 * GRP * (NG // 2))
            sp.dma_start(pairt, pairs.rearrange("(p t) c -> p (t c)", p=P)).then_inc(s.pair_ld, 16)
            sp.wait_ge(s.tmarked, 16 * 2 * HI)
            sp.dma_start(tslot[:, :], tdest.rearrange("(i q) a -> q (i a)", q=TPI), allow_slow_non_contiguous=True).then_inc(s.slot_ld, 16)
            sp.wait_ge(s.unpacked, 1)
            sp.dma_start(tkeep[:, :], tfirst.rearrange("t a -> a t").to_broadcast([P, NTC])).then_inc(s.keep_ld, 16)
            for c in range(RINGC):
                sp.dma_start(recL[:, c, :, :].rearrange("p s c -> p (s c)"), rec_v[:, c, :]).then_inc(s.l0_in[c], 16)
            with sp.Fori(0, NIT - 1) as i:
                for c in range(RINGC):
                    sp.wait_ge(s.l0_done, RINGC * i + c + 1)
                    sp.wait_ge(s.att_out[c], 16 * (i + 1))
                    sp.dma_start(recL[:, c, :, :].rearrange("p s c -> p (s c)"),
                                 rec_v[:, bass.ds(RINGC * (i + 1) + c, 1), :].rearrange("p w c -> p (w c)")).then_inc(s.l0_in[c], 16)
                sp.dma_start(st0_v[:, bass.ds(RINGC * i, RINGC), :], h0).then_inc(s.st_out, 16)
            sp.wait_ge(s.l0_done, COLS)
            sp.dma_start(st0_v[:, COLS - RINGC:COLS, :], h0).then_inc(s.st_out, 16)
            sp.wait_ge(s.carry_ready, 1)
            sp.dma_start(cr0[1:P + 1, :], cin[:, 0:W1]).then_inc(s.st_out, 16)
            for c in range(RINGC):
                sp.wait_ge(s.att_out[c], 16 * NIT)
            sp.wait_ge(s.slots_ready, 1)
            with sp.Fori(0, LAYERS) as L:
                sp.wait_ge(s.q_ready, L + 1)
                sp.dma_start(by_node(tabQ), qkm[:, :, 0:H]).then_inc(s.tab_w, 16)
                sp.wait_ge(s.k_ready, L + 1)
                sp.dma_start(by_node(tabK), kt[:, :, :]).then_inc(s.tab_w, 16)
                for c in range(RINGC):
                    sp.dma_start(att[:, c, :, :].rearrange("p s c -> p (s c)"), attrE[:, c, :]).then_inc(s.att_in[c], 16)

                def counts_out(it, c):
                    for j in range(TOFF[c], TOFF[c + 1]):
                        slot = sp.value_load(tslot[j:j + 1, bass.ds(it, 1)], min_val=0, max_val=NP * HI + TPI)
                        if j == TOFF[c]:
                            sp.wait_ge(s.cnt_done, RINGC * it + c + 1)
                        sp.dma_start(adj[bass.ds(slot, P, HI), :], acc[:, acc_slot(c, j), :]).then_inc(s.cnt_out[c], 16)

                with sp.Fori(0, NIT - 1) as i:
                    for c in range(RINGC):
                        sp.wait_ge(s.col_done, COLS * L + RINGC * i + c + 1)
                        sp.dma_start(att[:, c, :, :].rearrange("p s c -> p (s c)"),
                                     attrE[:, bass.ds(RINGC * (i + 1) + c, 1), :].rearrange("p w c -> p (w c)")).then_inc(s.att_in[c], 16)
                        counts_out(NIT * L + i, c)
                    sp.dma_start(stA_v[:, bass.ds(RINGC * i, RINGC), :], hist[:, :, :]).then_inc(s.stA_out, 16)
                for c in range(RINGC):
                    counts_out(NIT * L + NIT - 1, c)
                sp.wait_ge(s.col_done, COLS * (L + 1))
                sp.dma_start(stA_v[:, COLS - RINGC:COLS, :], hist[:, :, :]).then_inc(s.stA_out, 16)
                sp.wait_ge(s.carryA_ready, L + 1)
                sp.dma_start(crA[1:P + 1, :], cin[:, :]).then_inc(s.stA_out, 16)
            for c in range(RINGC):
                sp.wait_ge(s.cnt_out[c], 16 * (TOFF[c + 1] - TOFF[c]) * LAYERS * NIT)
            sp.wait_ge(s.x_ready, 1)
            with sp.Fori(0, STEPS) as L:
                for half in range(2):
                    with sp.Fori(0, HI // ADJR) as i:
                        for k in range(ADJR):
                            sp.wait_ge(s.adj_used, (2 * HI) * L + HI * half + ADJR * i + k + 1)
                            sp.dma_start(adjr[:, k, :], adj_v[bass.ds(ADJR * i + k, 1), :, half * NPH:(half + 1) * NPH].rearrange("i p c -> p (i c)")
                                         ).then_inc(s.adj_in[k], 16)
            sp.wait_ge(s.result, 1)
            sp.dma_start(out[0:(HI - 1) * P].rearrange("(h p) c -> p h c", p=P), h[:, 0:HI - 1, :]).then_inc(s.stored, 16)
            sp.dma_start(out[(HI - 1) * P:N].unsqueeze(1), h[0:LASTN, HI - 1:HI, :]).then_inc(s.stored, 16)
            sp.wait_ge(s.stored, 32)

        @block.gpsimd
        def _(pool):
            nc.gpsimd.iota(iotai[:, :], pattern=[[1, P]], base=0, channel_multiplier=0).then_inc(s.iota, 1)
            nc.gpsimd.iota(parti[:, :], pattern=[[0, 1]], base=0, channel_multiplier=1).then_inc(s.iota, 1)
            pool.wait_ge(s.nodes, 96)
            for hi in range(HI):
                pool.indirect_dma_start(eb[:, hi, :], None, io["L0_gnn_emb"][:, :],
                                        bass.IndirectOffsetOnAxis(zi[:, hi:hi + 1], 0)).then_inc(s.emb_g, 16)
            pool.wait_ge(s.rows_ready, 1)
            pool.wait_ge(s.zeroed, 16 * 5)
            for hi in range(HI):
                pool.indirect_dma_start(mark[:, :], bass.IndirectOffsetOnAxis(rowbi[:, hi:hi + 1], 0),
                                        ones[:, 0:1], None).then_inc(s.marked, 16)
            pool.wait_ge(s.tiles_ready, 1)
            for hi in range(HI):
                pool.indirect_dma_start(tfirst[:, :], bass.IndirectOffsetOnAxis(firstt[0:HI, hi:hi + 1], 0),
                                        ones[0:HI, 0:1], None).then_inc(s.tmarked, 16)
                pool.indirect_dma_start(tdest[:, :], bass.IndirectOffsetOnAxis(lastt[0:HI, hi:hi + 1], 0),
                                        destv[0:HI, hi:hi + 1], None).then_inc(s.tmarked, 16)
            with pool.Fori(0, NG // 2) as i:
                for b in range(2):
                    pool.wait_ge(s.rec_gate, 4 * i + 2 * b + 2)
                    pool.wait_ge(s.rec_fill, 2 * i + b + 1)
                    pool.sem_inc(s.go, 1)
                    for j in range(GRP):
                        pool.indirect_dma_start(recS[:, :], bass.IndirectOffsetOnAxis(pst[0][:, b, j:j + 1], 0),
                                                rec[:, b, j, :], None).then_inc(s.rec_out[b], 16)
                        pool.indirect_dma_start(pairs[:, :], bass.IndirectOffsetOnAxis(pst[1][:, b, j:j + 1], 0),
                                                srcst[:, b, j:j + 1], None).then_inc(s.idx_out[b], 16)
            pool.wait_ge(s.tab0_w, 32)
            pool.wait_ge(s.null, 96)
            with pool.Fori(0, NIT) as i:
                for c in range(RINGC):
                    pool.wait_ge(s.l0_in[c], 16 * (i + 1))
                    pool.wait_ge(s.l0_stg, RINGC * i + c + 1)
                    pool.sem_inc(s.go, 1)
                    for j in range(SLOTS):
                        pool.indirect_dma_start(G0[c][:, j, :], None, tab0[:, :],
                                                bass.IndirectOffsetOnAxis(recLi[:, c, j, REC - 1:REC], 0)).then_inc(s.l0_g[c], 16)
                    pool.indirect_dma_start(Gq[:, c, 0:G], None, tabE[:, :],
                                            bass.IndirectOffsetOnAxis(stg[:, c, SLOTS:SLOTS + 1], 0)).then_inc(s.l0_g[c], 16)
            pool.wait_ge(s.st_out, 16 * (NIT + 1))
            for hi in range(HI):
                pool.indirect_dma_start(sA0[:, hi, :], None, st0[:, :],
                                        bass.IndirectOffsetOnAxis(lasti[:, hi:hi + 1], 0)).then_inc(s.st_g, 16)
                pool.indirect_dma_start(sC0[:, hi, :], None, cr0[:, :],
                                        bass.IndirectOffsetOnAxis(carryi[:, hi:hi + 1], 0)).then_inc(s.st_g, 16)
            with pool.Fori(0, LAYERS) as L:
                pool.wait_ge(s.tab_w, 32 * L + 32)
                pool.sem_inc(s.go, 1)
                with pool.Fori(0, NIT) as i:
                    for c in range(RINGC):
                        pool.wait_ge(s.colstg, (COLS + RINGC) * L + RINGC * i + c + 1)
                        pool.sem_inc(s.go, 1)
                        pool.indirect_dma_start(Gq[:, c, :], None, tabQ[:, :],
                                                bass.IndirectOffsetOnAxis(stg[:, c, SLOTS:SLOTS + 1], 0)).then_inc(s.col_g[c], 16)
                        for j in range(SLOTS):
                            pool.indirect_dma_start(Gk[:, c, j, :], None, tabK[:, :],
                                                    bass.IndirectOffsetOnAxis(stg[:, c, j:j + 1], 0)).then_inc(s.col_g[c], 16)
                pool.wait_ge(s.stA_out, (16 * (NIT + 1)) * L + 16 * (NIT + 1))
                pool.sem_inc(s.go, 1)
                for hi in range(HI):
                    pool.indirect_dma_start(sA[:, hi, :], None, stA[:, :],
                                            bass.IndirectOffsetOnAxis(lasti[:, hi:hi + 1], 0)).then_inc(s.stA_g, 16)
                    pool.indirect_dma_start(sC[:, hi, :], None, crA[:, :],
                                            bass.IndirectOffsetOnAxis(carryi[:, hi:hi + 1], 0)).then_inc(s.stA_g, 16)

        @block.scalar
        def _(act):
            act.wait_ge(s.zero_set, 1)
            wr = COLS * SLOTS * REC // ZW
            act.dma_start(recS.rearrange("(p r) c -> p (r c)", p=P).rearrange("p (a z) -> p a z", z=ZW),
                          bc(zero[:, 0:ZW], 1, wr)).then_inc(s.zeroed, 16)
            act.dma_start(pairs.rearrange("(p a t) c -> p a (t c)", p=P, a=2), bc(zero[:, :].bitcast(I32), 1, 2)).then_inc(s.zeroed, 16)
            act.dma_start(mark.rearrange("(p a) c -> p (a c)", p=P), zero[:, 0:COLS]).then_inc(s.zeroed, 16)
            act.dma_start(tfirst.rearrange("(p t) a -> p (t a)", p=2), zero[0:2, :]).then_inc(s.zeroed, 16)
            act.dma_start(tdest.rearrange("(p t) a -> p (t a)", p=2), zero[0:2, :].bitcast(I32)).then_inc(s.zeroed, 16)
            act.wait_ge(s.dist_ready, 1)
            done(act, nc.scalar.activation(cw[:, :], cw[:, :], ACT.Sin, bias=halfpi[:, 0:1], scale=-float(np.pi) / 6.0), s.cos_ready, 1)
            act.wait_ge(s.mult_ready, 1)
            done(act, nc.scalar.activation(logm[:, :], logm[:, :], ACT.Ln), s.logm_ready, 1)
            act.wait_ge(s.deg_ready, 1)
            done(act, nc.scalar.activation(n4[:, :], n3[:, :], ACT.Sqrt), s.sqdeg_ready, 1)
            with act.Fori(0, NG // 2) as i:
                for b in range(2):
                    g = 2 * i + b

                    def copies(k, n):
                        act.wait_ge(s.rk_T, 2 * g + k + 1)
                        act.wait_ge(s.rk_g, 2 * g)
                        nc.scalar.copy(ohtb[0:n, k, :, :].rearrange("p j e -> p (j e)"), tabT[k][0:n, 0:GRP * P]).then_inc(s.rk_cp, 1)
                        nc.scalar.copy(ohtf[0:n, k, :, :].rearrange("p j e -> p (j e)"), tabT[k][0:n, 0:GRP * P]).then_inc(s.rk_cp, 1)

                    def features(m):
                        act.wait_ge(s.m_T, 2 * g + m + 1)
                        nc.scalar.copy(aT[:, :], bank[0][0:RBF, :]).then_inc(s.m_aT, 1)

                    def hidden(m):
                        act.wait_ge(s.m_f1, 2 * g + m + 1)
                        nc.scalar.activation(hid[0:H, :], bank[1][0:H, :], ACT.Silu, bias=f1b[:, 0:1]).then_inc(s.m_hid, 1)

                    def gate(m):
                        act.wait_ge(s.m_f2, 2 * g + m + 1)
                        nc.scalar.copy(rec[:, b, 4 * m:4 * m + 4, RBF:RBF + H], bank[0][:, 0:4 * H].rearrange("p (j c) -> p j c", c=H)).then_inc(s.rec_gate, 1)

                    copies(0, P)
                    features(0)
                    copies(1, HI)
                    hidden(0)
                    gate(0)
                    features(1)
                    hidden(1)
                    gate(1)
            for g, (lo, hi) in enumerate(NT):
                act.wait_ge(s.e_T, g + 1)
                nc.scalar.copy(ebT[:, 0:(hi - lo) * P], bank[1][0:G, 0:(hi - lo) * P]).then_inc(s.e_Tc, 1)
                act.wait_ge(s.e_mm, g + 1)
                nc.scalar.copy(t0[:, lo:hi, H:H + G], bank[2][:, 0:(hi - lo) * G].rearrange("p (j c) -> p j c", c=G)).then_inc(s.e_done, 1)
            with act.Fori(0, NIT) as i:
                for c in range(RINGC):
                    act.wait_ge(s.l0_in[c], 16 * (i + 1))
                    act.dma_start(attrE[:, bass.ds(RINGC * i + c, 1), :].rearrange("p w (s c) -> p (w s) c", c=RBF),
                                  recL[:, c, :, 0:RBF]).then_inc(s.att_out[c], 16)

            def root(n):
                act.wait_ge(s.var_ready, n)
                done(act, nc.scalar.activation(n2[:, :], n1[:, :], ACT.Sqrt, bias=epsc[:, 0:1], scale=1.0 / H), s.std_ready, n)
            root(1)
            with act.Fori(0, LAYERS) as L:
                for g, (lo, hi) in enumerate(NT):
                    act.wait_ge(s.p_T, NNT * L + g + 1)
                    nc.scalar.copy(hT[0:H, g % 2, 0:(hi - lo) * P], bank[g % 2][0:H, 0:(hi - lo) * P]).then_inc(s.p_Tc, 1)
                    act.wait_ge(s.p_mm, NNT * L + g + 1)
                    nc.scalar.copy(qkm[:, lo:hi, :], bank[2 + g % 2][:, 0:(hi - lo) * 3 * H].rearrange("p (j c) -> p j c", c=3 * H)).then_inc(s.p_done, 1)
                root(3 * L + 2)
                root(3 * L + 3)
                with act.Fori(0, NIT) as i:
                    for c in range(RINGC):
                        w = COLS * L + RINGC * i + c
                        act.wait_ge(s.max_ready, w + 1)
                        q = c % 2
                        nc.scalar.activation(sc[:, q, 1, :], sc[:, q, 0, :], ACT.Exp, bias=scal[:, q, 2:3], accum_out=ar[:, q, 0:1]).then_inc(s.exp_ready, 1)
                        nc.scalar.activation(scal[:, q, 3:4], scal[:, q, 1:2], ACT.Exp, bias=scal[:, q, 2:3]).then_inc(s.exp_ready, 1)
                act.wait_ge(s.cmax_ready, L + 1)
                done(act, nc.scalar.activation(mtr[:, :], mrow[:, :], ACT.Exp, bias=c1[:, 0:1]), s.cexp_ready, L + 1)
                act.wait_ge(s.nmax_ready, L + 1)
                done(act, nc.scalar.activation(n3[:, :], n3[:, :], ACT.Exp), s.nexp_ready, 2 * L + 1)
                done(act, nc.scalar.activation(n4[:, :], n4[:, :], ACT.Exp), s.nexp_ready, 2 * L + 2)
                for g, (lo, hi) in enumerate(NT):
                    act.wait_ge(s.u_T, NNT * L + g + 1)
                    nc.scalar.copy(hT[:, g % 2, 0:(hi - lo) * P], bank[g % 2][0:2 * H, 0:(hi - lo) * P]).then_inc(s.u_Tc, 1)
                    act.wait_ge(s.u_mm, NNT * L + g + 1)
                    nc.scalar.copy(t1[:, lo:hi, :], bank[2 + g % 2][:, 0:(hi - lo) * H].rearrange("p (j c) -> p j c", c=H)).then_inc(s.u_done, 1)
                root(3 * L + 4)
            root(3 * LAYERS + 2)
            with act.Fori(0, STEPS) as L:
                act.wait_ge(s.g_ready, L + 1)
                for half in range(2):
                    with act.Fori(0, HI // ADJR) as i:
                        for k in range(ADJR):
                            act.wait_ge(s.adj_used, (2 * HI) * L + HI * half + ADJR * i + k + 1)
                            nc.scalar.copy(blk[:, k, :], t1[:, bass.ds(ADJR * i + k, 1), :].rearrange("p i c -> p (i c)")).then_inc(s.blk_ready, 1)
                    act.wait_ge(s.prop_mm, 2 * L + half + 1)
                    for q in range(len(prop)):
                        nc.scalar.copy(sums[:, half * NPH + q * PC:half * NPH + (q + 1) * PC], prop[q][0:H, 0:PC]).then_inc(s.prop_cp, 1)
            root(3 * LAYERS + 3)

        @block.tensor
        def _(pe):
            pe.wait_ge(s.const_ready, 1)
            pe.sem_inc(s.adj_used, ADJR)
            for k in range(3):
                nc.tensor.matmul(bank[k][:, 0:HI], zb[:, 0:P], zb[:, 0:HI], start=True, stop=False).then_inc(s.h_mm, 1)
            with pe.Fori(0, NG) as i:
                for k in range(2):
                    pe.wait_ge(s.h_oh[k], i + 1)
                    for j in range(GRP):
                        last = nc.tensor.matmul(bank[k][:, 0:HI], ohl[:, k, j, :], ohh[:, k, j, :], start=False, stop=False)
                    if k:
                        for j in range(GRP):
                            last = nc.tensor.matmul(bank[2][0:HI, 0:HI], ohh[:, 0, j, :], ohh[:, 1, j, :], start=False, stop=False)
                last.then_inc(s.h_mm, 3)
            for k in range(3):
                nc.tensor.matmul(bank[k][:, 0:HI], zb[:, 0:P], zb[:, 0:HI], start=False, stop=True).then_inc(s.h_all, 1)
            pe.wait_ge(s.cnt_ready, 1)
            nc.tensor.matmul(bank[3][:, 0:HI], triu[:, :], rowt[0][:, :], start=True, stop=True)
            nc.tensor.matmul(bank[3][:, 64:64 + HI], ones[:, :], rowt[0][:, :], start=True, stop=True).then_inc(s.pre_mm, 1)
            pe.wait_ge(s.cnt_ready, 2)
            nc.tensor.matmul(bank[0][0:HI, 0:HI], triu[0:HI, 0:HI], rowt[0][0:HI, :], start=True, stop=True)
            nc.tensor.matmul(bank[0][0:HI, 64:64 + HI], ones[0:HI, 0:HI], rowt[0][0:HI, :], start=True, stop=True).then_inc(s.pre_mm, 1)
            pe.wait_ge(s.scan_ready, 1)
            nc.tensor.matmul(bank[3][:, 0:1], triu[:, :], cum[:, COLS - 1:COLS], start=True, stop=True).then_inc(s.pre_mm, 1)
            pe.wait_ge(s.ends_ready, 1)
            nc.tensor.matmul(bank[3][:, 128:256], nfl[:, 0, :], ident[:, :], start=True, stop=True)
            nc.tensor.matmul(bank[3][:, 256:384], nfl[:, 1, :], ident[:, :], start=True, stop=True).then_inc(s.pre_mm, 1)
            pe.wait_ge(s.run_ready, 1)
            pe.wait_ge(s.par, PARS)
            n_lo = (P, HI)
            with pe.Fori(0, NG // 2) as i:
                for b in range(2):
                    g = 2 * i + b
                    left = [ohl[:, 0, :, :], ohh[:, 0, :, :]]
                    right = [ohh[:, 0, :, :], ohh[:, 1, :, :]]

                    def features(m):
                        pe.wait_ge(s.rec_gate, 2 * g + m)
                        pe.wait_ge(s.rec_in[b], 48 * (i + 1))
                        pe.sem_inc(s.go, 1)
                        for j in range(4):
                            last = nc.tensor.transpose(bank[0][0:RBF, j * P:(j + 1) * P], rec[:, b, 4 * m + j, 0:RBF], ident[:, :])
                        last.then_inc(s.m_T, 1)

                    def hidden(m):
                        pe.wait_ge(s.m_aT, 2 * g + m + 1)
                        pe.sem_inc(s.go, 1)
                        nc.tensor.matmul(bank[1][0:H, :], f1w[:, :], aT[:, :], start=True, stop=True).then_inc(s.m_f1, 1)

                    def gate(m):
                        pe.wait_ge(s.m_hid, 2 * g + m + 1)
                        pe.sem_inc(s.go, 1)
                        for j in range(4):
                            last = nc.tensor.matmul(bank[0][:, j * H:(j + 1) * H], hid[:, j * P:(j + 1) * P], f2w[:, :], start=True, stop=True)
                        last.then_inc(s.m_f2, 1)

                    def same(k):
                        pe.wait_ge(s.rk_cp, 4 * g + 2 * k + 2)
                        if k:
                            pe.wait_ge(s.rk_eqm, 2 * g + 1)
                        pe.sem_inc(s.go, 1)
                        n = n_lo[k]
                        for j in range(GRP):
                            last = nc.tensor.matmul(wide[0][:, j * P:(j + 1) * P], ohtb[0:n, k, j, :], ohtb[0:n, k, j, :], start=True, stop=True)
                        last.then_inc(s.rk_eq, 1)

                    def ranks(k):
                        pe.wait_ge(s.rk_eqm, 2 * g + k + 1)
                        pe.sem_inc(s.go, 1)
                        n = n_lo[k]
                        for j in range(GRP):
                            o = bank[2 + k][:, j * HI:(j + 1) * HI]
                            nc.tensor.matmul(o, eqm[:, k, j, :], right[k][:, j, :], start=True, stop=False)
                            last = nc.tensor.matmul(o, ohtf[0:n, k, j, :], run[0:n, k, j, :], start=False, stop=True)
                        last.then_inc(s.rk_g, 1)

                    pe.wait_ge(s.rk_oh, g + 1)
                    pe.sem_inc(s.go, 1)
                    for k in range(2):
                        n = n_lo[k]
                        for j in range(GRP):
                            last = nc.tensor.transpose(tabT[k][0:n, j * P:(j + 1) * P], left[k][:, j, :], identb[:, :])
                        last.then_inc(s.rk_T, 1)
                        for j in range(GRP):
                            last = nc.tensor.matmul(bank[2 + k][0:n, j * HI:(j + 1) * HI], left[k][:, j, :], right[k][:, j, :], start=True, stop=True)
                        last.then_inc(s.rk_cnt, 1)
                    features(0)
                    same(0)
                    hidden(0)
                    same(1)
                    ranks(0)
                    gate(0)
                    features(1)
                    ranks(1)
                    hidden(1)
                    gate(1)
            pe.wait_ge(s.rec_fill, NG)
            pe.wait_ge(s.emb_g, 16 * HI)
            for g, (lo, hi) in enumerate(NT):
                if g:
                    pe.wait_ge(s.e_Tc, g)
                for j in range(lo, hi):
                    last = nc.tensor.transpose(bank[1][0:G, (j - lo) * P:(j - lo + 1) * P], eb[:, j, :], ident[:, :])
                last.then_inc(s.e_T, 1)
                pe.wait_ge(s.e_Tc, g + 1)
                if g:
                    pe.wait_ge(s.e_done, g)
                for j in range(lo, hi):
                    last = nc.tensor.matmul(bank[2][:, (j - lo) * G:(j - lo + 1) * G], ebT[:, (j - lo) * P:(j - lo + 1) * P], adapt[:, :], start=True, stop=True)
                last.then_inc(s.e_mm, 1)
            pe.wait_ge(s.l0_done, COLS)
            nc.tensor.matmul(bank[0][:, 0:W1], maskQP[:, :], h0[:, RINGC - 1, :], start=True, stop=True).then_inc(s.carry_mm, 1)
            with pe.Fori(0, LAYERS) as L:
                pe.wait_ge(s.h_ready, L + 1)
                for g, (lo, hi) in enumerate(NT):
                    pe.wait_ge(s.p_done, NNT * L + max(g - 1, 0))
                    pe.sem_inc(s.go, 1)
                    for j in range(lo, hi):
                        last = nc.tensor.transpose(bank[g % 2][0:H, (j - lo) * P:(j - lo + 1) * P], h[:, j, :], ident[:, :])
                    last.then_inc(s.p_T, 1)
                    pe.wait_ge(s.p_Tc, NNT * L + g + 1)
                    pe.sem_inc(s.go, 1)
                    for j in range(lo, hi):
                        last = nc.tensor.matmul(bank[2 + g % 2][:, (j - lo) * 3 * H:(j - lo + 1) * 3 * H], hT[0:H, g % 2, (j - lo) * P:(j - lo + 1) * P],
                                                wqkm[:, bass.ds(L, 1), :].rearrange("p l c -> p (l c)"), start=True, stop=True)
                    last.then_inc(s.p_mm, 1)
                with pe.Fori(0, NIT) as i:
                    for c in range(RINGC):
                        pe.wait_ge(s.cnt_oh, (COLS * L) + RINGC * i + c + 1)
                        pe.sem_inc(s.go, 1)
                        for j in range(TOFF[c + 1] - TOFF[c]):
                            last = nc.tensor.matmul(wide[1][:, j * P:(j + 1) * P], oht[:, 0, j, :], oht[:, 1, j, :], start=True, stop=True)
                        last.then_inc(s.cnt_mm, 1)
                pe.wait_ge(s.cm_ready, L + 1)
                nc.tensor.matmul(wide[0][:, 0:P], mtr[:, :], ident[:, :], start=True, stop=True).then_inc(s.carryA_mm, 1)
                pe.wait_ge(s.cw_ready, L + 1)
                nc.tensor.transpose(wide[0][:, 512:512 + P], mtr[:, :], ident[:, :]).then_inc(s.carryA_mm, 1)
                pe.wait_ge(s.cwT_ready, L + 1)
                nc.tensor.matmul(wide[1][:, 0:W1], mrow[:, :], hist[:, RINGC - 1, 1:WS], start=True, stop=True).then_inc(s.carryA_mm, 1)
                pe.wait_ge(s.cat_ready, L + 1)
                for g, (lo, hi) in enumerate(NT):
                    pe.wait_ge(s.u_done, NNT * L + max(g - 1, 0))
                    pe.sem_inc(s.go, 1)
                    for j in range(lo, hi):
                        last = nc.tensor.transpose(bank[g % 2][0:2 * H, (j - lo) * P:(j - lo + 1) * P], cat[:, j, :], ident[:, :])
                    last.then_inc(s.u_T, 1)
                    pe.wait_ge(s.u_Tc, NNT * L + g + 1)
                    pe.sem_inc(s.go, 1)
                    for j in range(lo, hi):
                        last = nc.tensor.matmul(bank[2 + g % 2][:, (j - lo) * H:(j - lo + 1) * H], hT[:, g % 2, (j - lo) * P:(j - lo + 1) * P],
                                                wu[:, bass.ds(L, 1), :].rearrange("p l c -> p (l c)"), start=True, stop=True)
                    last.then_inc(s.u_mm, 1)
            with pe.Fori(0, STEPS) as L:
                pe.wait_ge(s.g_ready, L + 1)
                for half in range(2):
                    pe.wait_ge(s.prop_cp, (2 * len(prop)) * L + len(prop) * half)
                    pe.sem_inc(s.go, 1)
                    for q in range(len(prop)):
                        nc.tensor.matmul(prop[q][0:H, 0:PC], zb[:, 0:H], zb[:, 0:PC], start=True, stop=False)
                    with pe.Fori(0, HI // ADJR) as i:
                        for k in range(ADJR):
                            pe.wait_ge(s.adj_in[k], (32 * (HI // ADJR)) * L + 16 * (HI // ADJR) * half + 16 * i + 16)
                            pe.wait_ge(s.blk_ready, (2 * HI) * L + HI * half + ADJR * i + k + 1)
                            pe.sem_inc(s.go, 1)
                            for q in range(len(prop)):
                                last = nc.tensor.matmul(prop[q][0:H, 0:PC], blk[:, k, :], adjr[:, k, q * PC:(q + 1) * PC], start=False, stop=False)
                            last.then_inc(s.adj_used, 1)
                    for q in range(len(prop)):
                        last = nc.tensor.matmul(prop[q][0:H, 0:PC], zb[:, 0:H], zb[:, 0:PC], start=False, stop=True)
                    last.then_inc(s.prop_mm, 1)
                pe.wait_ge(s.prop_cp, (2 * len(prop)) * L + 2 * len(prop))
                pe.sem_inc(s.go, 1)
                for q in range(5):
                    lo, hi = 10 * q, min(10 * q + 10, HI)
                    for j in range(lo, hi):
                        last = nc.tensor.transpose(propT[q][:, (j - lo) * H:(j - lo + 1) * H], sums[:, j * P:(j + 1) * P], ident[0:H, 0:H])
                    last.then_inc(s.prop_T, 1)

        @block.vector
        def _(dve):
            v = Steps(dve, s.dve_step)
            V = nc.vector

            def tt(o, x, y, op):
                return V.tensor_tensor(o, x, y, op)

            for t in (x0, mult, zi, idxR, hist, ones, stg):
                v(V.memset(t[:], 1 if t is ones else 0))
            v(V.memset(zb[:], 0))
            v(V.memset(epsc[:], 1e-5))
            v(V.memset(halfpi[:], float(np.pi) / 2))
            v(V.memset(hid[:], 1.0))
            v(V.memset(zrow[:], 0))
            v(V.memset(nullA[:], 0))
            v(V.memset(nullK[:], 0))
            v(V.memset(nullA[:, 0:1], -BIG))
            v(V.memset(nullK[:, H:H + 1], -BIG))
            done(dve, V.memset(zero[:], 0), s.zero_set, 1)
            v(V.memset(rec[:], 0))
            done(dve, V.memset(rowb[:], 0), s.cleared, 1)
            dve.wait_ge(s.iota, 2)
            v(V.tensor_copy(iota[:], iotai[:]))
            v(V.tensor_copy(part[:], parti[:]))
            v(V.tensor_scalar(ident[:], iota[:], part[:, 0:1], None, ALU.is_equal))
            v(V.tensor_copy(identb[:], ident[:]))
            v(V.tensor_scalar(triu[:], iota[:], part[:, 0:1], None, ALU.is_gt))
            v(V.tensor_scalar(tril[:], iota[:], part[:, 0:1], None, ALU.is_lt))
            v(V.tensor_scalar(edge245[:], iota[:], float(COLS), None, ALU.mult))
            v(V.tensor_scalar(iotab1[:], iota[:], 1.0, None, ALU.add))
            done(dve, V.tensor_copy(iotab[:], iota[:]), s.const_ready, 1)
            dve.wait_ge(s.keys, 96)
            v(V.tensor_scalar(c1[:], part[:], float(P - 1), None, ALU.is_lt))
            v(V.tensor_scalar(c2[:], c1[:], -float(NP - 1), float(NP - 1), ALU.mult, ALU.add))
            for k in range(2):
                v(V.tensor_copy(key[k][:], rowi[k][:]))
                v(V.tensor_scalar(key[k][:, 0:PADS], rowi[k][:, 0:PADS], c1[:, 0:1], c2[:, 0:1], ALU.mult, ALU.add))
                v(V.tensor_scalar(keyt[:], key[k][:], P - 1, None, ALU.bitwise_and))
                v(V.tensor_copy(klo[k][:], keyt[:]))
                if k == 0:
                    v(V.tensor_scalar(pair[:], keyt[:], 256, 256, ALU.mult, ALU.add))
                else:
                    v(tt(pair[:], pair[:], keyt[:], ALU.add))
                v(V.tensor_scalar(keyt[:], key[k][:], 7, None, ALU.logical_shift_right))
                v(V.tensor_copy(khi[k][:], keyt[:]))
                v(V.tensor_scalar(rowi[k][:], rowi[k][:], 1, None, ALU.add))
            within = key[0][:, :].bitcast(F32)
            v(V.tensor_scalar(within[:, :], cw[:], 6.0, None, ALU.is_lt))
            done(dve, V.tensor_scalar(cw[:], cw[:], 6.0, None, ALU.min), s.dist_ready, 1)
            dve.wait_ge(s.nodes, 96)
            done(dve, V.tensor_scalar(logm[:], mult[:], 1.0, None, ALU.max), s.mult_ready, 1)
            dve.wait_ge(s.cos_ready, 1)
            v(V.tensor_scalar(cw[:], cw[:], 1.0, 0.5, ALU.add, ALU.mult))
            v(tt(cw[:], cw[:], within[:, :], ALU.mult))

            def one_hot(o, keys, i, n):
                return tt(o, bc(keys[:, bass.ds(GRP * i, GRP)], 2, n), bc(iotab[:, 0:n], 1, GRP), ALU.is_equal)

            with dve.Fori(0, NG) as i:
                for k in range(2):
                    dve.wait_ge(s.h_mm, 3 * i + 3)
                    one_hot(ohl[:, k, :, :], klo[k], i, P)
                    one_hot(ohh[:, k, :, :], khi[k], i, HI).then_inc(s.h_oh[k], 1)
            dve.wait_ge(s.h_all, 3)
            cnt, rows, last, tmp = rowt[1], rowt[0], rowt[1], rowt[2]

            def ceil_div(o, per):
                v(V.tensor_scalar(sort_i[:], cnt[:], float(per - 1), None, ALU.add))
                v(V.tensor_scalar(sort_i[:], sort_i[:], per.bit_length() - 1, None, ALU.logical_shift_right))
                return V.tensor_scalar(o, sort_i[:], 1.0, None, ALU.max)

            v(V.tensor_copy(cnt[:], bank[1][:, 0:HI]))
            done(dve, V.tensor_scalar(n3[:], cnt[:], 1.0, None, ALU.add), s.deg_ready, 1)
            dve.wait_ge(s.sqdeg_ready, 1)
            v(V.reciprocal(dinv[:], n4[:]))
            v(V.tensor_copy(cnt[:], bank[0][:, 0:HI]))
            done(dve, ceil_div(rows[:], SLOTS), s.cnt_ready, 1)
            dve.wait_ge(s.pre_mm, 1)
            v(V.tensor_tensor_scan(tmp[:], bank[3][:, 64:64 + HI], zrow[:, 0:HI], 0.0, ALU.add, ALU.add))
            v(tt(tmp[:], tmp[:], bank[3][:, 64:64 + HI], ALU.subtract))
            v(tt(rowb[:], tmp[:], bank[3][:, 0:HI], ALU.add))
            done(dve, V.tensor_copy(rowbi[:], rowb[:]), s.rows_ready, 1)
            v(tt(last[:], rowb[:], rows[:], ALU.add))
            v(V.tensor_scalar(last[:], last[:], -1.0, None, ALU.add))
            v(V.tensor_copy(lasti[:], last[:]))
            v(tt(rcp, bc(last[:, :], 2, P), bc(edge245[:, :], 1, HI), ALU.is_ge))
            v(V.tensor_reduce(tmp[:], rcp, AX, ALU.add))
            v(V.tensor_scalar(rowt[3][:], tmp[:], float(COLS), -float(COLS), ALU.mult, ALU.add))
            v(tt(rowt[3][:], rowb[:], rowt[3][:], ALU.is_lt))
            v(tt(carryi[:], rowt[3][:], tmp[:], ALU.mult))
            v(V.tensor_scalar(run[:, 0, 0, :], rowb[:], float(SLOTS), None, ALU.mult))
            v(V.tensor_copy(cnt[0:HI, :], bank[2][0:HI, 0:HI]))
            done(dve, ceil_div(rows[:], P), s.cnt_ready, 2)
            dve.wait_ge(s.pre_mm, 2)
            v(V.tensor_tensor_scan(tmp[0:HI, :], bank[0][0:HI, 64:64 + HI], zrow[0:HI, 0:HI], 0.0, ALU.add, ALU.add))
            v(tt(tmp[0:HI, :], tmp[0:HI, :], bank[0][0:HI, 64:64 + HI], ALU.subtract))
            v(tt(tmp[0:HI, :], tmp[0:HI, :], bank[0][0:HI, 0:HI], ALU.add))
            v(V.tensor_copy(firstt[0:HI, :], tmp[0:HI, :]))
            v(V.tensor_scalar(run[0:HI, 1, 0, :], tmp[0:HI, :], float(P), None, ALU.mult))
            v(tt(last[0:HI, :], tmp[0:HI, :], rows[0:HI, :], ALU.add))
            v(V.tensor_scalar(lastt[0:HI, :], last[0:HI, :], -1.0, None, ALU.add))
            v(V.tensor_scalar(c1[:], part[:], float(NP), 1.0, ALU.mult, ALU.add))
            done(dve, V.tensor_scalar(destv[0:HI, :], iota[0:HI, 0:HI], c1[0:HI, 0:1], None, ALU.add), s.tiles_ready, 1)
            dve.wait_ge(s.mark_ld, 16)
            done(dve, V.tensor_tensor_scan(cum[:], markt[:, :], zrow[:, :], 0.0, ALU.add, ALU.add), s.scan_ready, 1)
            v(V.tensor_scalar(drop[:], markt[:], -BIG, None, ALU.mult))
            v(V.tensor_scalar(keep[:], markt[:], -1.0, 1.0, ALU.mult, ALU.add))
            dve.wait_ge(s.pre_mm, 3)
            v(V.tensor_copy(c1[:], bank[3][:, 0:1]))
            v(V.tensor_scalar(nodef[:], cum[:], c1[:, 0:1], None, ALU.add))
            v(V.tensor_copy(idxR[:, 0:COLS, SLOTS:SLOTS + 1], nodef[:, :].unsqueeze(2)))
            v(V.tensor_scalar(nfl[:, 0, :], ones[:], nodef[:, 0:1], None, ALU.mult))
            done(dve, V.tensor_scalar(nfl[:, 1, :], ones[:], nodef[:, COLS - 1:COLS], None, ALU.mult), s.ends_ready, 1)
            dve.wait_ge(s.pre_mm, 4)
            v(V.scalar_tensor_tensor(maskQP[:], bank[3][:, 128:256], nodef[:, COLS - 1:COLS], triu[:], ALU.is_equal, ALU.mult))
            v(V.scalar_tensor_tensor(maskPQ[:], bank[3][:, 256:384], nodef[:, 0:1], tril[:], ALU.is_equal, ALU.mult))
            done(dve, V.tensor_scalar(maskneg[:], maskPQ[:], -1.0, BIG, ALU.add, ALU.mult), s.run_ready, 1)
            counted = (P, HI)
            with v.loop(NG // 2, 2 * (2 * (GRP + 3) + 3)) as i:
                for b in range(2):
                    g = 2 * i + b
                    cols = bass.ds(GRP * g, GRP)
                    one_hot(ohl[:, 0, :, :], klo[0], g, P)
                    one_hot(ohh[:, 0, :, :], khi[0], g, HI)
                    one_hot(ohh[:, 1, :, :], khi[1], g, HI).then_inc(s.rk_oh, 1)
                    for k in range(2):
                        n = counted[k]
                        dve.wait_ge(s.rk_cnt, 2 * g + k + 1)
                        for j in range(GRP):
                            v(tt(run[0:n, k, j + 1, :], run[0:n, k, j, :], bank[2 + k][0:n, j * HI:(j + 1) * HI], ALU.add))
                        dve.wait_ge(s.rk_eq, 2 * g + k + 1)
                        tt(eqm[:, k, :, :], wide[0][:, :].rearrange("p (j e) -> p j e", e=P), bc(triu[:, :], 1, GRP),
                           ALU.mult).then_inc(s.rk_eqm, 1)
                    for k in range(2):
                        n = counted[k]
                        dve.wait_ge(s.rk_g, 2 * g + k + 1)
                        v(tt(gsel[:, k, :, :], bank[2 + k][:, 0:OH].rearrange("p (j c) -> p j c", c=HI), ohh[:, k, :, :], ALU.mult))
                        v(V.tensor_reduce(posf[:, k, :], gsel[:, k, :, :], AX, ALU.add))
                        v(V.tensor_copy(run[0:n, k, 0, :], run[0:n, k, GRP, :]))
                    dve.wait_ge(s.rec_out[b], 16 * GRP * i)
                    dve.wait_ge(s.idx_out[b], 16 * GRP * i)
                    V.tensor_copy(pst[0][:, b, :], posf[:, 0, :])
                    v(V.tensor_copy(qi[:, 0, :], posf[:, 1, :]))
                    v(V.tensor_scalar(qi[:, 1, :], qi[:, 0, :], 7, None, ALU.logical_shift_right))
                    v(V.tensor_scalar(qi[:, 0, :], qi[:, 0, :], P - 1, None, ALU.bitwise_and))
                    V.scalar_tensor_tensor(pst[1][:, b, :], qi[:, 0, :], NTC, qi[:, 1, :], ALU.mult, ALU.add)
                    V.tensor_scalar(rec[:, b, :, REC - 2], cw[:, cols], 1.0, None, ALU.mult)
                    V.tensor_scalar(reci[:, b, :, REC - 1], rowi[1][:, cols], 0, None, ALU.add)
                    V.tensor_scalar(srcst[:, b, :], pair[:, cols], 0, None, ALU.add).then_inc(s.rec_fill, 1)
            v(V.tensor_copy(t0[:, :, 0:H], x0[:, :, :]))
            dve.wait_ge(s.e_done, NNT)
            done(dve, V.tensor_copy(t0[:, :, W0 - 1:W0], mult[:, :].unsqueeze(2)), s.t0_ready, 1)
            for b in range(2):
                dve.wait_ge(s.rec_out[b], 16 * GRP * (NG // 2))
                dve.wait_ge(s.idx_out[b], 16 * GRP * (NG // 2))
            tkt = tkeep[:, :].bitcast(I32)
            dve.wait_ge(s.pair_ld, 16)
            dve.wait_ge(s.zeroed, 80)
            dve.wait_ge(s.null, 96)
            v(V.tensor_scalar(tkt, pairt, 8, None, ALU.logical_shift_right))
            v(V.tensor_copy(plo, tkt))
            v(V.tensor_scalar(tkt, pairt, 255, None, ALU.bitwise_and))
            done(dve, V.tensor_copy(phi[:, :], tkt), s.unpacked, 1)
            dve.wait_ge(s.slot_ld, 16)
            v(V.tensor_scalar(tnone[:, :], tslot[:, :], 0, None, ALU.is_equal))
            v(V.tensor_scalar(c1[:], part[:], float(NP * HI + 1), None, ALU.add))
            v(V.tensor_scalar(tnone[:, :], tnone[:, :], c1[0:TPI, 0:1], -1.0, ALU.mult, ALU.add))
            done(dve, tt(tslot[:, :], tslot[:, :], tnone[:, :], ALU.add), s.slots_ready, 1)
            dve.wait_ge(s.keep_ld, 16)
            v(V.tensor_scalar(tkeep[:, :], tkeep[:, :], -1.0, 1.0, ALU.mult, ALU.add))
            v(V.memset(acc[:], 0))

            def by_slot(ap):
                return ap.rearrange("p s c -> p c s")

            def int_copy(o, i_):
                return V.tensor_scalar(o, i_, 0, None, ALU.add)

            for c in range(RINGC):
                done(dve, int_copy(stg[:, c, SLOTS:], idxR[:, c, SLOTS:]), s.l0_stg, c + 1)
            with v.loop(NIT, 9 * RINGC) as i:
                dve.wait_ge(s.st_out, 16 * i)
                for c in range(RINGC):
                    w = RINGC * i + c
                    dve.wait_ge(s.l0_g[c], 16 * (SLOTS + 1) * (i + 1))
                    g0 = G0[c]
                    v(tt(prod[:, :, 0:G], g0[:, :, H:H + G], bc(Gq[:, c, 0:G], 1, SLOTS), ALU.mult))
                    v(V.tensor_reduce(sc[:, 0, 0, :], prod[:, :, 0:G], AX, ALU.add))
                    v(tt(prod2[:, :, :], recL[:, c, :, RBF:RBF + H], bc(sc[:, 0, 0, :], 2, H), ALU.add))
                    v(tt(prod2[:, :, :], prod2[:, :, :], g0[:, :, 0:H], ALU.mult))
                    v(tt(sc[:, 0, 1, :], recL[:, c, :, REC - 2], g0[:, :, W0 - 1], ALU.mult))
                    v(tt(prod2[:, :, :], prod2[:, :, :], bc(sc[:, 0, 1, :], 2, H), ALU.mult))
                    v(V.tensor_reduce(ar[:, 0, 0:H], by_slot(prod2[:, :, :]), AX, ALU.add))
                    v(V.tensor_reduce(ar[:, 0, H:W1], g0[:, :, W0 - 1], AX, ALU.add))
                    v(int_copy(idxR[:, bass.ds(w, 1), 0:SLOTS].rearrange("p w s -> p (w s)"), recLi[:, c, :, REC - 1]))
                    done(dve, V.scalar_tensor_tensor(h0[:, c, :], h0[:, (c - 1) % RINGC, :], keep[:, bass.ds(w, 1)], ar[:, 0, :],
                                                     ALU.mult, ALU.add), s.l0_done, w + 1)
                    done(dve, int_copy(stg[:, c, SLOTS:], idxR[:, bass.ds(w + RINGC, 1), SLOTS:].rearrange("p w s -> p (w s)")),
                         s.l0_stg, w + RINGC + 1)
            dve.wait_ge(s.carry_mm, 1)
            done(dve, V.tensor_copy(cin[:, 0:W1], bank[0][:, 0:W1]), s.carry_ready, 1)

            def layer_norm(o, x, n, gain=None, bias=None, signal=None, value=None):
                v(V.tensor_reduce(n1[:, :], x, AX, ALU.add))
                v(V.tensor_scalar(n1[:, :], n1[:, :], 1.0 / H, None, ALU.mult))
                v(tt(t2[:, :, :], x, bc(n1[:, :], 2, H), ALU.subtract))
                v(tt(o, t2[:, :, :], t2[:, :, :], ALU.mult))
                done(dve, V.tensor_reduce(n1[:, :], o, AX, ALU.add), s.var_ready, n)
                dve.wait_ge(s.std_ready, n)
                v(V.reciprocal(n3[:, :], n2[:, :]))
                last = tt(o, t2[:, :, :], bc(n3[:, :], 2, H), ALU.mult)
                if gain is not None:
                    v(last)
                    v(tt(o, o, gain, ALU.mult))
                    last = tt(o, o, bias, ALU.add)
                if signal is None:
                    v(last)
                else:
                    done(dve, last, signal, value)

            for c in range(RINGC):
                dve.wait_ge(s.att_out[c], 16 * NIT)
            dve.wait_ge(s.st_g, 32 * HI)
            dve.wait_ge(s.par, PARS)
            v(tt(sA0[:, :, :], sA0[:, :, :], sC0[:, :, :], ALU.add))
            v(V.tensor_scalar(n1[:, :], sA0[:, :, H], 1e-8, None, ALU.max))
            v(V.reciprocal(n4[:, :], n1[:, :]))
            v(tt(t1[:, :, :], sA0[:, :, 0:H], bc(n4[:, :], 2, H), ALU.mult))
            v(tt(t1[:, :, :], t1[:, :, :], x0[:, :, :], ALU.add))

            def all_nodes(p):
                return p.to_broadcast([P, HI, H])

            layer_norm(h[:, :, :], t1[:, :, :], 1, all_nodes(lnn["gn"][:, :, :]), all_nodes(lnn["bn"][:, :, :]), s.h_ready, 1)

            def layer(L):
                def par(n):
                    return all_nodes(lnp[n][:, bass.ds(L, 1), :])

                dve.wait_ge(s.p_done, NNT * L + NNT)
                layer_norm(qkm[:, :, 0:H], qkm[:, :, 0:H], 3 * L + 2, par("gq"), par("bq"), s.q_ready, L + 1)
                layer_norm(kt[:, :, 0:H], qkm[:, :, H:2 * H], 3 * L + 3, par("gk"), par("bk"))
                v(V.tensor_copy(kt[:, :, H:H + 1], logm[:, :].unsqueeze(2)))
                done(dve, V.tensor_copy(kt[:, :, H + 1:WK], qkm[:, :, 2 * H:3 * H]), s.k_ready, L + 1)
                v(V.memset(hist[:, RINGC - 1, :], 0))
                v(V.memset(hist[:, RINGC - 1, 0:1], -BIG))
                for c in range(RINGC):
                    done(dve, int_copy(stg[:, c, :], idxR[:, c, :]), s.colstg, (COLS + RINGC) * L + c + 1)

            def beat(L, i, c):
                score, message = c < RINGC, c > 0
                if score:
                    w, q, n = RINGC * i + c, c % 2, TOFF[c + 1] - TOFF[c]
                    prev = hist[:, (c - 1) % RINGC, :]
                    dve.wait_ge(s.att_in[c], (16 * NIT) * L + 16 * i + 16)
                    dve.wait_ge(s.col_g[c], (16 * (SLOTS + 1) * NIT) * L + 16 * (SLOTS + 1) * i + 16 * (SLOTS + 1))
                    v.start(tt(prod[:, :, 0:H], Gk[:, c, :, 0:H], bc(Gq[:, c, :], 1, SLOTS), ALU.mult))
                    dots = v.start(V.scalar_tensor_tensor(prod[:, :, H:], att[:, c, :, :], 0.1, bc(Gq[:, c, 0:RBF], 1, SLOTS), ALU.mult, ALU.mult))
                if message:
                    c0, q0 = c - 1, (c - 1) % 2
                    w0 = RINGC * i + c0
                    dve.wait_ge(s.exp_ready, (2 * COLS) * L + 2 * w0 + 2)
                    terms = v.start(tt(prod2[:, :, :], Gk[:, c0, :, H + 1:WK], bc(sc[:, q0, 1, :], 2, H), ALU.mult))
                if score:
                    cols = bass.ds((TPI * NIT) * L + TPI * i + TOFF[c], n)
                    tt(oht[:, 0, 0:n, :], bc(plo[:, cols], 2, P), bc(iotab1[:, :], 1, n), ALU.is_equal)
                    v.after(dots)
                    sums = v.start(V.tensor_reduce(sc[:, q, 0, :], prod[:, :, :], AX, ALU.add))
                if message:
                    v.after(terms)
                    msum = v.start(V.tensor_reduce(ar[:, q0, 1:W1], by_slot(prod2[:, :, :]), AX, ALU.add))
                if score:
                    tt(oht[:, 1, 0:n, :], bc(phi[:, cols], 2, P), bc(iotab[:, :], 1, n), ALU.is_equal).then_inc(s.cnt_oh, 1)
                    v.after(sums)
                    full = v.start(tt(sc[:, q, 0, :], sc[:, q, 0, :], Gk[:, c, :, H], ALU.add))
                if message:
                    fade = v.start(tt(scal[:, q0, 4:5], scal[:, q0, 3:4], keep[:, bass.ds(w0, 1)], ALU.mult))
                if score:
                    if c == 0:
                        dve.wait_ge(s.stA_out, (16 * (NIT + 1)) * L + 16 * i)
                    ran = v.start(tt(scal[:, q, 1:2], prev[:, 0:1], drop[:, bass.ds(w, 1)], ALU.add))
                    v.after(full)
                    top = v.start(V.tensor_reduce(scal[:, q, 0:1], sc[:, q, 0, :], AX, ALU.max))
                if message:
                    v.after(fade)
                    if c0:
                        dve.wait_ge(s.col_done, COLS * L + w0)
                    V.scalar_tensor_tensor(hist[:, c0, 1:WS], hist[:, (c0 - 1) % RINGC, 1:WS], scal[:, q0, 4:5], ar[:, q0, :],
                                           ALU.mult, ALU.add).then_inc(s.col_done, 1)
                if score:
                    v.after(top)
                    peak = v.start(tt(hist[:, c, 0:1], scal[:, q, 0:1], scal[:, q, 1:2], ALU.max))
                if message:
                    int_copy(stg[:, c0, :], idxR[:, bass.ds(w0 + RINGC, 1), :].rearrange("p w s -> p (w s)")).then_inc(s.colstg, 1)
                if score:
                    v.after(peak)
                    V.tensor_scalar(scal[:, q, 2:3], hist[:, c, 0:1], -1.0, None, ALU.mult).then_inc(s.max_ready, 1)
                    dve.wait_ge(s.cnt_mm, COLS * L + w + 1)
                    back = 1 if c < 2 else 0
                    r = (4, 3, 0, 1, 2)[c]
                    nr = TOFF[r + 1] - TOFF[r]
                    dve.wait_ge(s.cnt_out[r], (16 * nr * NIT) * L + 16 * nr * i + (0 if back else 16 * nr))
                    for j in range(TOFF[c], TOFF[c + 1]):
                        before = acc_slot(c, j - 1) if j > TOFF[c] else acc_slot((c - 1) % RINGC, TOFF[(c - 1) % RINGC + 1] - 1)
                        t = (TPI * NIT) * L + TPI * i + j
                        if j == TOFF[c]:
                            dve.wait_ge(s.cnt_done, COLS * L + w)
                        last = V.scalar_tensor_tensor(acc[:, acc_slot(c, j), :], acc[:, before, :], tkeep[:, bass.ds(t, 1)],
                                                      wide[1][:, (j - TOFF[c]) * P:(j - TOFF[c] + 1) * P], ALU.mult, ALU.add)
                        if j < TOFF[c + 1] - 1:
                            v(last)
                    last.then_inc(s.cnt_done, 1)

            def finish_layer(L):
                done(dve, V.tensor_scalar(mtr[:], ones[:], hist[:, RINGC - 1, 0:1], None, ALU.mult), s.cm_ready, L + 1)
                dve.wait_ge(s.carryA_mm, 3 * L + 1)
                v(tt(mrow[:], wide[0][:, 0:P], maskPQ[:], ALU.mult))
                v(tt(mrow[:], mrow[:], maskneg[:], ALU.add))
                v(V.tensor_reduce(cin[:, 0:1], mrow[:], AX, ALU.max))
                done(dve, V.tensor_scalar(c1[:], cin[:, 0:1], -1.0, None, ALU.mult), s.cmax_ready, L + 1)
                dve.wait_ge(s.cexp_ready, L + 1)
                done(dve, tt(mtr[:], mtr[:], maskPQ[:], ALU.mult), s.cw_ready, L + 1)
                dve.wait_ge(s.carryA_mm, 3 * L + 2)
                done(dve, V.tensor_copy(mrow[:], wide[0][:, 512:512 + P]), s.cwT_ready, L + 1)
                dve.wait_ge(s.carryA_mm, 3 * L + 3)
                done(dve, V.tensor_copy(cin[:, 1:WS], wide[1][:, 0:W1]), s.carryA_ready, L + 1)
                dve.wait_ge(s.stA_g, (32 * HI) * L + 32 * HI)
                v(tt(n1[:, :], sA[:, :, 0], sC[:, :, 0], ALU.max))
                v(tt(n3[:, :], sA[:, :, 0], n1[:, :], ALU.subtract))
                done(dve, tt(n4[:, :], sC[:, :, 0], n1[:, :], ALU.subtract), s.nmax_ready, L + 1)
                dve.wait_ge(s.nexp_ready, 2 * L + 2)
                v(tt(sA[:, :, 1:WS], sA[:, :, 1:WS], bc(n3[:, :], 2, W1), ALU.mult))
                v(tt(sC[:, :, 1:WS], sC[:, :, 1:WS], bc(n4[:, :], 2, W1), ALU.mult))
                v(tt(sA[:, :, 1:WS], sA[:, :, 1:WS], sC[:, :, 1:WS], ALU.add))
                v(V.tensor_scalar(n1[:, :], sA[:, :, 1], 1e-10, None, ALU.add))
                v(V.reciprocal(n4[:, :], n1[:, :]))
                v(tt(cat[:, :, H:2 * H], sA[:, :, 2:WS], bc(n4[:, :], 2, H), ALU.mult))
                done(dve, V.tensor_copy(cat[:, :, 0:H], h[:, :, :]), s.cat_ready, L + 1)
                dve.wait_ge(s.u_done, NNT * L + NNT)
                v(V.tensor_scalar(t2[:, :, :], t1[:, :, :], 0.01, None, ALU.mult))
                v(tt(t1[:, :, :], t1[:, :, :], t2[:, :, :], ALU.max))
                v(tt(t1[:, :, :], t1[:, :, :], h[:, :, :], ALU.add))
                layer_norm(h[:, :, :], t1[:, :, :], 3 * L + 4, all_nodes(lnp["go"][:, bass.ds(L, 1), :]),
                           all_nodes(lnp["bo"][:, bass.ds(L, 1), :]), s.h_ready, L + 2)

            around = 39
            with v.loop(LAYERS, (10 * RINGC + TPI - RINGC) * NIT + around) as L:
                layer(L)
                dve.sem_inc(s.go, 1)
                with v.loop(NIT, 10 * RINGC + TPI - RINGC) as i:
                    for c in range(RINGC + 1):
                        beat(L, i, c)
                dve.wait_ge(s.col_done, COLS * L + COLS)
                finish_layer(L)
            v(tt(t1[:, :, :], x0[:, :, :], h[:, :, :], ALU.add))
            layer_norm(h[:, :, :], t1[:, :, :], 3 * LAYERS + 2)
            v(V.tensor_copy(cat[:, :, 0:H], h[:, :, :]))
            done(dve, V.tensor_scalar(cat[:, :, H:2 * H], h[:, :, :], ALPHA, None, ALU.mult), s.x_ready, 1)
            with v.loop(STEPS, 7) as L:
                done(dve, tt(t1[:, :, :], h[:, :, :], bc(dinv[:, :], 2, H), ALU.mult), s.g_ready, L + 1)
                for q in range(5):
                    dve.wait_ge(s.prop_T, 5 * L + q + 1)
                    lo, hi = 10 * q, min(10 * q + 10, HI)
                    v(tt(t2[:, lo:hi, :], propT[q][:, 0:(hi - lo) * H].rearrange("p (j c) -> p j c", c=H), t1[:, lo:hi, :], ALU.add))
                v(tt(t2[:, :, :], t2[:, :, :], bc(dinv[:, :], 2, H), ALU.mult))
                v(V.scalar_tensor_tensor(h[:, :, :], t2[:, :, :], RING, cat[:, :, H:2 * H], ALU.mult, ALU.add))
            v(tt(t1[:, :, :], cat[:, :, 0:H], h[:, :, :], ALU.add))
            layer_norm(h[:, :, :], t1[:, :, :], 3 * LAYERS + 3, signal=s.result, value=1)


def kernel(**inputs):
    import concourse.bacc as bacc
    from concourse.bass_utils import run_bass_kernel_spmd

    nc = bacc.Bacc("TRN2", target_bir_lowering=False, num_devices=1)
    arrays, io = {}, {}
    for name, value in inputs.items():
        a = np.ascontiguousarray(value)
        arrays[f"in_{name}"] = a
        io[name] = nc.dram_tensor(f"in_{name}", a.shape, mybir.dt.from_np(a.dtype), kind="ExternalInput").ap()
    out = nc.dram_tensor("out_0", (N, H), F32, kind="ExternalOutput").ap()
    build(nc, io, out)
    r = run_bass_kernel_spmd(nc, [arrays], core_ids=[0])
    return r.results[0]["out_0"]
```

```python
import concourse.bass as bass
import numpy as np
from concourse import mybir
from contextlib import ExitStack, contextmanager

F32 = mybir.dt.float32
BF16 = mybir.dt.bfloat16
F16 = mybir.dt.float16
I32 = mybir.dt.int32
ALU = mybir.AluOpType
ACT = mybir.ActivationFunctionType
AX = mybir.AxisListType.X

P = 128
N = 6250
E = 200000
H = 48
RBF = 40
LAYERS = 4
G = 32
NELEM = 119
STEPS = 5
RING = 0.2
ALPHA = 0.8
HI = -(-N // P)
NP = HI * P
ADJR = 7
NPH = NP // 2
PC = NPH // 7
LASTN = N - (HI - 1) * P
GRP = 8
KE = -(-E // (P * GRP)) * GRP
NG = KE // GRP
PADS = P * KE - E
SLOTS = 8
ROWS = NP + P * KE // SLOTS
COLS = -(-ROWS // P)
RECR = 4
assert NG % RECR == 0
RINGC = 5
NIT = COLS // RINGC
assert NIT * RINGC == COLS
ZW = COLS * SLOTS
PARS = 16 * 17
REC = RBF + H + 2
W0 = H + G + 1
WK = 2 * H + 1
TPI = 21
TOFF = [0, 4, 8, 12, 16, TPI]
NTC = LAYERS * NIT * TPI
assert NTC >= HI * HI + P * KE // P
PART = 16.0
assert P * max(COLS * SLOTS, NTC) < PART * 2 ** 16
WS = H + 2
W1 = H + 1
BIG = 1e30
NT = [(a, min(a + 3, HI)) for a in range(0, HI, 3)]
NNT = len(NT)


def done(eng, ins, signal, value):
    ins.then_inc(signal, 1)
    eng.wait_ge(signal, value)


class Steps:

    def __init__(self, eng, signal):
        self.eng, self.sem, self.base, self.k = eng, signal, 0, 0

    def __call__(self, ins):
        self.k += 1
        ins.then_inc(self.sem, 1)
        self.eng.wait_ge(self.sem, self.base + self.k)

    def start(self, ins):
        self.k += 1
        ins.then_inc(self.sem, 1)
        return self.k

    def after(self, k):
        self.eng.wait_ge(self.sem, self.base + k)

    @contextmanager
    def loop(self, n, per):
        base, k = self.base, self.k
        with self.eng.Fori(0, n) as i:
            self.base, self.k = base + k + i * per, 0
            yield i
            assert self.k == per, (self.k, per)
        self.base, self.k = base, k + n * per


def bc(ap, axis, n):
    a = ap.unsqueeze(axis)
    shape = list(a.shape)
    shape[axis] = n
    return a.to_broadcast(shape)


def build(nc, io, out):
    ctx = ExitStack()
    with ctx:
        def sem(name):
            return ctx.enter_context(nc.semaphore(name))

        def dram(name, shape, dt=F32):
            return nc.dram_tensor(name, shape, dt, kind="Internal").ap()

        def sbx(c):
            return lambda name, shape, dt=F32: c.enter_context(nc.sbuf_tensor(name, shape, dt))

        sb = sbx(ctx)
        recS = dram("recS", (P * COLS * SLOTS, REC))
        pairs = dram("pairs", (P * NTC, 1), I32)
        tfirst = dram("tfirst", (NTC, 1))
        tdest = dram("tdest", (NTC, 1), I32)
        adj = dram("adj", ((HI + 1) * P * HI, P))
        attrE = dram("attrE", (P, COLS, SLOTS * RBF))
        mark = dram("mark", (P * COLS, 1))
        tab0 = dram("tab0", (NP + 1, W0))
        tabE = dram("tabE", (NP + 1, G))
        tabQ = dram("tabQ", (NP + 1, H))
        tabK = dram("tabK", (NP + 1, WK))
        st0 = dram("st0", (P * COLS, W1))
        stA = dram("stA", (P * COLS, WS))
        cr0 = dram("cr0", (NP + 1 + P, W1))
        crA = dram("crA", (NP + 1 + P, WS))

        iotai = sb("iotai", [P, P], I32)
        parti = sb("parti", [P, 1], I32)
        iota = sb("iota", [P, P])
        iotab = sb("iotab", [P, P], BF16)
        part = sb("part", [P, 1])
        ident = sb("ident", [P, P])
        identb = sb("identb", [P, P], BF16)
        triu = sb("triu", [P, P])
        tril = sb("tril", [P, P])
        ones = sb("ones", [P, P])
        edge245 = sb("edge245", [P, P])
        iotab1 = sb("iotab1", [P, P], BF16)
        zb = sb("zb", [P, 512], BF16)
        epsc = sb("epsc", [P, 1])
        halfpi = sb("halfpi", [P, 1])
        nullA = sb("nullA", [P, WS])
        nullK = sb("nullK", [1, WK])
        lnp = {n: sb(f"p_{n}", [P, LAYERS, H]) for n in ("gq", "bq", "gk", "bk", "go", "bo")}
        lnn = {n: sb(f"p_{n}", [P, 1, H]) for n in ("gn", "bn")}
        wqkm = sb("wqkm", [H, LAYERS, 3 * H])
        wu = sb("wu", [2 * H, LAYERS, H])
        f1w = sb("f1w", [RBF, H])
        f1b = sb("f1b", [H, 1])
        f2w = sb("f2w", [H + 1, H])
        adapt = sb("adapt", [G, G])
        x0 = sb("x0", [P, HI, H])
        h = sb("h", [P, HI, H])
        cat = sb("cat", [P, HI, 2 * H])
        mult = sb("mult", [P, HI])
        logm = sb("logm", [P, HI])
        dinv = sb("dinv", [P, HI])
        t1 = sb("t1", [P, HI, H])
        t2 = sb("t2", [P, HI, H])
        n1 = sb("n1", [P, HI])
        n2 = sb("n2", [P, HI])
        n3 = sb("n3", [P, HI])
        n4 = sb("n4", [P, HI])
        lasti = sb("lasti", [P, HI], I32)
        crow = sb("crow", [P, 1], I32)
        crf = sb("crf", [P, 2])
        idxR = sb("idxR", [P, COLS + RINGC, SLOTS + 1], I32)
        keep = sb("keep", [P, COLS])
        drop = sb("drop", [P, COLS])
        maskneg = sb("maskneg", [P, P])
        maskQP = sb("maskQP", [P, P])
        maskPQ = sb("maskPQ", [P, P])
        stg = sb("stg", [P, RINGC, SLOTS + 1], I32)
        hist = sb("hist", [P, RINGC, WS])
        cin = sb("cin", [P, WS])
        mrow = sb("mrow", [P, P])
        mtr = sb("mtr", [P, P])
        c1 = sb("c1", [P, 1])
        c2 = sb("c2", [P, 1])

        zero = sb("zero", [P, NTC // 2])
        plo = zero[:, :].bitcast(BF16)

        sort = ExitStack()
        sbs = sbx(sort)
        keys2 = sbs("keys2", [P, 2 * KE], I32)
        key = [keys2[:, k * KE:(k + 1) * KE] for k in range(2)]
        klo = [sbs(f"klo{k}", [P, KE + GRP], BF16) for k in range(2)]
        khi = [sbs(f"khi{k}", [P, KE + GRP], BF16) for k in range(2)]
        keyt = sbs("keyt", [P, KE], I32)
        pair = sbs("pair", [P, KE], I32)
        rowi = [sbs(f"rowi{k}", [P, KE], I32) for k in range(2)]
        cw = sbs("cw", [P, KE])
        ohl = sbs("ohl", [P, 2, GRP, P], BF16)
        ohh2 = [sbs(f"ohh{b}", [P, 2, GRP, HI], BF16) for b in range(2)]
        ohh = ohh2[0]
        ohtb = [sbs("ohtb0", [P, 2, GRP, P], BF16)[:, :, :, :],
                keyt[:, 0:GRP * P].bitcast(BF16).rearrange("p (k j e) -> p k j e", k=2, j=GRP)]
        oht16 = [sbs("oht16", [P, 2, GRP, P], F16)[:, :, :, :],
                 keys2[:, 0:GRP * P].bitcast(F16).rearrange("p (k j e) -> p k j e", k=2, j=GRP)]
        runhi = sbs("runhi", [P, 2, GRP, HI], F16)
        runlo = sbs("runlo", [P, 2, GRP, HI], BF16)
        eqm = sbs("eqm", [P, 2, GRP, P], BF16)
        run = t1[:, :, :].rearrange("p h c -> p (h c)")[:, 0:2 * (GRP + 1) * HI].rearrange(
            "p (k j c) -> p k j c", k=2, c=HI)
        gsel = t2[:, :, :].rearrange("p h c -> p (h c)")[:, 0:2 * GRP * HI].rearrange("p (k j c) -> p k j c", k=2, c=HI)
        qi = sbs("qi", [P, 2, GRP], I32)
        posf = sbs("posf", [P, 2, GRP])
        rec = sbs("rec", [P, RECR, GRP, REC])
        aT = sbs("aT", [RBF, 4 * P])
        hid = sbs("hid", [H + 1, 4 * P])
        sort_i = sbs("sort_i", [P, HI], I32)
        zi = sbs("zi", [P, HI], I32)
        nrow = sbs("nrow", [P, HI, 2], BF16)
        eb = sbs("eb", [P, HI, G])
        ebT = sbs("ebT", [G, 3 * P])
        rowbi = sbs("rowbi", [P, HI], I32)
        lastt = sbs("lastt", [P, HI], I32)
        firstt = sbs("firstt", [P, HI], I32)
        destv = sbs("destv", [P, HI], I32)
        markt = sbs("markt", [P, COLS])
        cum = sbs("cum", [P, COLS])
        zrow = sbs("zrow", [P, COLS])
        rowb = sbs("rowb", [P, HI])
        nodef = sbs("nodef", [P, COLS])
        rowt = [sbs(f"rowt{k}", [P, HI]) for k in range(4)]
        t0 = cat[:, :, 0:W0]
        rcp = cat[:, :, :].rearrange("p h c -> p (h c)").bitcast(BF16)[:, 0:HI * P].rearrange("p (h c) -> p h c", c=P)
        nfl = sbs("nfl", [P, 2, P])
        pst = [sbs(f"pst{k}", [P, RECR, GRP], I32) for k in range(2)]
        srcst = sbs("srcst", [P, RECR, GRP], I32)
        sort.close()
        lay = ExitStack()
        sbl = sbx(lay)
        qkm = sbl("qkm", [P, HI, 3 * H])
        kt = sbl("kt", [P, HI, WK])
        sA, sC = (qkm[:, :, :].rearrange("p h c -> p (h c)")[:, k * HI * WS:(k + 1) * HI * WS].rearrange("p (h c) -> p h c", c=WS)
                  for k in range(2))
        Gk = sbl("Gk", [P, RINGC, SLOTS, WK])
        Gq = sbl("Gq", [P, RINGC, H])
        att = sbl("att", [P, RINGC, SLOTS, RBF])
        recL = kt[:, :, :].rearrange("p h c -> p (h c)")[:, 0:RINGC * SLOTS * REC].rearrange(
            "p (r s c) -> p r s c", r=RINGC, s=SLOTS)
        pairt = qkm[:, :, :].rearrange("p h c -> p (h c)").bitcast(I32)[:, 0:NTC]
        phi = sbl("phi", [P, NTC], BF16)
        tkeep = sbl("tkeep", [P, NTC])
        tslot = sbl("tslot", [TPI, NTC // TPI], I32)
        tnone = sbl("tnone", [TPI, NTC // TPI], I32)
        oht = sbl("oht", [P, 2, 5, P], BF16)
        acc = sbl("acc", [P, 10, P])
        prod = sbl("prod", [P, SLOTS, H + RBF])
        prod2 = sbl("prod2", [P, SLOTS, H])
        sc = sbl("sc", [P, 2, 2, SLOTS])
        scal = sbl("scal", [P, 2, 8])
        ar = sbl("ar", [P, 2, W1])
        hT = sbl("hT", [2 * H, 2, 3 * P])
        lay.close()
        walk = ExitStack()
        sbw = sbx(walk)
        adjr = sbw("adjr", [P, ADJR, NPH])
        blk = sbw("blk", [P, ADJR, H])
        sums = sbw("sums", [H, NP])
        walk.close()

        wide = [ctx.enter_context(nc.psum_tensor(f"wide{i}", [P, 1024], F32)) for i in range(2)]
        bank = [ctx.enter_context(nc.psum_tensor(f"bank{i}", [P, 512], F32)) for i in range(4)]


        class s:
            adj_in = [sem(f"adj_in{k}") for k in range(ADJR)]
            adj_used = sem("adj_used")
            att_in = [sem(f"att_in{k}") for k in range(RINGC)]
            att_out = [sem(f"att_out{k}") for k in range(RINGC)]
            blk_ready = sem("blk_ready")
            carryA_mm = sem("carryA_mm")
            carryA_ready = sem("carryA_ready")
            carry_mm = sem("carry_mm")
            carry_ready = sem("carry_ready")
            cat_ready = sem("cat_ready")
            cexp_ready = sem("cexp_ready")
            cleared = sem("cleared")
            cm_ready = sem("cm_ready")
            cmax_ready = sem("cmax_ready")
            cnt_done = sem("cnt_done")
            cnt_mm = sem("cnt_mm")
            cnt_oh = sem("cnt_oh")
            cnt_out = [sem(f"cnt_out{k}") for k in range(RINGC)]
            cnt_ready = sem("cnt_ready")
            col_done = sem("col_done")
            col_g = [sem(f"col_g{k}") for k in range(RINGC)]
            colstg = sem("colstg")
            const_ready = sem("const_ready")
            cos_ready = sem("cos_ready")
            cr_in = sem("cr_in")
            cr_put = sem("cr_put")
            cwT_ready = sem("cwT_ready")
            cw_ready = sem("cw_ready")
            deg_ready = sem("deg_ready")
            dist_ready = sem("dist_ready")
            dve_step = sem("dve_step")
            e_T = sem("e_T")
            e_Tc = sem("e_Tc")
            e_done = sem("e_done")
            e_mm = sem("e_mm")
            emb_g = sem("emb_g")
            ends_ready = sem("ends_ready")
            exp_ready = sem("exp_ready")
            g_ready = sem("g_ready")
            go = sem("go")
            h_all = sem("h_all")
            h_mm = sem("h_mm")
            h_oh = [sem(f"h_oh{k}") for k in range(2)]
            h_ready = sem("h_ready")
            idx_out = [sem(f"idx_out{k}") for k in range(RECR)]
            iota = sem("iota")
            k_ready = sem("k_ready")
            keep_ld = sem("keep_ld")
            keys = sem("keys")
            l0_done = sem("l0_done")
            l0_g = [sem(f"l0_g{k}") for k in range(RINGC)]
            l0_in = [sem(f"l0_in{k}") for k in range(RINGC)]
            l0_stg = sem("l0_stg")
            logm_ready = sem("logm_ready")
            m_T = sem("m_T")
            m_aT = sem("m_aT")
            m_f1 = sem("m_f1")
            m_f2 = sem("m_f2")
            m_hid = sem("m_hid")
            mark_ld = sem("mark_ld")
            marked = sem("marked")
            max_ready = sem("max_ready")
            mult_ready = sem("mult_ready")
            nexp_ready = sem("nexp_ready")
            nmax_ready = sem("nmax_ready")
            nodes = sem("nodes")
            null = sem("null")
            p_T = sem("p_T")
            p_Tc = sem("p_Tc")
            p_done = sem("p_done")
            p_mm = sem("p_mm")
            pair_ld = sem("pair_ld")
            par = sem("par")
            pre_mm = sem("pre_mm")
            prop_T = sem("prop_T")
            prop_cp = sem("prop_cp")
            prop_mm = sem("prop_mm")
            q_ready = sem("q_ready")
            rec_fill = sem("rec_fill")
            rec_gate = sem("rec_gate")
            rec_in = [sem(f"rec_in{k}") for k in range(RECR)]
            rec_out = [sem(f"rec_out{k}") for k in range(RECR)]
            result = sem("result")
            rk_T = sem("rk_T")
            rk_cnt = sem("rk_cnt")
            rk_cp = sem("rk_cp")
            rk_eq = sem("rk_eq")
            rk_eqm = sem("rk_eqm")
            rk_g = sem("rk_g")
            rk_oh = sem("rk_oh")
            rk_sel = sem("rk_sel")
            rows_ready = sem("rows_ready")
            run_ready = sem("run_ready")
            scan_ready = sem("scan_ready")
            slot_ld = sem("slot_ld")
            slots_ready = sem("slots_ready")
            sqdeg_ready = sem("sqdeg_ready")
            stA_g = sem("stA_g")
            stA_out = sem("stA_out")
            st_g = sem("st_g")
            st_out = sem("st_out")
            std_ready = sem("std_ready")
            stored = sem("stored")
            t0_ready = sem("t0_ready")
            tab0_w = sem("tab0_w")
            tab_w = sem("tab_w")
            tiles_ready = sem("tiles_ready")
            tmarked = sem("tmarked")
            u_T = sem("u_T")
            u_Tc = sem("u_Tc")
            u_done = sem("u_done")
            u_mm = sem("u_mm")
            unpacked = sem("unpacked")
            var_ready = sem("var_ready")
            x_ready = sem("x_ready")
            zero_set = sem("zero_set")
            zeroed = sem("zeroed")

        block = ctx.enter_context(nc.Block())
        Gk2 = Gk[:, :, :, :].rearrange("p c s w -> p c (s w)")
        G0 = [Gk2[:, c, 0:SLOTS * W0].rearrange("p (s w) -> p s w", w=W0) for c in range(RINGC)]
        recLi = recL.bitcast(I32)
        reci = rec[:, :, :, :].bitcast(I32)
        hist2 = hist[:, :, :].rearrange("p c w -> p (c w)")
        h0 = hist2[:, 0:RINGC * W1].rearrange("p (c w) -> p c w", w=W1)
        sA2, sC2 = sA.rearrange("p h w -> p (h w)"), sC.rearrange("p h w -> p (h w)")
        sA0, sC0 = (t[:, 0:HI * W1].rearrange("p (h w) -> p h w", w=W1) for t in (sA2, sC2))
        rec_v = recS.rearrange("(p w s) c -> p w (s c)", p=P, s=SLOTS)
        st0_v, stA_v = (t.rearrange("(p w) c -> p w c", p=P) for t in (st0, stA))
        tabT = [wide[1][:, 512 * k:512 * (k + 1)].bitcast(BF16) for k in range(2)]
        adj_v = adj[0:HI * P * HI].rearrange("(i p j) c -> i p (j c)", i=HI, p=P)
        halves = [wide[k][:, 512 * q:512 * (q + 1)] for k in range(2) for q in range(2)]
        prop = halves + bank[0:3]
        propT = [bank[3]] + halves
        ea = io["edge_attr_40"]
        ea_v = ea[0:(P - 1) * KE].rearrange("(p t) c -> p t c", t=KE)
        ea_l = ea[E - KE:E].unsqueeze(0)
        OH = HI * GRP

        def acc_slot(c, j):
            return 5 * (c % 2) + j - TOFF[c]

        def by_node(ap):
            return ap[1:NP + 1].rearrange("(h p) c -> p h c", p=P)

        def load_edges(eng, tile, src, signal):
            eng.dma_start(tile[0:P - 1, :], src[0:(P - 1) * KE].rearrange("(p t) -> p t", t=KE)).then_inc(signal, 16)
            eng.dma_start(tile[P - 1:P, :], src[E - KE:E].unsqueeze(0)).then_inc(signal, 16)

        def load_nodes(eng, tile, src, signal):
            spec = "(h p) c -> p h c" if len(src.shape) == 2 else "(h p) -> p h"
            eng.dma_start(tile[:, 0:HI - 1], src[0:(HI - 1) * P].rearrange(spec, p=P),
                          allow_slow_non_contiguous=len(src.shape) == 1).then_inc(signal, 16)
            eng.dma_start(tile[0:LASTN, HI - 1:HI], src[(HI - 1) * P:N].unsqueeze(1)).then_inc(signal, 16)

        @block.sync
        def _(sp):
            for x in (s.st_out, s.stA_out, *s.cnt_out):
                sp.sem_inc(x, 1)
            sp.wait_ge(s.cleared, 1)
            for k, name in enumerate(("src", "dst")):
                load_edges(sp, rowi[k], io[name], s.keys)
            load_edges(sp, cw, io["edge_weight"], s.keys)
            load_nodes(sp, x0, io["x"], s.nodes)
            load_nodes(sp, mult, io["node_vec"], s.nodes)
            load_nodes(sp, zi, io["node_type_119"], s.nodes)
            sp.dma_start(f1w[:, :], io["L0_gnn_F1W"]).then_inc(s.par, 16)
            sp.dma_start(f1b[:, :], io["L0_gnn_F1b"].unsqueeze(1)).then_inc(s.par, 16)
            sp.dma_start(f2w[0:H, :], io["L0_gnn_F2W"]).then_inc(s.par, 16)
            sp.dma_start(f2w[H:H + 1, :], io["L0_gnn_F2b"].unsqueeze(0)).then_inc(s.par, 16)
            sp.dma_start(adapt[:, :], io["L0_gnn_adapt"]).then_inc(s.par, 16)
            for j, n in enumerate(("Wq", "Wk", "Wm")):
                sp.dma_start(wqkm[:, :, j * H:(j + 1) * H], io["L0_gnn_" + n].rearrange("l a b -> a l b")).then_inc(s.par, 16)
            sp.dma_start(wu[:, :, :], io["L0_gnn_Wu"].rearrange("l a b -> a l b")).then_inc(s.par, 16)
            for n, t in lnp.items():
                sp.dma_start(t[:, :, :], io["L0_gnn_" + n].unsqueeze(0).to_broadcast([P, LAYERS, H])).then_inc(s.par, 16)
            for n, t in lnn.items():
                sp.dma_start(t[:, :, :], io["L0_gnn_" + n].unsqueeze(0).unsqueeze(0).to_broadcast([P, 1, H])).then_inc(s.par, 16)
            for t in (tab0, tabE, tabQ):
                sp.dma_start(t[0:1, :], zero[0:1, 0:t.shape[1]]).then_inc(s.null, 16)
            sp.dma_start(tabK[0:1, :], nullK[:, :]).then_inc(s.null, 16)
            sp.dma_start(by_node(cr0), bc(zero[:, 0:W1], 1, HI)).then_inc(s.null, 16)
            sp.dma_start(by_node(crA), bc(nullA[:, :], 1, HI)).then_inc(s.null, 16)
            sp.wait_ge(s.marked, 16 * HI)
            sp.dma_start(markt[:, :], mark.rearrange("(p w) c -> p (w c)", p=P)).then_inc(s.mark_ld, 16)
            def load_rec(b, g):
                cols = bass.ds(GRP * g, GRP)
                for lo, hi in ((0, 112), (112, P - 1)):
                    sp.dma_start(rec[lo:hi, b, :, 0:RBF], ea_v[lo:hi, cols, :]).then_inc(s.rec_in[b], 16)
                sp.dma_start(rec[P - 1:P, b, :, 0:RBF], ea_l[:, cols, :]).then_inc(s.rec_in[b], 16)

            for b in range(RECR):
                load_rec(b, b)
            with sp.Fori(0, NG // RECR - 1) as i:
                for b in range(RECR):
                    sp.wait_ge(s.rec_out[b], 16 * GRP * (i + 1))
                    sp.wait_ge(s.idx_out[b], 16 * GRP * (i + 1))
                    load_rec(b, RECR * (i + 1) + b)
            sp.wait_ge(s.t0_ready, 1)
            sp.dma_start(by_node(tab0), t0[:, :, :]).then_inc(s.tab0_w, 16)
            sp.wait_ge(s.emb_g, 16 * HI)
            sp.dma_start(by_node(tabE), eb[:, :, :]).then_inc(s.tab0_w, 16)
            sp.wait_ge(s.tab0_w, 32)
            for b in range(RECR):
                sp.wait_ge(s.rec_out[b], 16 * GRP * (NG // RECR))
                sp.wait_ge(s.idx_out[b], 16 * GRP * (NG // RECR))
            sp.dma_start(pairt, pairs.rearrange("(p t) c -> p (t c)", p=P)).then_inc(s.pair_ld, 16)
            sp.wait_ge(s.tmarked, 16 * 2 * HI)
            sp.dma_start(tslot[:, :], tdest.rearrange("(i q) a -> q (i a)", q=TPI), allow_slow_non_contiguous=True).then_inc(s.slot_ld, 16)
            sp.wait_ge(s.unpacked, 1)
            sp.dma_start(tkeep[:, :], tfirst.rearrange("t a -> a t").to_broadcast([P, NTC])).then_inc(s.keep_ld, 16)
            for c in range(RINGC):
                sp.dma_start(recL[:, c, :, :].rearrange("p s c -> p (s c)"), rec_v[:, c, :]).then_inc(s.l0_in[c], 16)
            with sp.Fori(0, NIT - 1) as i:
                for c in range(RINGC):
                    sp.wait_ge(s.l0_done, RINGC * i + c + 1)
                    sp.wait_ge(s.att_out[c], 16 * (i + 1))
                    sp.dma_start(recL[:, c, :, :].rearrange("p s c -> p (s c)"),
                                 rec_v[:, bass.ds(RINGC * (i + 1) + c, 1), :].rearrange("p w c -> p (w c)")).then_inc(s.l0_in[c], 16)
                sp.dma_start(st0_v[:, bass.ds(RINGC * i, RINGC), :], h0).then_inc(s.st_out, 16)
            sp.wait_ge(s.l0_done, COLS)
            sp.dma_start(st0_v[:, COLS - RINGC:COLS, :], h0).then_inc(s.st_out, 16)
            sp.wait_ge(s.carry_ready, 1)
            sp.wait_ge(s.cr_put, 16)
            sp.dma_start(sC0, by_node(cr0)).then_inc(s.cr_in, 16)
            for c in range(RINGC):
                sp.wait_ge(s.att_out[c], 16 * NIT)
            sp.wait_ge(s.slots_ready, 1)
            with sp.Fori(0, LAYERS) as L:
                sp.wait_ge(s.q_ready, L + 1)
                sp.dma_start(by_node(tabQ), qkm[:, :, 0:H]).then_inc(s.tab_w, 16)
                sp.wait_ge(s.k_ready, L + 1)
                sp.dma_start(by_node(tabK), kt[:, :, :]).then_inc(s.tab_w, 16)
                for c in range(RINGC):
                    sp.dma_start(att[:, c, :, :].rearrange("p s c -> p (s c)"), attrE[:, c, :]).then_inc(s.att_in[c], 16)

                def counts_out(it, c):
                    for j in range(TOFF[c], TOFF[c + 1]):
                        slot = sp.value_load(tslot[j:j + 1, bass.ds(it, 1)], min_val=0, max_val=NP * HI + TPI)
                        if j == TOFF[c]:
                            sp.wait_ge(s.cnt_done, 1 + RINGC * it + c + 1)
                        sp.dma_start(adj[bass.ds(slot, P, HI), :], acc[:, acc_slot(c, j), :]).then_inc(s.cnt_out[c], 16)

                with sp.Fori(0, NIT - 1) as i:
                    for c in range(RINGC):
                        sp.wait_ge(s.col_done, COLS * L + RINGC * i + c + 1)
                        sp.dma_start(att[:, c, :, :].rearrange("p s c -> p (s c)"),
                                     attrE[:, bass.ds(RINGC * (i + 1) + c, 1), :].rearrange("p w c -> p (w c)")).then_inc(s.att_in[c], 16)
                        counts_out(NIT * L + i, c)
                    sp.dma_start(stA_v[:, bass.ds(RINGC * i, RINGC), :], hist[:, :, :]).then_inc(s.stA_out, 16)
                for c in range(RINGC):
                    counts_out(NIT * L + NIT - 1, c)
                sp.wait_ge(s.col_done, COLS * (L + 1))
                sp.dma_start(stA_v[:, COLS - RINGC:COLS, :], hist[:, :, :]).then_inc(s.stA_out, 16)
                sp.wait_ge(s.carryA_ready, L + 1)
                sp.wait_ge(s.tab_w, 32 * L + 32)
                sp.wait_ge(s.cr_put, 16 * L + 32)
                sp.sem_inc(s.go, 1)
                sp.dma_start(sC, by_node(crA)).then_inc(s.cr_in, 16)
            for c in range(RINGC):
                sp.wait_ge(s.cnt_out[c], 1 + 16 * (TOFF[c + 1] - TOFF[c]) * LAYERS * NIT)
            sp.wait_ge(s.x_ready, 1)
            with sp.Fori(0, STEPS) as L:
                for half in range(2):
                    with sp.Fori(0, HI // ADJR) as i:
                        for k in range(ADJR):
                            sp.wait_ge(s.adj_used, (2 * HI) * L + HI * half + ADJR * i + k + 1)
                            sp.dma_start(adjr[:, k, :], adj_v[bass.ds(ADJR * i + k, 1), :, half * NPH:(half + 1) * NPH].rearrange("i p c -> p (i c)")
                                         ).then_inc(s.adj_in[k], 16)
            sp.wait_ge(s.result, 1)
            sp.dma_start(out[0:(HI - 1) * P].rearrange("(h p) c -> p h c", p=P), h[:, 0:HI - 1, :]).then_inc(s.stored, 16)
            sp.dma_start(out[(HI - 1) * P:N].unsqueeze(1), h[0:LASTN, HI - 1:HI, :]).then_inc(s.stored, 16)
            sp.wait_ge(s.stored, 32)

        @block.gpsimd
        def _(pool):
            nc.gpsimd.iota(iotai[:, :], pattern=[[1, P]], base=0, channel_multiplier=0).then_inc(s.iota, 1)
            nc.gpsimd.iota(parti[:, :], pattern=[[0, 1]], base=0, channel_multiplier=1).then_inc(s.iota, 1)
            pool.wait_ge(s.nodes, 96)
            for hi in range(HI):
                pool.indirect_dma_start(eb[:, hi, :], None, io["L0_gnn_emb"][:, :],
                                        bass.IndirectOffsetOnAxis(zi[:, hi:hi + 1], 0)).then_inc(s.emb_g, 16)
            pool.wait_ge(s.rows_ready, 1)
            pool.wait_ge(s.zeroed, 16 * 5)
            for hi in range(HI):
                pool.indirect_dma_start(mark[:, :], bass.IndirectOffsetOnAxis(rowbi[:, hi:hi + 1], 0),
                                        ones[:, 0:1], None).then_inc(s.marked, 16)
            pool.wait_ge(s.tiles_ready, 1)
            for hi in range(HI):
                pool.indirect_dma_start(tfirst[:, :], bass.IndirectOffsetOnAxis(firstt[0:HI, hi:hi + 1], 0),
                                        ones[0:HI, 0:1], None).then_inc(s.tmarked, 16)
                pool.indirect_dma_start(tdest[:, :], bass.IndirectOffsetOnAxis(lastt[0:HI, hi:hi + 1], 0),
                                        destv[0:HI, hi:hi + 1], None).then_inc(s.tmarked, 16)
            with pool.Fori(0, NG // RECR) as i:
                for b in range(RECR):
                    pool.wait_ge(s.rec_gate, 1 + 2 * RECR * i + 2 * b + 2)
                    pool.wait_ge(s.rec_fill, RECR * i + b + 1)
                    pool.sem_inc(s.go, 1)
                    for j in range(GRP):
                        pool.indirect_dma_start(recS[:, :], bass.IndirectOffsetOnAxis(pst[0][:, b, j:j + 1], 0),
                                                rec[:, b, j, :], None).then_inc(s.rec_out[b], 16)
                        pool.indirect_dma_start(pairs[:, :], bass.IndirectOffsetOnAxis(pst[1][:, b, j:j + 1], 0),
                                                srcst[:, b, j:j + 1], None).then_inc(s.idx_out[b], 16)
            pool.wait_ge(s.tab0_w, 32)
            pool.wait_ge(s.null, 96)
            with pool.Fori(0, NIT) as i:
                for c in range(RINGC):
                    pool.wait_ge(s.l0_in[c], 16 * (i + 1))
                    pool.wait_ge(s.l0_stg, RINGC * i + c + 1)
                    pool.sem_inc(s.go, 1)
                    for j in range(SLOTS):
                        pool.indirect_dma_start(G0[c][:, j, :], None, tab0[:, :],
                                                bass.IndirectOffsetOnAxis(recLi[:, c, j, REC - 1:REC], 0)).then_inc(s.l0_g[c], 16)
                    pool.indirect_dma_start(Gq[:, c, 0:G], None, tabE[:, :],
                                            bass.IndirectOffsetOnAxis(stg[:, c, SLOTS:SLOTS + 1], 0)).then_inc(s.l0_g[c], 16)
            pool.wait_ge(s.carry_ready, 1)
            pool.indirect_dma_start(cr0[:, :], bass.IndirectOffsetOnAxis(crow[:, 0:1], 0), cin[:, 0:W1], None).then_inc(s.cr_put, 16)
            pool.wait_ge(s.st_out, 1 + 16 * NIT)
            for hi in range(HI):
                pool.indirect_dma_start(sA0[:, hi, :], None, st0[:, :],
                                        bass.IndirectOffsetOnAxis(lasti[:, hi:hi + 1], 0)).then_inc(s.st_g, 16)
            with pool.Fori(0, LAYERS) as L:
                pool.wait_ge(s.tab_w, 32 * L + 32)
                pool.sem_inc(s.go, 1)
                with pool.Fori(0, NIT) as i:
                    for c in range(RINGC):
                        pool.wait_ge(s.colstg, (COLS + RINGC) * L + RINGC * i + c + 1)
                        pool.sem_inc(s.go, 1)
                        pool.indirect_dma_start(Gq[:, c, :], None, tabQ[:, :],
                                                bass.IndirectOffsetOnAxis(stg[:, c, SLOTS:SLOTS + 1], 0)).then_inc(s.col_g[c], 16)
                        for j in range(SLOTS):
                            pool.indirect_dma_start(Gk[:, c, j, :], None, tabK[:, :],
                                                    bass.IndirectOffsetOnAxis(stg[:, c, j:j + 1], 0)).then_inc(s.col_g[c], 16)
                pool.wait_ge(s.carryA_ready, L + 1)
                pool.sem_inc(s.go, 1)
                pool.indirect_dma_start(crA[:, :], bass.IndirectOffsetOnAxis(crow[:, 0:1], 0), cin[:, :], None).then_inc(s.cr_put, 16)
                pool.wait_ge(s.stA_out, 1 + (16 * NIT) * L + 16 * NIT)
                pool.sem_inc(s.go, 1)
                for hi in range(HI):
                    pool.indirect_dma_start(sA[:, hi, :], None, stA[:, :],
                                            bass.IndirectOffsetOnAxis(lasti[:, hi:hi + 1], 0)).then_inc(s.stA_g, 16)

        @block.scalar
        def _(act):
            for x in (s.rec_gate, s.prop_cp):
                act.sem_inc(x, 1)
            act.wait_ge(s.zero_set, 1)
            wr = COLS * SLOTS * REC // ZW
            act.dma_start(pairs.rearrange("(p a t) c -> p a (t c)", p=P, a=2), bc(zero[:, :].bitcast(I32), 1, 2)).then_inc(s.zeroed, 16)
            act.dma_start(mark.rearrange("(p a) c -> p (a c)", p=P), zero[:, 0:COLS]).then_inc(s.zeroed, 16)
            act.dma_start(tfirst.rearrange("(p t) a -> p (t a)", p=2), zero[0:2, :]).then_inc(s.zeroed, 16)
            act.dma_start(tdest.rearrange("(p t) a -> p (t a)", p=2), zero[0:2, :].bitcast(I32)).then_inc(s.zeroed, 16)
            act.wait_ge(s.keys, 96)
            act.dma_start(recS.rearrange("(p r) c -> p (r c)", p=P).rearrange("p (a z) -> p a z", z=ZW),
                          bc(zero[:, 0:ZW], 1, wr)).then_inc(s.zeroed, 16)
            act.wait_ge(s.dist_ready, 1)
            done(act, nc.scalar.activation(cw[:, :], cw[:, :], ACT.Sin, bias=halfpi[:, 0:1], scale=-float(np.pi) / 6.0), s.cos_ready, 1)
            act.wait_ge(s.mult_ready, 1)
            done(act, nc.scalar.activation(logm[:, :], logm[:, :], ACT.Ln), s.logm_ready, 1)
            act.wait_ge(s.deg_ready, 1)
            done(act, nc.scalar.activation(n4[:, :], n3[:, :], ACT.Sqrt), s.sqdeg_ready, 1)
            def copies(b, g, k):
                n = (P, HI)[k]
                act.wait_ge(s.rk_T, 2 * g + k + 1)
                nc.scalar.copy(ohtb[b][0:n, k, :, :].rearrange("p j e -> p (j e)"), tabT[k][0:n, 0:GRP * P]).then_inc(s.rk_cp, 1)
                nc.scalar.mul(oht16[b][0:n, k, :, :].rearrange("p j e -> p (j e)"), tabT[k][0:n, 0:GRP * P], PART).then_inc(s.rk_cp, 1)

            with act.Fori(0, NG // RECR) as i:
                for b in range(RECR):
                    g, o = RECR * i + b, b % 2

                    def features(m):
                        act.wait_ge(s.m_T, 2 * g + m + 1)
                        nc.scalar.copy(aT[:, :], bank[0][0:RBF, :]).then_inc(s.m_aT, 1)

                    def hidden(m):
                        act.wait_ge(s.m_f1, 2 * g + m + 1)
                        nc.scalar.activation(hid[0:H, :], bank[1][0:H, :], ACT.Silu, bias=f1b[:, 0:1]).then_inc(s.m_hid, 1)

                    def gate(m):
                        act.wait_ge(s.m_f2, 2 * g + m + 1)
                        nc.scalar.copy(rec[:, b, 4 * m:4 * m + 4, RBF:RBF + H], bank[0][:, 0:4 * H].rearrange("p (j c) -> p j c", c=H)).then_inc(s.rec_gate, 1)

                    act.wait_ge(s.rk_g, 1 + 2 * g)
                    copies(o, g, 0)
                    features(0)
                    copies(o, g, 1)
                    hidden(0)
                    gate(0)
                    features(1)
                    hidden(1)
                    gate(1)
            for g, (lo, hi) in enumerate(NT):
                act.wait_ge(s.e_T, g + 1)
                nc.scalar.copy(ebT[:, 0:(hi - lo) * P], bank[1][0:G, 0:(hi - lo) * P]).then_inc(s.e_Tc, 1)
                act.wait_ge(s.e_mm, g + 1)
                nc.scalar.copy(t0[:, lo:hi, H:H + G], bank[2][:, 0:(hi - lo) * G].rearrange("p (j c) -> p j c", c=G)).then_inc(s.e_done, 1)
            with act.Fori(0, NIT) as i:
                for c in range(RINGC):
                    act.wait_ge(s.l0_in[c], 16 * (i + 1))
                    act.dma_start(attrE[:, bass.ds(RINGC * i + c, 1), :].rearrange("p w (s c) -> p (w s) c", c=RBF),
                                  recL[:, c, :, 0:RBF]).then_inc(s.att_out[c], 16)

            def root(n):
                act.wait_ge(s.var_ready, n)
                done(act, nc.scalar.activation(n2[:, :], n1[:, :], ACT.Sqrt, bias=epsc[:, 0:1], scale=1.0 / H), s.std_ready, n)
            root(1)
            with act.Fori(0, LAYERS) as L:
                for g, (lo, hi) in enumerate(NT):
                    act.wait_ge(s.p_T, NNT * L + g + 1)
                    if g >= 2:
                        act.wait_ge(s.p_mm, NNT * L + g - 1)
                    nc.scalar.copy(hT[0:H, g % 2, 0:(hi - lo) * P], bank[g % 2][0:H, 0:(hi - lo) * P]).then_inc(s.p_Tc, 1)
                root(3 * L + 2)
                root(3 * L + 3)
                with act.Fori(0, NIT) as i:
                    for c in range(RINGC):
                        w = COLS * L + RINGC * i + c
                        act.wait_ge(s.max_ready, w + 1)
                        q = c % 2
                        nc.scalar.activation(sc[:, q, 1, :], sc[:, q, 0, :], ACT.Exp, bias=scal[:, q, 2:3], accum_out=ar[:, q, 0:1]).then_inc(s.exp_ready, 1)
                        nc.scalar.activation(scal[:, q, 3:4], scal[:, q, 1:2], ACT.Exp, bias=scal[:, q, 2:3]).then_inc(s.exp_ready, 1)
                act.wait_ge(s.cmax_ready, L + 1)
                done(act, nc.scalar.activation(mtr[:, :], mrow[:, :], ACT.Exp, bias=c1[:, 0:1]), s.cexp_ready, L + 1)
                act.wait_ge(s.nmax_ready, L + 1)
                done(act, nc.scalar.activation(n3[:, :], n3[:, :], ACT.Exp), s.nexp_ready, 2 * L + 1)
                done(act, nc.scalar.activation(n4[:, :], n4[:, :], ACT.Exp), s.nexp_ready, 2 * L + 2)
                for g, (lo, hi) in enumerate(NT):
                    act.wait_ge(s.u_T, NNT * L + g + 1)
                    if g >= 2:
                        act.wait_ge(s.u_mm, NNT * L + g - 1)
                    nc.scalar.copy(hT[:, g % 2, 0:(hi - lo) * P], bank[g % 2][0:2 * H, 0:(hi - lo) * P]).then_inc(s.u_Tc, 1)
                root(3 * L + 4)
            root(3 * LAYERS + 2)
            with act.Fori(0, STEPS) as L:
                act.wait_ge(s.g_ready, L + 1)
                for half in range(2):
                    with act.Fori(0, HI // ADJR) as i:
                        for k in range(ADJR):
                            act.wait_ge(s.adj_used, (2 * HI) * L + HI * half + ADJR * i + k + 1)
                            nc.scalar.copy(blk[:, k, :], t1[:, bass.ds(ADJR * i + k, 1), :].rearrange("p i c -> p (i c)")).then_inc(s.blk_ready, 1)
                    act.wait_ge(s.prop_mm, 2 * L + half + 1)
                    for q in range(len(prop)):
                        nc.scalar.copy(sums[:, half * NPH + q * PC:half * NPH + (q + 1) * PC], prop[q][0:H, 0:PC]).then_inc(s.prop_cp, 1)
            root(3 * LAYERS + 3)

        @block.tensor
        def _(pe):
            pe.wait_ge(s.const_ready, 1)
            pe.sem_inc(s.rk_g, 1)
            pe.sem_inc(s.adj_used, ADJR)
            for k in range(3):
                nc.tensor.matmul(bank[k][:, 0:HI], zb[:, 0:P], zb[:, 0:HI], start=True, stop=False).then_inc(s.h_mm, 1)
            with pe.Fori(0, NG) as i:
                for k in range(2):
                    pe.wait_ge(s.h_oh[k], i + 1)
                    for j in range(GRP):
                        last = nc.tensor.matmul(bank[k][:, 0:HI], ohl[:, k, j, :], ohh[:, k, j, :], start=False, stop=False)
                    if k:
                        for j in range(GRP):
                            last = nc.tensor.matmul(bank[2][0:HI, 0:HI], ohh[:, 0, j, :], ohh[:, 1, j, :], start=False, stop=False)
                last.then_inc(s.h_mm, 3)
            for k in range(3):
                nc.tensor.matmul(bank[k][:, 0:HI], zb[:, 0:P], zb[:, 0:HI], start=False, stop=True).then_inc(s.h_all, 1)
            pe.wait_ge(s.cnt_ready, 1)
            nc.tensor.matmul(bank[3][:, 0:HI], triu[:, :], rowt[0][:, :], start=True, stop=True)
            nc.tensor.matmul(bank[3][:, 64:64 + HI], ones[:, :], rowt[0][:, :], start=True, stop=True).then_inc(s.pre_mm, 1)
            pe.wait_ge(s.cnt_ready, 2)
            nc.tensor.matmul(bank[0][0:HI, 0:HI], triu[0:HI, 0:HI], rowt[0][0:HI, :], start=True, stop=True)
            nc.tensor.matmul(bank[0][0:HI, 64:64 + HI], ones[0:HI, 0:HI], rowt[0][0:HI, :], start=True, stop=True).then_inc(s.pre_mm, 1)
            pe.wait_ge(s.scan_ready, 1)
            nc.tensor.matmul(bank[3][:, 0:1], triu[:, :], cum[:, COLS - 1:COLS], start=True, stop=True).then_inc(s.pre_mm, 1)
            pe.wait_ge(s.ends_ready, 1)
            nc.tensor.matmul(bank[3][:, 128:256], nfl[:, 0, :], ident[:, :], start=True, stop=True)
            nc.tensor.matmul(bank[3][:, 256:384], nfl[:, 1, :], ident[:, :], start=True, stop=True).then_inc(s.pre_mm, 1)
            pe.wait_ge(s.run_ready, 1)
            for hi in range(HI):
                last = nc.tensor.matmul(bank[1][:, 0:2], rcp[:, hi, :], nrow[:, hi, :], start=hi == 0, stop=hi == HI - 1)
            last.then_inc(s.pre_mm, 1)
            pe.wait_ge(s.par, PARS)
            n_lo = (P, HI)

            def left(b, k):
                return ohh2[b][:, 0, :, :] if k else ohl[:, b, :, :]

            def turn(b, g, k):
                pe.wait_ge(s.rk_oh, g + 1)
                pe.sem_inc(s.go, 1)
                for j in range(GRP):
                    last = nc.tensor.transpose(tabT[k][0:n_lo[k], j * P:(j + 1) * P], left(b, k)[:, j, :], identb[:, :])
                last.then_inc(s.rk_T, 1)

            for k in range(2):
                turn(0, 0, k)
            with pe.Fori(0, NG // RECR) as i:
                for b in range(RECR):
                    g, o = RECR * i + b, b % 2
                    right = [ohh2[o][:, 0, :, :], ohh2[o][:, 1, :, :]]

                    def features(m):
                        pe.wait_ge(s.rec_gate, 1 + 2 * g + m)
                        pe.wait_ge(s.rec_in[b], 48 * (i + 1))
                        pe.sem_inc(s.go, 1)
                        for j in range(4):
                            last = nc.tensor.transpose(bank[0][0:RBF, j * P:(j + 1) * P], rec[:, b, 4 * m + j, 0:RBF], ident[:, :])
                        last.then_inc(s.m_T, 1)

                    def hidden(m):
                        pe.wait_ge(s.m_aT, 2 * g + m + 1)
                        pe.sem_inc(s.go, 1)
                        nc.tensor.matmul(bank[1][0:H, :], f1w[:, :], aT[:, :], start=True, stop=True).then_inc(s.m_f1, 1)

                    def gate(m):
                        pe.wait_ge(s.m_hid, 2 * g + m + 1)
                        pe.sem_inc(s.go, 1)
                        for j in range(4):
                            last = nc.tensor.matmul(bank[0][:, j * H:(j + 1) * H], hid[:, j * P:(j + 1) * P], f2w[:, :], start=True, stop=True)
                        last.then_inc(s.m_f2, 1)

                    def same(k):
                        pe.wait_ge(s.rk_cp, 4 * g + 2 * k + 2)
                        if k:
                            pe.wait_ge(s.rk_eqm, 2 * g + 1)
                        pe.sem_inc(s.go, 1)
                        n = n_lo[k]
                        for j in range(GRP):
                            last = nc.tensor.matmul(wide[0][:, j * P:(j + 1) * P], ohtb[o][0:n, k, j, :], ohtb[o][0:n, k, j, :], start=True, stop=True)
                        last.then_inc(s.rk_eq, 1)

                    def ranks(k):
                        pe.wait_ge(s.rk_eqm, 2 * g + k + 1)
                        pe.sem_inc(s.go, 1)
                        n = n_lo[k]
                        for j in range(GRP):
                            at = bank[2 + k][:, j * HI:(j + 1) * HI]
                            nc.tensor.matmul(at, eqm[:, k, j, :], right[k][:, j, :], start=True, stop=False)
                            nc.tensor.matmul(at, oht16[o][0:n, k, j, :], runhi[0:n, k, j, :], start=False, stop=False)
                            last = nc.tensor.matmul(at, ohtb[o][0:n, k, j, :], runlo[0:n, k, j, :], start=False, stop=True)
                        last.then_inc(s.rk_g, 1)

                    pe.wait_ge(s.rk_sel, 1 + 2 * g)
                    pe.sem_inc(s.go, 1)
                    for k in range(2):
                        n = n_lo[k]
                        for j in range(GRP):
                            last = nc.tensor.matmul(bank[2 + k][0:n, j * HI:(j + 1) * HI], left(o, k)[:, j, :], right[k][:, j, :], start=True, stop=True)
                        last.then_inc(s.rk_cnt, 1)
                    features(0)
                    same(0)
                    hidden(0)
                    same(1)
                    gate(0)
                    ranks(0)
                    features(1)
                    ranks(1)
                    turn(1 - o, g + 1, 0)
                    turn(1 - o, g + 1, 1)
                    hidden(1)
                    gate(1)
            pe.wait_ge(s.rec_fill, NG)
            pe.wait_ge(s.emb_g, 16 * HI)
            for g, (lo, hi) in enumerate(NT):
                if g:
                    pe.wait_ge(s.e_Tc, g)
                for j in range(lo, hi):
                    last = nc.tensor.transpose(bank[1][0:G, (j - lo) * P:(j - lo + 1) * P], eb[:, j, :], ident[:, :])
                last.then_inc(s.e_T, 1)
                pe.wait_ge(s.e_Tc, g + 1)
                if g:
                    pe.wait_ge(s.e_done, g)
                for j in range(lo, hi):
                    last = nc.tensor.matmul(bank[2][:, (j - lo) * G:(j - lo + 1) * G], ebT[:, (j - lo) * P:(j - lo + 1) * P], adapt[:, :], start=True, stop=True)
                last.then_inc(s.e_mm, 1)
            pe.wait_ge(s.l0_done, COLS)
            nc.tensor.matmul(bank[0][:, 0:W1], maskQP[:, :], h0[:, RINGC - 1, :], start=True, stop=True).then_inc(s.carry_mm, 1)
            with pe.Fori(0, LAYERS) as L:
                pe.wait_ge(s.h_ready, L + 1)
                def turn_p(g):
                    lo, hi = NT[g]
                    for j in range(lo, hi):
                        last = nc.tensor.transpose(bank[g % 2][0:H, (j - lo) * P:(j - lo + 1) * P], h[:, j, :], ident[:, :])
                    last.then_inc(s.p_T, 1)

                pe.sem_inc(s.go, 1)
                turn_p(0)
                for g, (lo, hi) in enumerate(NT):
                    if g + 1 < NNT:
                        turn_p(g + 1)
                    pe.wait_ge(s.p_Tc, NNT * L + g + 1)
                    if g >= 2:
                        pe.wait_ge(s.p_done, NNT * L + g - 1)
                    pe.sem_inc(s.go, 1)
                    for j in range(lo, hi):
                        last = nc.tensor.matmul(bank[2 + g % 2][:, (j - lo) * 3 * H:(j - lo + 1) * 3 * H], hT[0:H, g % 2, (j - lo) * P:(j - lo + 1) * P],
                                                wqkm[:, bass.ds(L, 1), :].rearrange("p l c -> p (l c)"), start=True, stop=True)
                    last.then_inc(s.p_mm, 1)
                with pe.Fori(0, NIT) as i:
                    for c in range(RINGC):
                        pe.wait_ge(s.cnt_oh, (COLS * L) + RINGC * i + c + 1)
                        pe.sem_inc(s.go, 1)
                        for j in range(TOFF[c + 1] - TOFF[c]):
                            last = nc.tensor.matmul(wide[1][:, j * P:(j + 1) * P], oht[:, 0, j, :], oht[:, 1, j, :], start=True, stop=True)
                        last.then_inc(s.cnt_mm, 1)
                pe.wait_ge(s.cm_ready, L + 1)
                nc.tensor.matmul(wide[0][:, 0:P], mtr[:, :], ident[:, :], start=True, stop=True).then_inc(s.carryA_mm, 1)
                pe.wait_ge(s.cw_ready, L + 1)
                nc.tensor.transpose(wide[0][:, 512:512 + P], mtr[:, :], ident[:, :]).then_inc(s.carryA_mm, 1)
                pe.wait_ge(s.cwT_ready, L + 1)
                nc.tensor.matmul(wide[1][:, 0:W1], mrow[:, :], hist[:, RINGC - 1, 1:WS], start=True, stop=True).then_inc(s.carryA_mm, 1)
                pe.wait_ge(s.cat_ready, L + 1)
                def turn_u(g):
                    lo, hi = NT[g]
                    for j in range(lo, hi):
                        last = nc.tensor.transpose(bank[g % 2][0:2 * H, (j - lo) * P:(j - lo + 1) * P], cat[:, j, :], ident[:, :])
                    last.then_inc(s.u_T, 1)

                pe.sem_inc(s.go, 1)
                turn_u(0)
                for g, (lo, hi) in enumerate(NT):
                    if g + 1 < NNT:
                        turn_u(g + 1)
                    pe.wait_ge(s.u_Tc, NNT * L + g + 1)
                    if g >= 2:
                        pe.wait_ge(s.u_done, NNT * L + g - 1)
                    pe.sem_inc(s.go, 1)
                    for j in range(lo, hi):
                        last = nc.tensor.matmul(bank[2 + g % 2][:, (j - lo) * H:(j - lo + 1) * H], hT[:, g % 2, (j - lo) * P:(j - lo + 1) * P],
                                                wu[:, bass.ds(L, 1), :].rearrange("p l c -> p (l c)"), start=True, stop=True)
                    last.then_inc(s.u_mm, 1)
            with pe.Fori(0, STEPS) as L:
                pe.wait_ge(s.g_ready, L + 1)
                for half in range(2):
                    pe.wait_ge(s.prop_cp, 1 + (2 * len(prop)) * L + len(prop) * half)
                    pe.sem_inc(s.go, 1)
                    for q in range(len(prop)):
                        nc.tensor.matmul(prop[q][0:H, 0:PC], zb[:, 0:H], zb[:, 0:PC], start=True, stop=False)
                    with pe.Fori(0, HI // ADJR) as i:
                        for k in range(ADJR):
                            pe.wait_ge(s.adj_in[k], (32 * (HI // ADJR)) * L + 16 * (HI // ADJR) * half + 16 * i + 16)
                            pe.wait_ge(s.blk_ready, (2 * HI) * L + HI * half + ADJR * i + k + 1)
                            pe.sem_inc(s.go, 1)
                            for q in range(len(prop)):
                                last = nc.tensor.matmul(prop[q][0:H, 0:PC], blk[:, k, :], adjr[:, k, q * PC:(q + 1) * PC], start=False, stop=False)
                            last.then_inc(s.adj_used, 1)
                    for q in range(len(prop)):
                        last = nc.tensor.matmul(prop[q][0:H, 0:PC], zb[:, 0:H], zb[:, 0:PC], start=False, stop=True)
                    last.then_inc(s.prop_mm, 1)
                pe.wait_ge(s.prop_cp, 1 + (2 * len(prop)) * L + 2 * len(prop))
                pe.sem_inc(s.go, 1)
                for q in range(5):
                    lo, hi = 10 * q, min(10 * q + 10, HI)
                    for j in range(lo, hi):
                        last = nc.tensor.transpose(propT[q][:, (j - lo) * H:(j - lo + 1) * H], sums[:, j * P:(j + 1) * P], ident[0:H, 0:H])
                    last.then_inc(s.prop_T, 1)

        @block.vector
        def _(dve):
            v = Steps(dve, s.dve_step)
            V = nc.vector
            for x in (s.cnt_done, s.rk_sel):
                dve.sem_inc(x, 1)

            def tt(o, x, y, op):
                return V.tensor_tensor(o, x, y, op)

            for t in (x0, mult, zi, idxR, hist, ones, stg):
                v(V.memset(t[:], 1 if t is ones else 0))
            v(V.memset(zb[:], 0))
            v(V.memset(epsc[:], 1e-5))
            v(V.memset(halfpi[:], float(np.pi) / 2))
            v(V.memset(hid[:], 1.0))
            v(V.memset(zrow[:], 0))
            v(V.memset(nullA[:], 0))
            v(V.memset(nullK[:], 0))
            v(V.memset(nullA[:, 0:1], -BIG))
            v(V.memset(nullK[:, H:H + 1], -BIG))
            done(dve, V.memset(zero[:], 0), s.zero_set, 1)
            v(V.memset(rec[:], 0))
            done(dve, V.memset(rowb[:], 0), s.cleared, 1)
            dve.wait_ge(s.iota, 2)
            v(V.tensor_copy(iota[:], iotai[:]))
            v(V.tensor_copy(part[:], parti[:]))
            v(V.tensor_scalar(ident[:], iota[:], part[:, 0:1], None, ALU.is_equal))
            v(V.tensor_copy(identb[:], ident[:]))
            v(V.tensor_scalar(triu[:], iota[:], part[:, 0:1], None, ALU.is_gt))
            v(V.tensor_scalar(tril[:], iota[:], part[:, 0:1], None, ALU.is_lt))
            v(V.tensor_scalar(edge245[:], iota[:], float(COLS), None, ALU.mult))
            v(V.tensor_scalar(iotab1[:], iota[:], 1.0, None, ALU.add))
            done(dve, V.tensor_copy(iotab[:], iota[:]), s.const_ready, 1)
            dve.wait_ge(s.keys, 96)
            v(V.tensor_scalar(c1[:], part[:], float(P - 1), None, ALU.is_lt))
            v(V.tensor_scalar(c2[:], c1[:], -float(NP - 1), float(NP - 1), ALU.mult, ALU.add))
            for k in range(2):
                v(V.tensor_copy(key[k][:], rowi[k][:]))
                v(V.tensor_scalar(key[k][:, 0:PADS], rowi[k][:, 0:PADS], c1[:, 0:1], c2[:, 0:1], ALU.mult, ALU.add))
                v(V.tensor_scalar(keyt[:], key[k][:], P - 1, None, ALU.bitwise_and))
                v(V.tensor_copy(klo[k][:, 0:KE], keyt[:]))
                if k == 0:
                    v(V.tensor_scalar(pair[:], keyt[:], 256, 256, ALU.mult, ALU.add))
                else:
                    v(tt(pair[:], pair[:], keyt[:], ALU.add))
                v(V.tensor_scalar(keyt[:], key[k][:], 7, None, ALU.logical_shift_right))
                v(V.tensor_copy(khi[k][:, 0:KE], keyt[:]))
                v(V.tensor_scalar(rowi[k][:], rowi[k][:], 1, None, ALU.add))
            within = key[0][:, :].bitcast(F32)
            v(V.tensor_scalar(within[:, :], cw[:], 6.0, None, ALU.is_lt))
            done(dve, V.tensor_scalar(cw[:], cw[:], 6.0, None, ALU.min), s.dist_ready, 1)

            def one_hot(o, keys, i, n):
                return tt(o, bc(keys[:, bass.ds(GRP * i, GRP)], 2, n), bc(iotab[:, 0:n], 1, GRP), ALU.is_equal)

            with dve.Fori(0, NG) as i:
                for k in range(2):
                    dve.wait_ge(s.h_mm, 3 * i + 3)
                    one_hot(ohl[:, k, :, :], klo[k], i, P)
                    one_hot(ohh[:, k, :, :], khi[k], i, HI).then_inc(s.h_oh[k], 1)
            dve.wait_ge(s.cos_ready, 1)
            v(V.tensor_scalar(cw[:], cw[:], 1.0, 0.5, ALU.add, ALU.mult))
            v(tt(cw[:], cw[:], within[:, :], ALU.mult))
            dve.wait_ge(s.nodes, 96)
            done(dve, V.tensor_scalar(logm[:], mult[:], 1.0, None, ALU.max), s.mult_ready, 1)
            dve.wait_ge(s.h_all, 3)
            cnt, rows, last, tmp = rowt[1], rowt[0], rowt[1], rowt[2]

            def ceil_div(o, per):
                v(V.tensor_scalar(sort_i[:], cnt[:], float(per - 1), None, ALU.add))
                v(V.tensor_scalar(sort_i[:], sort_i[:], per.bit_length() - 1, None, ALU.logical_shift_right))
                return V.tensor_scalar(o, sort_i[:], 1.0, None, ALU.max)

            v(V.tensor_copy(cnt[:], bank[1][:, 0:HI]))
            done(dve, V.tensor_scalar(n3[:], cnt[:], 1.0, None, ALU.add), s.deg_ready, 1)
            dve.wait_ge(s.sqdeg_ready, 1)
            v(V.reciprocal(dinv[:], n4[:]))
            v(V.tensor_copy(cnt[:], bank[0][:, 0:HI]))
            done(dve, ceil_div(rows[:], SLOTS), s.cnt_ready, 1)
            dve.wait_ge(s.pre_mm, 1)
            v(V.tensor_tensor_scan(tmp[:], bank[3][:, 64:64 + HI], zrow[:, 0:HI], 0.0, ALU.add, ALU.add))
            v(tt(tmp[:], tmp[:], bank[3][:, 64:64 + HI], ALU.subtract))
            v(tt(rowb[:], tmp[:], bank[3][:, 0:HI], ALU.add))
            done(dve, V.tensor_copy(rowbi[:], rowb[:]), s.rows_ready, 1)
            v(tt(last[:], rowb[:], rows[:], ALU.add))
            v(V.tensor_scalar(last[:], last[:], -1.0, None, ALU.add))
            v(V.tensor_copy(lasti[:], last[:]))
            v(tt(rcp, bc(last[:, :], 2, P), bc(edge245[:, :], 1, HI), ALU.is_ge))
            v(V.tensor_reduce(tmp[:], rcp, AX, ALU.add))
            v(V.tensor_scalar(rowt[3][:], tmp[:], float(COLS), -float(COLS), ALU.mult, ALU.add))
            v(tt(rowt[3][:], rowb[:], rowt[3][:], ALU.is_lt))
            v(tt(rowt[3][:], rowt[3][:], tmp[:], ALU.mult))
            v(V.tensor_scalar(rowt[3][:], rowt[3][:], -1.0, None, ALU.add))
            v(tt(rcp, bc(rowt[3][:, :], 2, P), bc(iota[:, :], 1, HI), ALU.is_equal))
            v(V.tensor_scalar(nrow[:, :, 0], ones[:, 0:HI], part[:, 0:1], 1.0, ALU.mult, ALU.add))
            v(V.tensor_scalar(nrow[:, :, 1], iota[:, 0:HI], 0.0, None, ALU.add))
            v(V.tensor_scalar(run[:, 0, 0, :], rowb[:], float(SLOTS), None, ALU.mult))
            v(V.tensor_copy(cnt[0:HI, :], bank[2][0:HI, 0:HI]))
            done(dve, ceil_div(rows[:], P), s.cnt_ready, 2)
            dve.wait_ge(s.pre_mm, 2)
            v(V.tensor_tensor_scan(tmp[0:HI, :], bank[0][0:HI, 64:64 + HI], zrow[0:HI, 0:HI], 0.0, ALU.add, ALU.add))
            v(tt(tmp[0:HI, :], tmp[0:HI, :], bank[0][0:HI, 64:64 + HI], ALU.subtract))
            v(tt(tmp[0:HI, :], tmp[0:HI, :], bank[0][0:HI, 0:HI], ALU.add))
            v(V.tensor_copy(firstt[0:HI, :], tmp[0:HI, :]))
            v(V.tensor_scalar(run[0:HI, 1, 0, :], tmp[0:HI, :], float(P), None, ALU.mult))
            v(tt(last[0:HI, :], tmp[0:HI, :], rows[0:HI, :], ALU.add))
            v(V.tensor_scalar(lastt[0:HI, :], last[0:HI, :], -1.0, None, ALU.add))
            v(V.tensor_scalar(c1[:], part[:], float(NP), 1.0, ALU.mult, ALU.add))
            done(dve, V.tensor_scalar(destv[0:HI, :], iota[0:HI, 0:HI], c1[0:HI, 0:1], None, ALU.add), s.tiles_ready, 1)
            dve.wait_ge(s.mark_ld, 16)
            done(dve, V.tensor_tensor_scan(cum[:], markt[:, :], zrow[:, :], 0.0, ALU.add, ALU.add), s.scan_ready, 1)
            v(V.tensor_scalar(drop[:], markt[:], -BIG, None, ALU.mult))
            v(V.tensor_scalar(keep[:], markt[:], -1.0, 1.0, ALU.mult, ALU.add))
            dve.wait_ge(s.pre_mm, 3)
            v(V.tensor_copy(c1[:], bank[3][:, 0:1]))
            v(V.tensor_scalar(nodef[:], cum[:], c1[:, 0:1], None, ALU.add))
            v(V.tensor_copy(idxR[:, 0:COLS, SLOTS:SLOTS + 1], nodef[:, :].unsqueeze(2)))
            v(V.tensor_scalar(nfl[:, 0, :], ones[:], nodef[:, 0:1], None, ALU.mult))
            done(dve, V.tensor_scalar(nfl[:, 1, :], ones[:], nodef[:, COLS - 1:COLS], None, ALU.mult), s.ends_ready, 1)
            dve.wait_ge(s.pre_mm, 4)
            v(V.scalar_tensor_tensor(maskQP[:], bank[3][:, 128:256], nodef[:, COLS - 1:COLS], triu[:], ALU.is_equal, ALU.mult))
            v(V.scalar_tensor_tensor(maskPQ[:], bank[3][:, 256:384], nodef[:, 0:1], tril[:], ALU.is_equal, ALU.mult))
            for t in klo + khi:
                v(V.memset(t[:, KE:], 0))
            done(dve, V.tensor_scalar(maskneg[:], maskPQ[:], -1.0, BIG, ALU.add, ALU.mult), s.run_ready, 1)
            dve.wait_ge(s.pre_mm, 5)
            v(V.tensor_copy(crf[:], bank[1][:, 0:2]))
            v(V.scalar_tensor_tensor(c1[:], crf[:, 1:2], float(P), crf[:, 0:1], ALU.mult, ALU.add))
            v(V.tensor_scalar(c2[:], part[:], float(NP + 1), None, ALU.add))
            v(V.scalar_tensor_tensor(c2[:], c1[:], 0.0, c2[:], ALU.is_equal, ALU.mult))
            v(tt(crow[:], c1[:], c2[:], ALU.add))
            counted = (P, HI)

            def one_hots(b, g):
                one_hot(ohl[:, b, :, :], klo[0], g, P)
                one_hot(ohh2[b][:, 0, :, :], khi[0], g, HI)
                one_hot(ohh2[b][:, 1, :, :], khi[1], g, HI).then_inc(s.rk_oh, 1)

            one_hots(0, 0)
            with v.loop(NG // RECR, RECR * (2 * (GRP + 4) + 3)) as i:
                for b in range(RECR):
                    g, o = RECR * i + b, b % 2
                    cols = bass.ds(GRP * g, GRP)
                    before = [None, None]
                    for j in range(GRP):
                        for k in range(2):
                            n = counted[k]
                            if j == 0:
                                dve.wait_ge(s.rk_cnt, 2 * g + k + 1)
                            else:
                                v.after(before[k])
                            before[k] = v.start(tt(run[0:n, k, j + 1, :], run[0:n, k, j, :], bank[2 + k][0:n, j * HI:(j + 1) * HI], ALU.add))
                    v.after(before[1])
                    for k in range(2):
                        n = counted[k]
                        before[k] = v.start(V.tensor_scalar(runhi[0:n, k, :, :], run[0:n, k, 0:GRP, :], 1 / PART, None, ALU.mult))
                    for k in range(2):
                        n = counted[k]
                        v.after(before[k])
                        v.start(V.scalar_tensor_tensor(runlo[0:n, k, :, :], runhi[0:n, k, :, :], -PART, run[0:n, k, 0:GRP, :], ALU.mult, ALU.add))
                    for k in range(2):
                        dve.wait_ge(s.rk_eq, 2 * g + k + 1)
                        tt(eqm[:, k, :, :], wide[0][:, :].rearrange("p (j e) -> p j e", e=P), bc(triu[:, :], 1, GRP),
                           ALU.mult).then_inc(s.rk_eqm, 1)
                    one_hots(1 - o, g + 1)
                    for k in range(2):
                        n = counted[k]
                        dve.wait_ge(s.rk_g, 1 + 2 * g + k + 1)
                        tt(gsel[:, k, :, :], bank[2 + k][:, 0:OH].rearrange("p (j c) -> p j c", c=HI), ohh2[o][:, k, :, :], ALU.mult).then_inc(s.rk_sel, 1)
                        v.start(V.tensor_copy(run[0:n, k, 0, :], run[0:n, k, GRP, :]))
                    for k in range(2):
                        dve.wait_ge(s.rk_sel, 1 + 2 * g + k + 1)
                        at = v.start(V.tensor_reduce(posf[:, k, :], gsel[:, k, :, :], AX, ALU.add))
                    v.after(at)
                    dve.wait_ge(s.rec_in[b], 48 * (i + 1))
                    V.tensor_copy(pst[0][:, b, :], posf[:, 0, :])
                    v(V.tensor_copy(qi[:, 0, :], posf[:, 1, :]))
                    v(V.tensor_scalar(qi[:, 1, :], qi[:, 0, :], 7, None, ALU.logical_shift_right))
                    v(V.tensor_scalar(qi[:, 0, :], qi[:, 0, :], P - 1, None, ALU.bitwise_and))
                    V.scalar_tensor_tensor(pst[1][:, b, :], qi[:, 0, :], NTC, qi[:, 1, :], ALU.mult, ALU.add)
                    V.tensor_scalar(rec[:, b, :, REC - 2], cw[:, cols], 1.0, None, ALU.mult)
                    V.tensor_scalar(reci[:, b, :, REC - 1], rowi[1][:, cols], 0, None, ALU.add)
                    V.tensor_scalar(srcst[:, b, :], pair[:, cols], 0, None, ALU.add).then_inc(s.rec_fill, 1)
            v(V.tensor_copy(t0[:, :, 0:H], x0[:, :, :]))
            dve.wait_ge(s.e_done, NNT)
            done(dve, V.tensor_copy(t0[:, :, W0 - 1:W0], mult[:, :].unsqueeze(2)), s.t0_ready, 1)
            for b in range(RECR):
                dve.wait_ge(s.rec_out[b], 16 * GRP * (NG // RECR))
                dve.wait_ge(s.idx_out[b], 16 * GRP * (NG // RECR))
            tkt = tkeep[:, :].bitcast(I32)
            dve.wait_ge(s.pair_ld, 16)
            dve.wait_ge(s.zeroed, 80)
            dve.wait_ge(s.null, 96)
            v(V.tensor_scalar(tkt, pairt, 8, None, ALU.logical_shift_right))
            v(V.tensor_copy(plo, tkt))
            v(V.tensor_scalar(tkt, pairt, 255, None, ALU.bitwise_and))
            done(dve, V.tensor_copy(phi[:, :], tkt), s.unpacked, 1)
            dve.wait_ge(s.slot_ld, 16)
            v(V.tensor_scalar(tnone[:, :], tslot[:, :], 0, None, ALU.is_equal))
            v(V.tensor_scalar(c1[:], part[:], float(NP * HI + 1), None, ALU.add))
            v(V.tensor_scalar(tnone[:, :], tnone[:, :], c1[0:TPI, 0:1], -1.0, ALU.mult, ALU.add))
            done(dve, tt(tslot[:, :], tslot[:, :], tnone[:, :], ALU.add), s.slots_ready, 1)
            dve.wait_ge(s.keep_ld, 16)
            v(V.tensor_scalar(tkeep[:, :], tkeep[:, :], -1.0, 1.0, ALU.mult, ALU.add))
            v(V.memset(acc[:], 0))

            def by_slot(ap):
                return ap.rearrange("p s c -> p c s")

            def int_copy(o, i_):
                return V.tensor_scalar(o, i_, 0, None, ALU.add)

            for c in range(RINGC):
                done(dve, int_copy(stg[:, c, SLOTS:], idxR[:, c, SLOTS:]), s.l0_stg, c + 1)
            with v.loop(NIT, 9 * RINGC) as i:
                dve.wait_ge(s.st_out, 1 + 16 * i)
                for c in range(RINGC):
                    w = RINGC * i + c
                    dve.wait_ge(s.l0_g[c], 16 * (SLOTS + 1) * (i + 1))
                    g0 = G0[c]
                    v(tt(prod[:, :, 0:G], g0[:, :, H:H + G], bc(Gq[:, c, 0:G], 1, SLOTS), ALU.mult))
                    v(V.tensor_reduce(sc[:, 0, 0, :], prod[:, :, 0:G], AX, ALU.add))
                    v(tt(prod2[:, :, :], recL[:, c, :, RBF:RBF + H], bc(sc[:, 0, 0, :], 2, H), ALU.add))
                    v(tt(prod2[:, :, :], prod2[:, :, :], g0[:, :, 0:H], ALU.mult))
                    v(tt(sc[:, 0, 1, :], recL[:, c, :, REC - 2], g0[:, :, W0 - 1], ALU.mult))
                    v(tt(prod2[:, :, :], prod2[:, :, :], bc(sc[:, 0, 1, :], 2, H), ALU.mult))
                    v(V.tensor_reduce(ar[:, 0, 0:H], by_slot(prod2[:, :, :]), AX, ALU.add))
                    v(V.tensor_reduce(ar[:, 0, H:W1], g0[:, :, W0 - 1], AX, ALU.add))
                    v(int_copy(idxR[:, bass.ds(w, 1), 0:SLOTS].rearrange("p w s -> p (w s)"), recLi[:, c, :, REC - 1]))
                    done(dve, V.scalar_tensor_tensor(h0[:, c, :], h0[:, (c - 1) % RINGC, :], keep[:, bass.ds(w, 1)], ar[:, 0, :],
                                                     ALU.mult, ALU.add), s.l0_done, w + 1)
                    done(dve, int_copy(stg[:, c, SLOTS:], idxR[:, bass.ds(w + RINGC, 1), SLOTS:].rearrange("p w s -> p (w s)")),
                         s.l0_stg, w + RINGC + 1)
            dve.wait_ge(s.carry_mm, 1)
            done(dve, V.tensor_copy(cin[:, 0:W1], bank[0][:, 0:W1]), s.carry_ready, 1)

            def layer_norm(o, x, n, gain=None, bias=None, signal=None, value=None):
                v(V.tensor_reduce(n1[:, :], x, AX, ALU.add))
                v(V.tensor_scalar(n1[:, :], n1[:, :], 1.0 / H, None, ALU.mult))
                v(tt(t2[:, :, :], x, bc(n1[:, :], 2, H), ALU.subtract))
                v(tt(o, t2[:, :, :], t2[:, :, :], ALU.mult))
                done(dve, V.tensor_reduce(n1[:, :], o, AX, ALU.add), s.var_ready, n)
                dve.wait_ge(s.std_ready, n)
                v(V.reciprocal(n3[:, :], n2[:, :]))
                last = tt(o, t2[:, :, :], bc(n3[:, :], 2, H), ALU.mult)
                if gain is not None:
                    v(last)
                    v(tt(o, o, gain, ALU.mult))
                    last = tt(o, o, bias, ALU.add)
                if signal is None:
                    v(last)
                else:
                    done(dve, last, signal, value)

            for c in range(RINGC):
                dve.wait_ge(s.att_out[c], 16 * NIT)
            dve.wait_ge(s.st_g, 16 * HI)
            dve.wait_ge(s.cr_in, 16)
            dve.wait_ge(s.par, PARS)
            v(tt(sA0[:, :, :], sA0[:, :, :], sC0[:, :, :], ALU.add))
            v(V.tensor_scalar(n1[:, :], sA0[:, :, H], 1e-8, None, ALU.max))
            v(V.reciprocal(n4[:, :], n1[:, :]))
            v(tt(t1[:, :, :], sA0[:, :, 0:H], bc(n4[:, :], 2, H), ALU.mult))
            v(tt(t1[:, :, :], t1[:, :, :], x0[:, :, :], ALU.add))

            def all_nodes(p):
                return p.to_broadcast([P, HI, H])

            layer_norm(h[:, :, :], t1[:, :, :], 1, all_nodes(lnn["gn"][:, :, :]), all_nodes(lnn["bn"][:, :, :]), s.h_ready, 1)

            def layer(L):
                def par(n):
                    return all_nodes(lnp[n][:, bass.ds(L, 1), :])

                for g, (lo, hi) in enumerate(NT):
                    dve.wait_ge(s.p_mm, NNT * L + g + 1)
                    V.tensor_copy(qkm[:, lo:hi, :], bank[2 + g % 2][:, 0:(hi - lo) * 3 * H].rearrange("p (j c) -> p j c", c=3 * H)).then_inc(s.p_done, 1)
                dve.wait_ge(s.p_done, NNT * L + NNT)
                layer_norm(qkm[:, :, 0:H], qkm[:, :, 0:H], 3 * L + 2, par("gq"), par("bq"), s.q_ready, L + 1)
                layer_norm(kt[:, :, 0:H], qkm[:, :, H:2 * H], 3 * L + 3, par("gk"), par("bk"))
                v(V.tensor_copy(kt[:, :, H:H + 1], logm[:, :].unsqueeze(2)))
                done(dve, V.tensor_copy(kt[:, :, H + 1:WK], qkm[:, :, 2 * H:3 * H]), s.k_ready, L + 1)
                v(V.memset(hist[:, RINGC - 1, :], 0))
                v(V.memset(hist[:, RINGC - 1, 0:1], -BIG))
                for c in range(RINGC):
                    done(dve, int_copy(stg[:, c, :], idxR[:, c, :]), s.colstg, (COLS + RINGC) * L + c + 1)
                v(V.tensor_copy(cat[:, :, 0:H], h[:, :, :]))

            def beat(L, i, c):
                score, message = c < RINGC, c > 0
                if score:
                    w, q, n = RINGC * i + c, c % 2, TOFF[c + 1] - TOFF[c]
                    prev = hist[:, (c - 1) % RINGC, :]
                    dve.wait_ge(s.att_in[c], (16 * NIT) * L + 16 * i + 16)
                    dve.wait_ge(s.col_g[c], (16 * (SLOTS + 1) * NIT) * L + 16 * (SLOTS + 1) * i + 16 * (SLOTS + 1))
                    v.start(tt(prod[:, :, 0:H], Gk[:, c, :, 0:H], bc(Gq[:, c, :], 1, SLOTS), ALU.mult))
                    dots = v.start(V.scalar_tensor_tensor(prod[:, :, H:], att[:, c, :, :], 0.1, bc(Gq[:, c, 0:RBF], 1, SLOTS), ALU.mult, ALU.mult))
                if message:
                    c0, q0 = c - 1, (c - 1) % 2
                    w0 = RINGC * i + c0
                    dve.wait_ge(s.exp_ready, (2 * COLS) * L + 2 * w0 + 2)
                    terms = v.start(tt(prod2[:, :, :], Gk[:, c0, :, H + 1:WK], bc(sc[:, q0, 1, :], 2, H), ALU.mult))
                if score:
                    cols = bass.ds((TPI * NIT) * L + TPI * i + TOFF[c], n)
                    tt(oht[:, 0, 0:n, :], bc(plo[:, cols], 2, P), bc(iotab1[:, :], 1, n), ALU.is_equal)
                    v.after(dots)
                    sums = v.start(V.tensor_reduce(sc[:, q, 0, :], prod[:, :, :], AX, ALU.add))
                if message:
                    v.after(terms)
                    msum = v.start(V.tensor_reduce(ar[:, q0, 1:W1], by_slot(prod2[:, :, :]), AX, ALU.add))
                if score:
                    tt(oht[:, 1, 0:n, :], bc(phi[:, cols], 2, P), bc(iotab[:, :], 1, n), ALU.is_equal).then_inc(s.cnt_oh, 1)
                    v.after(sums)
                    full = v.start(tt(sc[:, q, 0, :], sc[:, q, 0, :], Gk[:, c, :, H], ALU.add))
                if message:
                    fade = v.start(tt(scal[:, q0, 4:5], scal[:, q0, 3:4], keep[:, bass.ds(w0, 1)], ALU.mult))
                if score:
                    if c == 0:
                        dve.wait_ge(s.stA_out, 1 + (16 * NIT) * L + 16 * i)
                    ran = v.start(tt(scal[:, q, 1:2], prev[:, 0:1], drop[:, bass.ds(w, 1)], ALU.add))
                    v.after(full)
                    top = v.start(V.tensor_reduce(scal[:, q, 0:1], sc[:, q, 0, :], AX, ALU.max))
                if message:
                    v.after(fade)
                    if c0:
                        dve.wait_ge(s.col_done, COLS * L + w0)
                    V.scalar_tensor_tensor(hist[:, c0, 1:WS], hist[:, (c0 - 1) % RINGC, 1:WS], scal[:, q0, 4:5], ar[:, q0, :],
                                           ALU.mult, ALU.add).then_inc(s.col_done, 1)
                if score:
                    v.after(top)
                    peak = v.start(tt(hist[:, c, 0:1], scal[:, q, 0:1], scal[:, q, 1:2], ALU.max))
                if message:
                    int_copy(stg[:, c0, :], idxR[:, bass.ds(w0 + RINGC, 1), :].rearrange("p w s -> p (w s)")).then_inc(s.colstg, 1)
                if score:
                    v.after(peak)
                    V.tensor_scalar(scal[:, q, 2:3], hist[:, c, 0:1], -1.0, None, ALU.mult).then_inc(s.max_ready, 1)
                    dve.wait_ge(s.cnt_mm, COLS * L + w + 1)
                    back = 1 if c < 2 else 0
                    r = (4, 3, 0, 1, 2)[c]
                    nr = TOFF[r + 1] - TOFF[r]
                    dve.wait_ge(s.cnt_out[r], 1 + (16 * nr * NIT) * L + 16 * nr * i + (0 if back else 16 * nr))
                    for j in range(TOFF[c], TOFF[c + 1]):
                        before = acc_slot(c, j - 1) if j > TOFF[c] else acc_slot((c - 1) % RINGC, TOFF[(c - 1) % RINGC + 1] - 1)
                        t = (TPI * NIT) * L + TPI * i + j
                        if j == TOFF[c]:
                            dve.wait_ge(s.cnt_done, 1 + COLS * L + w)
                        last = V.scalar_tensor_tensor(acc[:, acc_slot(c, j), :], acc[:, before, :], tkeep[:, bass.ds(t, 1)],
                                                      wide[1][:, (j - TOFF[c]) * P:(j - TOFF[c] + 1) * P], ALU.mult, ALU.add)
                        if j < TOFF[c + 1] - 1:
                            v(last)
                    last.then_inc(s.cnt_done, 1)

            def finish_layer(L):
                done(dve, V.tensor_scalar(mtr[:], ones[:], hist[:, RINGC - 1, 0:1], None, ALU.mult), s.cm_ready, L + 1)
                dve.wait_ge(s.carryA_mm, 3 * L + 1)
                v(tt(mrow[:], wide[0][:, 0:P], maskPQ[:], ALU.mult))
                v(tt(mrow[:], mrow[:], maskneg[:], ALU.add))
                v(V.tensor_reduce(cin[:, 0:1], mrow[:], AX, ALU.max))
                done(dve, V.tensor_scalar(c1[:], cin[:, 0:1], -1.0, None, ALU.mult), s.cmax_ready, L + 1)
                dve.wait_ge(s.cexp_ready, L + 1)
                done(dve, tt(mtr[:], mtr[:], maskPQ[:], ALU.mult), s.cw_ready, L + 1)
                dve.wait_ge(s.carryA_mm, 3 * L + 2)
                done(dve, V.tensor_copy(mrow[:], wide[0][:, 512:512 + P]), s.cwT_ready, L + 1)
                dve.wait_ge(s.carryA_mm, 3 * L + 3)
                done(dve, V.tensor_copy(cin[:, 1:WS], wide[1][:, 0:W1]), s.carryA_ready, L + 1)
                dve.wait_ge(s.stA_g, (16 * HI) * L + 16 * HI)
                dve.wait_ge(s.cr_in, 16 * L + 32)
                v(tt(n1[:, :], sA[:, :, 0], sC[:, :, 0], ALU.max))
                v(tt(n3[:, :], sA[:, :, 0], n1[:, :], ALU.subtract))
                done(dve, tt(n4[:, :], sC[:, :, 0], n1[:, :], ALU.subtract), s.nmax_ready, L + 1)
                dve.wait_ge(s.nexp_ready, 2 * L + 2)
                v(tt(sA[:, :, 1:WS], sA[:, :, 1:WS], bc(n3[:, :], 2, W1), ALU.mult))
                v(tt(sC[:, :, 1:WS], sC[:, :, 1:WS], bc(n4[:, :], 2, W1), ALU.mult))
                v(tt(sA[:, :, 1:WS], sA[:, :, 1:WS], sC[:, :, 1:WS], ALU.add))
                v(V.tensor_scalar(n1[:, :], sA[:, :, 1], 1e-10, None, ALU.add))
                v(V.reciprocal(n4[:, :], n1[:, :]))
                done(dve, tt(cat[:, :, H:2 * H], sA[:, :, 2:WS], bc(n4[:, :], 2, H), ALU.mult), s.cat_ready, L + 1)
                for g, (lo, hi) in enumerate(NT):
                    dve.wait_ge(s.u_mm, NNT * L + g + 1)
                    z = bank[2 + g % 2][:, 0:(hi - lo) * H].rearrange("p (j c) -> p j c", c=H)
                    V.tensor_copy(t1[:, lo:hi, :], z).then_inc(s.u_done, 1)
                dve.wait_ge(s.u_done, NNT * L + NNT)
                v(V.scalar_tensor_tensor(t1[:, :, :], t1[:, :, :], 0.01, t1[:, :, :], ALU.mult, ALU.max))
                v(tt(t1[:, :, :], t1[:, :, :], h[:, :, :], ALU.add))
                layer_norm(h[:, :, :], t1[:, :, :], 3 * L + 4, all_nodes(lnp["go"][:, bass.ds(L, 1), :]),
                           all_nodes(lnp["bo"][:, bass.ds(L, 1), :]), s.h_ready, L + 2)

            around = 38
            with v.loop(LAYERS, (10 * RINGC + TPI - RINGC) * NIT + around) as L:
                layer(L)
                dve.sem_inc(s.go, 1)
                with v.loop(NIT, 10 * RINGC + TPI - RINGC) as i:
                    for c in range(RINGC + 1):
                        beat(L, i, c)
                dve.wait_ge(s.col_done, COLS * L + COLS)
                finish_layer(L)
            v(tt(t1[:, :, :], x0[:, :, :], h[:, :, :], ALU.add))
            layer_norm(h[:, :, :], t1[:, :, :], 3 * LAYERS + 2)
            v(V.tensor_copy(cat[:, :, 0:H], h[:, :, :]))
            done(dve, V.tensor_scalar(cat[:, :, H:2 * H], h[:, :, :], ALPHA, None, ALU.mult), s.x_ready, 1)
            with v.loop(STEPS, 7) as L:
                done(dve, tt(t1[:, :, :], h[:, :, :], bc(dinv[:, :], 2, H), ALU.mult), s.g_ready, L + 1)
                for q in range(5):
                    dve.wait_ge(s.prop_T, 5 * L + q + 1)
                    lo, hi = 10 * q, min(10 * q + 10, HI)
                    v(tt(t2[:, lo:hi, :], propT[q][:, 0:(hi - lo) * H].rearrange("p (j c) -> p j c", c=H), t1[:, lo:hi, :], ALU.add))
                v(tt(t2[:, :, :], t2[:, :, :], bc(dinv[:, :], 2, H), ALU.mult))
                v(V.scalar_tensor_tensor(h[:, :, :], t2[:, :, :], RING, cat[:, :, H:2 * H], ALU.mult, ALU.add))
            v(tt(t1[:, :, :], cat[:, :, 0:H], h[:, :, :], ALU.add))
            layer_norm(h[:, :, :], t1[:, :, :], 3 * LAYERS + 3, signal=s.result, value=1)


def kernel(**inputs):
    import concourse.bacc as bacc
    from concourse.bass_utils import run_bass_kernel_spmd

    nc = bacc.Bacc("TRN2", target_bir_lowering=False, num_devices=1)
    arrays, io = {}, {}
    for name, value in inputs.items():
        a = np.ascontiguousarray(value)
        arrays[f"in_{name}"] = a
        io[name] = nc.dram_tensor(f"in_{name}", a.shape, mybir.dt.from_np(a.dtype), kind="ExternalInput").ap()
    out = nc.dram_tensor("out_0", (N, H), F32, kind="ExternalOutput").ap()
    build(nc, io, out)
    r = run_bass_kernel_spmd(nc, [arrays], core_ids=[0])
    return r.results[0]["out_0"]
```
